# Optimizing a Trainium2 kernel written in Bass

```python
import numpy as np
import jax
import jax.numpy as jnp

def _softmax(x, axis=-1):
    return jax.nn.softmax(x, axis=axis)

def _gelu(x):
    return jax.nn.gelu(x, approximate=True)

def _silu(x):
    return jax.nn.silu(x)

def _sigmoid(x):
    return jax.nn.sigmoid(x)

def _layernorm(x, axis=-1, eps=1e-05):
    m = jnp.mean(x, axis=axis, keepdims=True)
    v = jnp.var(x, axis=axis, keepdims=True)
    return (x - m) / jnp.sqrt(v + eps)

def _scatter_add(tgt, idx, src, axis=0):
    return tgt.at[idx].add(src)

def _segment_sum(src, seg, n):
    return jax.ops.segment_sum(src, seg, n)
kernel_name = 'mk_gnn_resnorm_d1_gnn_r8_98109c'

def setup_inputs(seed: int=0):
    np.random.seed(seed)
    _w = jnp.asarray

    def _rec_inputs():
        import jax
        import jax.numpy as jnp
        _gk = jax.random.key(seed)
        x = -8.776e-05 + 1 * jax.random.normal(jax.random.fold_in(_gk, 1), (12500, 128), jnp.float32)
        src = jax.random.randint(jax.random.fold_in(_gk, 2), (400000,), 0, 12500, jnp.int32)
        dst = jnp.minimum((12500 * jax.random.uniform(jax.random.fold_in(_gk, 3), (400000,)) ** 2.0).astype(jnp.int32), 99999)
        _o = jnp.argsort(dst, stable=True)
        src = src[_o]
        dst = dst[_o]
        edge_weight = jax.random.uniform(jax.random.fold_in(_gk, 12), (400000,), jnp.float32, 0.0, 12)
        return (x, src, dst, edge_weight)
    x, src, dst, edge_weight = _rec_inputs()

    def _L0_gnn_setup():
        import jax, jax.numpy as jnp
        import numpy as np
        import math
        N_ATOMS = 5000
        HIDDEN = 128
        NUM_RBF = 50
        CUTOFF = 10.0
        N_EDGES = 80000
        key = jax.random.key(seed)
        ks = jax.random.split(key, 12)
        s = lambda fan_in: 1.0 / np.sqrt(fan_in)
        inp = {'h': jax.random.normal(ks[0], (N_ATOMS, HIDDEN), dtype=jnp.float32), 'edge_index': jax.random.randint(ks[1], (2, N_EDGES), 0, N_ATOMS, dtype=jnp.int64), 'distances': jax.random.uniform(ks[2], (N_EDGES,), dtype=jnp.float32) * 12.0, 'fw1': jax.random.uniform(ks[3], (NUM_RBF, HIDDEN), jnp.float32, -s(NUM_RBF), s(NUM_RBF)), 'fb1': jnp.zeros((HIDDEN,), jnp.float32), 'fw2': jax.random.uniform(ks[4], (HIDDEN, HIDDEN), jnp.float32, -s(HIDDEN), s(HIDDEN)), 'fb2': jnp.zeros((HIDDEN,), jnp.float32), 'pw': jax.random.uniform(ks[5], (HIDDEN, HIDDEN), jnp.float32, -s(HIDDEN), s(HIDDEN)), 'pb': jnp.zeros((HIDDEN,), jnp.float32), 'mw1': jax.random.uniform(ks[6], (HIDDEN, HIDDEN), jnp.float32, -s(HIDDEN), s(HIDDEN)), 'mb1': jnp.zeros((HIDDEN,), jnp.float32), 'mw2': jax.random.uniform(ks[7], (HIDDEN, HIDDEN), jnp.float32, -s(HIDDEN), s(HIDDEN)), 'mb2': jnp.zeros((HIDDEN,), jnp.float32)}
        return inp
    _L0_gnn_all = _L0_gnn_setup()
    _L0_gnn_in = {k: v for k, v in _L0_gnn_all.items() if k in ('fw1', 'fb1', 'fw2', 'fb2', 'pw', 'pb', 'mw1', 'mb1', 'mw2', 'mb2')}
    del _L0_gnn_all
    return {'x': x, 'src': src, 'dst': dst, 'edge_weight': edge_weight, 'L0_gnn_fw1': _L0_gnn_in['fw1'], 'L0_gnn_fb1': _L0_gnn_in['fb1'], 'L0_gnn_fw2': _L0_gnn_in['fw2'], 'L0_gnn_fb2': _L0_gnn_in['fb2'], 'L0_gnn_pw': _L0_gnn_in['pw'], 'L0_gnn_pb': _L0_gnn_in['pb'], 'L0_gnn_mw1': _L0_gnn_in['mw1'], 'L0_gnn_mb1': _L0_gnn_in['mb1'], 'L0_gnn_mw2': _L0_gnn_in['mw2'], 'L0_gnn_mb2': _L0_gnn_in['mb2']}

def reference(x, src, dst, edge_weight, L0_gnn_fw1, L0_gnn_fb1, L0_gnn_fw2, L0_gnn_fb2, L0_gnn_pw, L0_gnn_pb, L0_gnn_mw1, L0_gnn_mb1, L0_gnn_mw2, L0_gnn_mb2):
    import jax
    import jax.numpy as jnp

    def _L0_gnn_ref(h, edge_index, distances, fw1, fb1, fw2, fb2, pw, pb, mw1, mb1, mw2, mb2):
        import jax, jax.numpy as jnp
        import numpy as np
        import math
        N_ATOMS = 5000
        HIDDEN = 128
        NUM_RBF = 50
        CUTOFF = 10.0
        N_EDGES = 80000
        src, dst = (edge_index[0], edge_index[1])
        num_atoms = h.shape[0]
        width = CUTOFF / NUM_RBF * 0.5
        centers = jnp.linspace(0.0, CUTOFF, NUM_RBF)
        rbf = jnp.exp(-(distances[:, None] - centers) ** 2 / (2.0 * width * width))
        cut = 0.5 * (jnp.cos(jnp.pi * distances / CUTOFF) + 1.0) * (distances <= CUTOFF).astype(h.dtype)
        W = (jax.nn.silu(rbf @ fw1 + fb1) @ fw2 + fb2) * cut[:, None]
        messages = (h[src] @ pw + pb) * W
        agg = jax.ops.segment_sum(messages, dst, num_segments=num_atoms)
        return h + (jax.nn.silu(agg @ mw1 + mb1) @ mw2 + mb2)
    edge_index = jnp.stack([src, dst])
    x = _layernorm(x + _L0_gnn_ref(x, edge_index, edge_weight, L0_gnn_fw1, L0_gnn_fb1, L0_gnn_fw2, L0_gnn_fb2, L0_gnn_pw, L0_gnn_pb, L0_gnn_mw1, L0_gnn_mb1, L0_gnn_mw2, L0_gnn_mb2), axis=-1)
    return x

_drawn_inputs = setup_inputs


def setup_inputs(seed=0):
    import zlib

    import numpy as np

    out = dict(_drawn_inputs(seed))
    spreads = {'L0_gnn_fb1': (0.0, 0.8),
     'L0_gnn_fb2': (0.0, 0.346),
     'L0_gnn_pb': (0.0, 0.432),
     'L0_gnn_mb1': (0.0, 0.512),
     'L0_gnn_mb2': (0.0, 0.1)}
    factors = {'edge_weight': 4.688, 'L0_gnn_fw1': 8.0, 'L0_gnn_fw2': 7.36, 'L0_gnn_pw': 3.245}
    for name, (base, spread) in spreads.items():
        noise = np.random.default_rng([zlib.crc32(name.encode()), seed]).standard_normal(out[name].shape)
        drawn = base * np.exp(spread * noise) if base else spread * noise
        out[name] = jnp.asarray(drawn.astype(out[name].dtype))
    for name, factor in factors.items():
        out[name] = (out[name] * factor).astype(out[name].dtype)
    return out
```

```python
import math
from contextlib import ExitStack

import concourse.bass as bass
from concourse import mybir

F32, I32, BF16 = mybir.dt.float32, mybir.dt.int32, mybir.dt.bfloat16
ALU, ACT, AX = mybir.AluOpType, mybir.ActivationFunctionType, mybir.AxisListType

NODES, HIDDEN, EDGES = 12500, 128, 400000
RBF, CUTOFF, EPS = 50, 10.0, 1e-5
WIDTH = CUTOFF / RBF * 0.5
P = 128

EDGE_COLS = 625
ROWS = EDGES // EDGE_COLS
GROUPS = ROWS // P
BLOCKS = -(-EDGE_COLS // P)
ROW_SLOTS = BLOCKS * P
STEPS = EDGE_COLS.bit_length()
ID_BITS = NODES.bit_length()
ID_MASK = (1 << ID_BITS) - 1
FAR = 2 * CUTOFF
NO_NODE = 65536.0

MACRO = 4
WINDOW = 192
WINDOW1 = 64
ORDER = (0, 2, 1, 3)
UNIT = 4 * MACRO
MACROS = P // MACRO
UNITS = P // UNIT
AGG_COLS = 12800
WIDE = 512
ALL_WINDOWS = AGG_COLS // WIDE

EXTRA_TILES = ROWS * (BLOCKS - 1)
EXTRA_GROUPS = EXTRA_TILES // P
ALL_TILES = ROWS * BLOCKS
ALL_GROUPS = ALL_TILES // P

NODE_TILE = 125
CHUNK = 4
CHUNK_NODES = NODE_TILE * CHUNK
CHUNKS = NODES // CHUNK_NODES
RING = 4

COS = [(-1) ** k / math.factorial(2 * k) for k in range(9)]


def build(nc, x, src, dst, edge_weight, fw1, fb1, fw2, fb2, pw, pb, mw1, mb1, mw2, mb2, out):
    ctx = ExitStack()
    with ctx:
        def sb(name, shape, dtype=F32):
            return ctx.enter_context(nc.sbuf_tensor(name, shape, dtype))

        def sem(name):
            return ctx.enter_context(nc.semaphore(name))

        proj = nc.dram_tensor("proj_rows", (NODES, HIDDEN), F32).ap()
        dist_tiles = nc.dram_tensor("dist_tiles", (ALL_TILES + 1, P), F32).ap()
        ids_tiles = nc.dram_tensor("ids_tiles", (ALL_TILES + 1, P), I32).ap()
        extra_dist = nc.dram_tensor("extra_dist", (EXTRA_TILES, P), F32).ap()

        dist_rows = dist_tiles[0:ALL_TILES, :].rearrange("(r b) s -> r (b s)", b=BLOCKS)
        ids_rows = ids_tiles[0:ALL_TILES, :].rearrange("(r b) s -> r (b s)", b=BLOCKS)
        edge_rows = [a.rearrange("(r c) -> r c", c=EDGE_COLS) for a in (edge_weight, src, dst)]
        x_nodes = x.rearrange("(j p) f -> p j f", p=NODE_TILE)
        proj_nodes = proj.rearrange("(j p) f -> p j f", p=NODE_TILE)
        out_nodes = out.rearrange("(j p) f -> p j f", p=NODE_TILE)

        ident = sb("ident", [P, P])
        ones_row = sb("ones_row", [1, P])
        before = sb("before", [P, P])
        all_ones = sb("all_ones", [P, P])
        iota_i = sb("iota_i", [P, ROW_SLOTS], I32)
        iota_f = sb("iota_f", [P, ROW_SLOTS])
        lane_i = sb("lane_i", [P, 1], I32)
        lane_f = sb("lane_f", [P, 1])
        rbf_scale = sb("rbf_scale", [P, 1])
        rbf_shift = sb("rbf_shift", [P, 1])
        fw1_halves = sb("fw1_halves", [P, 2, P])
        fw2_half = sb("fw2_half", [P, P])
        pw_sb = sb("pw_sb", [P, P])
        mw1_sb = sb("mw1_sb", [P, P])
        mw2_half = sb("mw2_half", [P, P])
        raw_w = sb("raw_w", [P, 2, P])
        bias_in = sb("bias_in", [1, 4, P])
        bias_rest = sb("bias_rest", [1, 4, P])
        bias_parts = sb("bias_parts", [1, 3, 4, P], BF16)
        bias_lanes = sb("bias_lanes", [P, 4, P], BF16)
        bias_rhs = sb("bias_rhs", [P, 3, CHUNK, P], BF16)
        one_lanes = sb("one_lanes", [P, 512], BF16)

        dist = sb("dist", [P, ROW_SLOTS])
        ids = sb("ids", [P, ROW_SLOTS], I32)
        src_in = sb("src_in", [P, EDGE_COLS], I32)
        dst_in = sb("dst_in", [P, EDGE_COLS], I32)
        drop = sb("drop", [P, ROW_SLOTS])
        dropped = sb("dropped", [P, EDGE_COLS])
        move = [sb(f"move{i}", [P, EDGE_COLS], I32) for i in range(2)]
        moves_now = sb("moves_now", [P, EDGE_COLS], I32)
        ones_cols = sb("ones_cols", [P, EDGE_COLS])
        counts = sb("counts", [P, GROUPS])

        row_dist = sb("row_dist", [P, P])
        row_ids = sb("row_ids", [P, P], I32)
        row_cut = sb("row_cut", [P, P])
        row_src = sb("row_src", [P, P])
        row_dst = sb("row_dst", [P, P])
        row_int = sb("row_int", [P, 2, P], I32)
        row_a = sb("row_a", [P, P])
        row_b = sb("row_b", [P, P])
        row_min = sb("row_min", [P, 1])
        base_f = sb("base_f", [1, P])
        base_next = sb("base_next", [1, P], I32)
        base_now = sb("base_now", [1, P], I32)
        src_next = sb("src_next", [P, P], I32)
        dst_next = sb("dst_next", [P, P])
        cut_next = sb("cut_next", [P, P])
        src_now = sb("src_now", [P, P], I32)
        dst_now = sb("dst_now", [P, P])
        cut_now = sb("cut_now", [P, P])
        farthest = sb("farthest", [P, 2])
        reach = sb("reach", [P, 1])

        dist_bc = sb("dist_bc", [P, 2, MACRO, 2 * P])
        square = sb("square", [P, MACRO * 2 * P])
        rbf = sb("rbf", [P, 2, MACRO, 2 * P])
        half_tanh = sb("half_tanh", [P, 2, 512])
        act_t = sb("act_t", [P, 2, 512])
        gathered = sb("gathered", [P, 2 * UNIT, P])
        message = sb("message", [P, 2, 512])
        member = sb("member", [P, 2, MACRO, WINDOW])
        index = sb("index", [P, 2, UNIT], I32)
        agg = sb("agg", [P, AGG_COLS])

        more = sb("more", [P, GROUPS, BLOCKS - 1])
        rank = sb("rank", [P, GROUPS * (BLOCKS - 1)])
        tile_id = sb("tile_id", [P, GROUPS, BLOCKS - 1])
        tile_id_i = sb("tile_id_i", [P, GROUPS, BLOCKS - 1], I32)
        total = sb("total", [P, 1])
        offset = sb("offset", [P, 1])
        n_extra_i = sb("n_extra_i", [P, 1], I32)
        outside_i = sb("outside_i", [P, 1], I32)
        chosen = sb("chosen", [P, 2, P])
        extra_list = sb("extra_list", [P, 1], I32)
        empty_dist = sb("empty_dist", [1, P])
        empty_ids = sb("empty_ids", [1, P], I32)
        beyond = sb("beyond", [P, 2])
        dst_left = sb("dst_left", [P, MACRO])

        x_ring = sb("x_ring", [NODE_TILE, RING, 512])
        y_ring = sb("y_ring", [NODE_TILE, RING, 512])
        x_t = sb("x_t", [P, 2, 512])
        stats = sb("stats", [NODE_TILE, 2, CHUNK, 6])
        mean_var = sb("mean_var", [NODE_TILE, 2, CHUNK, 2])
        rstd = sb("rstd", [NODE_TILE, 2, CHUNK])
        shift = sb("shift", [NODE_TILE, 2, CHUNK])
        minus_half = sb("minus_half", [NODE_TILE, CHUNK])
        pre_norm = sb("pre_norm", [NODE_TILE, 2, 512])

        def bank(name):
            return ctx.enter_context(nc.psum_tensor(name, [P, 512], F32))

        ps_h = [bank("ps_h0"), bank("ps_h1")]
        ps_w = [bank("ps_w0"), bank("ps_w1")]
        ps_sum = [bank("ps_sum0"), bank("ps_sum1")]
        ps_rows = bank("ps_rows")
        ps_misc = bank("ps_misc")

        weights_loaded = sem("weights_loaded")
        fw1_loaded = sem("fw1_loaded")
        fw1_cleared = sem("fw1_cleared")
        const_built = sem("const_built")
        pool_step = sem("pool_step")
        dve_step = sem("dve_step")
        biases_split = sem("biases_split")
        bias_placed = sem("bias_placed")
        weights_ready = sem("weights_ready")

        x_loaded = [sem(f"x_loaded{i}") for i in range(RING)]
        x_turned = sem("x_turned")
        x_t_ready = sem("x_t_ready")
        projected = sem("projected")
        proj_copied = sem("proj_copied")
        proj_stored = [sem(f"proj_stored{i}") for i in range(RING)]
        proj_table = sem("proj_table")

        edges_loaded = sem("edges_loaded")
        compacted = sem("compacted")
        rows_stored = sem("rows_stored")
        empty_stored = sem("empty_stored")

        class Pass:

            def __init__(self, name):
                self.rows_ready = sem(name + "_rows_ready")
                self.turned = sem(name + "_turned")
                self.base_ready = sem(name + "_base_ready")
                self.base_spread = sem(name + "_base_spread")
                self.tables_ready = sem(name + "_tables_ready")
                self.dist_loaded = [sem(f"{name}_dist_loaded{i}") for i in range(2)]
                self.squared = sem(name + "_squared")
                self.rbf_ready = sem(name + "_rbf_ready")
                self.h_ready = sem(name + "_h_ready")
                self.tanh_ready = sem(name + "_tanh_ready")
                self.act_ready = sem(name + "_act_ready")
                self.w_ready = sem(name + "_w_ready")
                self.gathered = [sem(f"{name}_gathered{i}") for i in range(8)]
                self.index_ready = sem(name + "_index_ready")
                self.msg_ready = sem(name + "_msg_ready")
                self.summed = sem(name + "_summed")
                self.added = sem(name + "_added")

        main = Pass("main")
        extra = Pass("extra")
        general = Pass("general")
        extra_flagged = sem("extra_flagged")
        extra_counted = sem("extra_counted")
        n_extra_ready = sem("n_extra_ready")
        chosen_ready = sem("chosen_ready")
        chosen_used = sem("chosen_used")
        list_ready = sem("list_ready")
        extra_step = sem("extra_step")
        extra_rows_loaded = sem("extra_rows_loaded")
        extra_dist_stored = sem("extra_dist_stored")
        beyond_flagged = sem("beyond_flagged")
        beyond_counted = sem("beyond_counted")
        outside_ready = sem("outside_ready")
        extra_rows_free = sem("extra_rows_free")
        general_slots_free = sem("general_slots_free")
        general_step = sem("general_step")
        general_rows_loaded = sem("general_rows_loaded")
        wide_members = sem("wide_members")
        wide_moved = sem("wide_moved")

        agg_done = sem("agg_done")
        node_step = sem("node_step")
        node_h = sem("node_h")
        node_tanh = sem("node_tanh")
        node_act = sem("node_act")
        node_out = sem("node_out")
        node_stats = sem("node_stats")
        node_scaled = sem("node_scaled")
        node_normed = sem("node_normed")
        x_again = [sem(f"x_again{i}") for i in range(RING)]
        out_stored = [sem(f"out_stored{i}") for i in range(RING)]

        paused = sem("paused")

        def wait_apart(engine, semaphore, value):
            engine.wait_ge(semaphore, value)
            engine.sem_inc(paused, 1)

        block = ctx.enter_context(nc.Block())

        @block.sync
        def _(sp):
            def load_edges(g):
                sp.dma_start(dist[:, 0:EDGE_COLS], edge_rows[0][bass.ds(g * P, P), :]).then_inc(edges_loaded, 16)
                sp.dma_start(src_in[:, :], edge_rows[1][bass.ds(g * P, P), :]).then_inc(edges_loaded, 16)
                sp.dma_start(dst_in[:, :], edge_rows[2][bass.ds(g * P, P), :]).then_inc(edges_loaded, 16)

            def store_rows(g):
                sp.wait_ge(compacted, g + 1)
                sp.wait_ge(main.tables_ready, g + 1)
                sp.dma_start(dist_rows[bass.ds(g * P, P), :], dist[:, :]).then_inc(rows_stored, 16)
                sp.dma_start(ids_rows[bass.ds(g * P, P), :], ids[:, :]).then_inc(rows_stored, 16)
                sp.wait_ge(rows_stored, 32 * (g + 1))

            sp.sem_inc(extra_rows_free, 1)
            load_edges(0)
            sp.dma_start(pw_sb[:, :], pw).then_inc(weights_loaded, 16)
            sp.dma_start(mw1_sb[:, :], mw1).then_inc(weights_loaded, 16)
            sp.dma_start(raw_w[:, 0, :], fw2).then_inc(weights_loaded, 16)
            sp.dma_start(raw_w[:, 1, :], mw2).then_inc(weights_loaded, 16)
            for i, b in enumerate((fb2, pb, mb2, mb1)):
                sp.dma_start(bias_in[0:1, i, :], b.rearrange("(a n) -> a n", a=1)).then_inc(weights_loaded, 16)
            sp.wait_ge(fw1_cleared, 1)
            for half in range(2):
                sp.dma_start(fw1_halves[64 * half:64 * half + RBF, half, :], fw1).then_inc(fw1_loaded, 16)
                sp.dma_start(fw1_halves[64 * half + RBF:64 * half + RBF + 1, half, :],
                             fb1.rearrange("(a n) -> a n", a=1)).then_inc(fw1_loaded, 16)
            sp.wait_ge(biases_split, 1)
            for part in range(3):
                sp.dma_start(bias_lanes[part:part + 1, :, :], bias_parts[0:1, part, :, :]).then_inc(bias_placed, 16)

            def load_x(i, sems, slot):
                sp.dma_start(x_ring[:, slot, :].rearrange("p (j f) -> p j f", f=P),
                             x_nodes[:, bass.ds(i * CHUNK, CHUNK), :]).then_inc(sems[slot], 16)

            def store_proj(i, slot):
                sp.wait_ge(proj_copied, i + 1)
                sp.dma_start(proj_nodes[:, bass.ds(i * CHUNK, CHUNK), :],
                             y_ring[:, slot, :].rearrange("p (j f) -> p j f", f=P)).then_inc(proj_stored[slot], 16)

            for i in range(RING):
                load_x(i, x_loaded, i)
            for i in range(CHUNKS):
                if i + RING < CHUNKS:
                    sp.wait_ge(x_turned, i + 1)
                    load_x(i + RING, x_loaded, i % RING)
                store_proj(i, i % RING)
            for slot in range(RING):
                sp.wait_ge(proj_stored[slot], 16 * len(range(slot, CHUNKS, RING)))
            sp.sem_inc(proj_table, 1)

            def load_unit(tiles, stride_rows, unit, parity, loaded):
                rows = tiles[bass.ds(unit * (UNIT * stride_rows), UNIT * stride_rows), :]
                for half in range(2):
                    v = rows.rearrange("(k h b) s -> h b k s", h=2, b=stride_rows)[half, 0]
                    sp.dma_start(dist_bc[64 * half:64 * half + 64, parity, :, :]
                                 .rearrange("p m (t s) -> p (m t) s", s=P),
                                 v.partition_broadcast(64)).then_inc(loaded[parity], 16)

            store_rows(0)
            load_edges(1)

            def group(g, last, next_edges):
                for q in range(UNITS):
                    unit = g * UNITS + q
                    if not (isinstance(unit, int) and unit < 2):
                        sp.wait_ge(main.squared, unit)
                    load_unit(dist_tiles, BLOCKS, unit, q % 2, main.dist_loaded)
                if not last:
                    store_rows(g + 1)
                if next_edges:
                    load_edges(g + 2)

            group(0, False, True)
            with sp.Fori(1, GROUPS - 2) as g:
                group(g, False, True)
            group(GROUPS - 2, False, False)
            group(GROUPS - 1, True, False)

            sp.wait_ge(const_built, 2)
            sp.dma_start(dist_tiles[ALL_TILES:ALL_TILES + 1, :], empty_dist[:, :]).then_inc(empty_stored, 16)
            sp.dma_start(ids_tiles[ALL_TILES:ALL_TILES + 1, :], empty_ids[:, :]).then_inc(empty_stored, 16)
            sp.wait_ge(empty_stored, 32)
            sp.wait_ge(main.squared, GROUPS * UNITS + 1)

            sp.wait_ge(n_extra_ready, 1)
            n_extra = sp.value_load(n_extra_i[0:1, 0:1], min_val=0, max_val=EXTRA_TILES)
            with sp.Fori(0, EXTRA_GROUPS) as k:
                with sp.If(n_extra > k * P):
                    sp.wait_ge(extra_rows_loaded, 32 * (k + 1))
                    sp.dma_start(extra_dist[bass.ds(k * P, P), :], row_dist[:, :]).then_inc(extra_dist_stored, 16)
                    sp.wait_ge(extra_dist_stored, 16 * (k + 1))
                    sp.sem_inc(extra_rows_free, 1)
                    wait_apart(sp, extra.squared, k * UNITS + 1)
                    for q in range(UNITS):
                        with sp.If(n_extra > k * P + q * UNIT):
                            if q >= 2:
                                sp.wait_ge(extra.squared, k * UNITS + q)
                            load_unit(extra_dist, 1, k * UNITS + q, q % 2, extra.dist_loaded)

            sp.wait_ge(outside_ready, 1)
            outside = sp.value_load(outside_i[0:1, 0:1], min_val=0, max_val=2 * P)
            with sp.If(outside > 0):
                with sp.Fori(0, ALL_GROUPS) as k:
                    sp.wait_ge(general.tables_ready, k + 1)
                    sp.dma_start(row_dist[:, :], dist_tiles[bass.ds(k * P, P), :]).then_inc(general_rows_loaded, 16)
                    sp.dma_start(row_ids[:, :], ids_tiles[bass.ds(k * P, P), :]).then_inc(general_rows_loaded, 16)
                    for q in range(UNITS):
                        sp.wait_ge(general.squared, k * UNITS + (q + 1))
                        load_unit(dist_tiles, 1, k * UNITS + q, 0, general.dist_loaded)

            def load_x_again(i, slot):
                load_x(i, x_again, slot)

            for i in range(RING):
                load_x_again(i, i)
            for i in range(CHUNKS):
                sp.wait_ge(node_normed, i + 1)
                sp.dma_start(out_nodes[:, i * CHUNK:(i + 1) * CHUNK, :],
                             y_ring[:, i % RING, :].rearrange("p (j f) -> p j f", f=P))\
                  .then_inc(out_stored[i % RING], 16)
                if i + RING < CHUNKS:
                    load_x_again(i + RING, i % RING)
            for slot in range(RING):
                sp.wait_ge(out_stored[slot], 16 * len(range(slot, CHUNKS, RING)))

        @block.gpsimd
        def _(pool):
            n = [0]

            def step(ins):
                n[0] += 1
                ins.then_inc(pool_step, 1)
                pool.wait_ge(pool_step, n[0])

            step(nc.gpsimd.memset(fw1_halves[:, :, :], 0.0))
            pool.sem_inc(fw1_cleared, 1)
            step(nc.gpsimd.iota(iota_i[:, :], pattern=[[1, ROW_SLOTS]], base=0, channel_multiplier=0))
            step(nc.gpsimd.iota(lane_i[:, :], pattern=[[1, 1]], base=0, channel_multiplier=1))
            step(nc.gpsimd.memset(ident[:, :], 0.0))
            step(nc.gpsimd.affine_select(out=ident[:, :], in_=ident[:, :], compare_op=ALU.not_equal, fill=1.0,
                                         base=0, pattern=[[-1, P]], channel_multiplier=1))
            step(nc.gpsimd.memset(ids[:, EDGE_COLS:ROW_SLOTS], 0))
            step(nc.gpsimd.memset(dist[:, EDGE_COLS:ROW_SLOTS], FAR))
            step(nc.gpsimd.memset(ones_cols[:, :], 1.0))
            step(nc.gpsimd.memset(bias_lanes[:, :, :], 0.0))
            step(nc.gpsimd.memset(one_lanes[:, :], 0.0))
            step(nc.gpsimd.memset(one_lanes[0:3, :], 1.0))
            pool.sem_inc(const_built, 1)
            step(nc.gpsimd.memset(all_ones[:, :], 1.0))
            step(nc.gpsimd.memset(ones_row[:, :], 1.0))
            step(nc.gpsimd.affine_select(out=before[:, :], in_=all_ones[:, :], compare_op=ALU.is_gt, fill=0.0,
                                         base=0, pattern=[[1, P]], channel_multiplier=-1))
            step(nc.gpsimd.iota(tile_id_i[:, :, :], pattern=[[P * BLOCKS, GROUPS], [1, BLOCKS - 1]],
                                base=1, channel_multiplier=BLOCKS))
            step(nc.gpsimd.memset(agg[:, :], 0.0))
            step(nc.gpsimd.memset(minus_half[:, :], -0.5))
            step(nc.gpsimd.memset(empty_dist[:, :], FAR))
            step(nc.gpsimd.memset(empty_ids[:, :], 0))
            pool.sem_inc(const_built, 1)
            pool.wait_ge(proj_table, 1)

            def gather_tile(table, c, slot, done):
                nc.gpsimd.indirect_dma_start(
                    out=gathered[:, slot, :], out_offset=None, in_=proj,
                    in_offset=bass.IndirectOffsetOnAxis(ap=table[:, c:c + 1], axis=0)).then_inc(done, 16)

            def gather_unit(p, unit, parity, first):
                pool.wait_ge(p.index_ready, unit + 1)
                for j in range(MACRO):
                    if not first:
                        wait_apart(pool, p.msg_ready, unit * MACRO + (j - 7))
                    for t in range(MACRO):
                        c = MACRO * j + ORDER[t]
                        gather_tile(index[:, parity, :], c, UNIT * parity + MACRO * j + t,
                                    p.gathered[MACRO * parity + j])

            for parity in range(2):
                gather_unit(main, parity, parity, True)
            with pool.Fori(2, GROUPS * UNITS, 2) as u:
                for parity in range(2):
                    gather_unit(main, u + parity, parity, False)

            pool.wait_ge(empty_stored, 32)
            pool.wait_ge(rows_stored, 32 * GROUPS)
            pool.wait_ge(n_extra_ready, 1)
            n_extra = pool.value_load(n_extra_i[0:1, 0:1], min_val=0, max_val=EXTRA_TILES)
            with pool.Fori(0, EXTRA_GROUPS) as k:
                with pool.If(n_extra > k * P):
                    pool.wait_ge(list_ready, k + 1)
                    wait_apart(pool, extra_rows_free, k + 1)
                    for rows, tiles in ((row_dist, dist_tiles), (row_ids, ids_tiles)):
                        nc.gpsimd.indirect_dma_start(
                            out=rows[:, :], out_offset=None, in_=tiles,
                            in_offset=bass.IndirectOffsetOnAxis(ap=extra_list[:, 0:1], axis=0),
                        ).then_inc(extra_rows_loaded, 16)
                    wait_apart(pool, extra.index_ready, k + 1)
                    for q in range(UNITS):
                        with pool.If(n_extra > k * P + q * UNIT):
                            for j in range(MACRO):
                                if q >= 2:
                                    wait_apart(pool, extra.msg_ready, k * MACROS + (MACRO * q + j - 7))
                                for t in range(MACRO):
                                    gather_tile(src_now, UNIT * q + MACRO * j + ORDER[t],
                                                UNIT * (q % 2) + MACRO * j + t, extra.gathered[MACRO * (q % 2) + j])

            pool.wait_ge(outside_ready, 1)
            outside = pool.value_load(outside_i[0:1, 0:1], min_val=0, max_val=2 * P)
            with pool.If(outside > 0):
                with pool.Fori(0, ALL_GROUPS) as k:
                    pool.wait_ge(general.index_ready, k + 1)
                    for q in range(UNITS):
                        wait_apart(pool, general_slots_free, k * UNITS + (q + 1))
                        for j in range(MACRO):
                            for t in range(MACRO):
                                gather_tile(src_now, UNIT * q + MACRO * j + ORDER[t], MACRO * j + t,
                                            general.gathered[j])

            for i in range(CHUNKS):
                pool.wait_ge(node_stats, i + 1)
                if i >= 2:
                    pool.wait_ge(node_normed, i - 1)
                step(nc.gpsimd.tensor_scalar(shift[:, i % 2, :], mean_var[:, i % 2, :, 1], EPS, None, ALU.add))
                step(nc.gpsimd.tensor_tensor(rstd[:, i % 2, :], shift[:, i % 2, :], minus_half[:, :], ALU.pow))
                step(nc.gpsimd.tensor_tensor(shift[:, i % 2, :], mean_var[:, i % 2, :, 0], rstd[:, i % 2, :], ALU.mult))
                step(nc.gpsimd.tensor_scalar(shift[:, i % 2, :], shift[:, i % 2, :], -1.0, None, ALU.mult))
                pool.sem_inc(node_scaled, 1)

        @block.scalar
        def _(act):
            for p in (main, extra, general):
                act.sem_inc(p.squared, 1)
            for i in range(CHUNKS):
                act.wait_ge(x_turned, i + 1)
                if i >= 2:
                    act.wait_ge(projected, i - 1)
                nc.scalar.activation(x_t[:, i % 2, 0:CHUNK_NODES], ps_h[i % 2][:, 0:CHUNK_NODES], ACT.Copy)\
                  .then_inc(x_t_ready, 1)
                act.wait_ge(projected, i + 1)
                if i >= RING:
                    act.wait_ge(proj_stored[i % RING], 16 * (i // RING))
                nc.scalar.activation(y_ring[:, i % RING, :], ps_w[i % 2][0:NODE_TILE, :], ACT.Copy)\
                  .then_inc(proj_copied, 1)

            act.wait_ge(weights_ready, 1)

            def radial(p, unit, parity, wait=True):
                if wait:
                    act.wait_ge(p.dist_loaded[parity], 16 * (unit + (2 - parity)))
                nc.scalar.activation(square[:, :], dist_bc[:, parity, :, :], ACT.Square,
                                     bias=rbf_shift[:, 0:1], scale=rbf_scale[:, 0:1]).then_inc(p.squared, 1)
                act.wait_ge(p.squared, unit + 2)
                nc.scalar.activation(rbf[:, parity, :, :], square[:, :], ACT.Exp,
                                     scale=-1.0 / (2.0 * WIDTH * WIDTH)).then_inc(p.rbf_ready, 1)

            def tanh(p, macro, parity):
                act.wait_ge(p.h_ready, macro + 1)
                nc.scalar.activation(half_tanh[:, parity, :], ps_h[parity][:, :], ACT.Tanh, scale=0.5)\
                  .then_inc(p.tanh_ready, 1)

            def pair(u, last):
                for parity in range(2):
                    for j in range(MACRO):
                        if j == MACRO - 1 and not (last and parity):
                            radial(main, u + (parity + 1), 1 - parity)
                        tanh(main, u * MACRO + (MACRO * parity + j), j % 2)

            radial(main, 0, 0)
            with act.Fori(0, GROUPS * UNITS - 2, 2) as u:
                pair(u, False)
            pair(GROUPS * UNITS - 2, True)

            act.wait_ge(n_extra_ready, 1)
            n_extra = act.value_load(n_extra_i[0:1, 0:1], min_val=0, max_val=EXTRA_TILES)
            with act.Fori(0, EXTRA_GROUPS) as k:
                with act.If(n_extra > k * P):
                    for q in range(UNITS):
                        with act.If(n_extra > k * P + q * UNIT):
                            radial(extra, k * UNITS + q, q % 2)
                            for j in range(MACRO):
                                tanh(extra, k * MACROS + (MACRO * q + j), j % 2)

            act.wait_ge(outside_ready, 1)
            outside = act.value_load(outside_i[0:1, 0:1], min_val=0, max_val=2 * P)
            with act.If(outside > 0):
                with act.Fori(0, ALL_GROUPS * UNITS) as u:
                    act.wait_ge(general.dist_loaded[0], 32 * (u + 1))
                    radial(general, u, 0, wait=False)
                    for j in range(MACRO):
                        tanh(general, u * MACRO + j, j % 2)

            for i in range(CHUNKS + 1):
                if i < CHUNKS:
                    act.wait_ge(node_h, i + 1)
                    nc.scalar.activation(half_tanh[:, i % 2, 0:CHUNK_NODES], ps_h[i % 2][:, 0:CHUNK_NODES],
                                         ACT.Tanh, scale=0.5).then_inc(node_tanh, 1)
                if i >= 1:
                    k = i - 1
                    act.wait_ge(node_scaled, k + 1)
                    if k >= RING:
                        act.wait_ge(out_stored[k % RING], 16 * (k // RING))
                    for t in range(CHUNK):
                        last = nc.scalar.activation(y_ring[:, k % RING, t * P:(t + 1) * P],
                                                    pre_norm[:, k % 2, t * P:(t + 1) * P], ACT.Identity,
                                                    scale=rstd[:, k % 2, t:t + 1], bias=shift[:, k % 2, t:t + 1])
                    last.then_inc(node_normed, 1)

        @block.tensor
        def _(pe):
            pe.wait_ge(const_built, 1)
            pe.wait_ge(weights_ready, 1)

            def turn(i):
                pe.wait_ge(x_loaded[i % RING], 16 * (i // RING + 1))
                if i >= 2:
                    pe.wait_ge(x_t_ready, i - 1)
                for t in range(CHUNK):
                    last = nc.tensor.transpose(ps_h[i % 2][:, t * NODE_TILE:(t + 1) * NODE_TILE],
                                               x_ring[:, i % RING, t * P:(t + 1) * P],
                                               ident[0:NODE_TILE, 0:NODE_TILE])
                last.then_inc(x_turned, 1)

            def project(i):
                pe.wait_ge(x_t_ready, i + 1)
                if i >= 2:
                    pe.wait_ge(proj_copied, i - 1)
                nc.tensor.matmul(ps_w[i % 2][0:NODE_TILE, :], one_lanes[:, 0:NODE_TILE],
                                 bias_rhs[:, 1, :, :], start=True, stop=False, skip_group_check=True)
                for t in range(CHUNK):
                    last = nc.tensor.matmul(ps_w[i % 2][0:NODE_TILE, t * P:(t + 1) * P],
                                            x_t[:, i % 2, t * NODE_TILE:(t + 1) * NODE_TILE], pw_sb[:, :],
                                            start=False, stop=True, skip_group_check=True)
                last.then_inc(projected, 1)

            turn(0)
            for i in range(CHUNKS):
                if i + 1 < CHUNKS:
                    turn(i + 1)
                project(i)

            def tables(p, k, windows):
                pe.wait_ge(p.rows_ready, k + 1)
                for c, t in enumerate((row_src, row_dst, row_cut)):
                    nc.tensor.transpose(ps_rows[:, c * P:(c + 1) * P], t[:, :], ident[:, :])
                nc.tensor.transpose(ps_rows[0:1, 3 * P:4 * P], row_min[:, :], ident[:, :]).then_inc(p.turned, 1)
                if windows == 0:
                    return
                pe.wait_ge(p.base_ready, k + 1)
                nc.tensor.matmul(ps_misc[:, 0:windows], ones_row[0:1, :], base_f[0:1, 0:windows],
                                 start=True, stop=True).then_inc(p.base_spread, 1)

            def first_layer(p, n, units):
                pe.wait_ge(p.rbf_ready, units)
                for half in range(2):
                    last = nc.tensor.matmul(ps_h[n % 2][:, 256 * half:256 * half + 256], fw1_halves[:, half, :],
                                            rbf[:, (n // MACRO) % 2, n % MACRO, :], start=True, stop=True)
                last.then_inc(p.h_ready, 1)

            def second_layer(p, macro, n):
                pe.wait_ge(p.act_ready, macro + 1)
                nc.tensor.matmul(ps_w[n % 2][:, :], one_lanes[:, 0:P], bias_rhs[:, 0, :, :],
                                 start=True, stop=False, skip_group_check=True)
                for t in range(MACRO):
                    last = nc.tensor.matmul(ps_w[n % 2][:, t * P:(t + 1) * P], act_t[:, n % 2, t * P:(t + 1) * P],
                                            fw2_half[:, :], start=False, stop=True, skip_group_check=True)
                last.then_inc(p.w_ready, 1)

            def sum_shared(p, macro, n, bank_wait):
                pe.wait_ge(p.msg_ready, macro + 1)
                if bank_wait is not None:
                    pe.wait_ge(p.added, bank_wait + 1)
                for t in range(MACRO):
                    last = nc.tensor.matmul(ps_sum[n % 2][:, 0:WINDOW], message[:, n % 2, t * P:(t + 1) * P],
                                            member[:, n % 2, t, :], start=(t == 0), stop=(t == MACRO - 1))
                last.then_inc(p.summed, 1)

            def group(g, last):
                at = g * MACROS
                unit = g * UNITS
                first_layer(main, 0, unit + 1)
                for n in range(MACROS):
                    if n + 1 < MACROS:
                        first_layer(main, n + 1, unit + ((n + 1) // MACRO + 1))
                    second_layer(main, at + n, n)
                    if n >= 1:
                        sum_shared(main, at + (n - 1), n - 1, at if n == 1 else at + (n - 2) if n >= 3 else None)
                    if n == 24 and not last:
                        tables(main, g + 1, MACROS)
                sum_shared(main, at + (MACROS - 1), MACROS - 1, at + (MACROS - 2))

            pe.wait_ge(const_built, 2)
            tables(main, 0, MACROS)
            with pe.Fori(0, GROUPS - 1) as g:
                group(g, False)
            group(GROUPS - 1, True)

            def sum_single(p, macro, n, bank_wait):
                pe.wait_ge(p.msg_ready, macro + 1)
                pe.wait_ge(p.added, bank_wait + 1)
                for t in range(MACRO):
                    last = nc.tensor.matmul(ps_sum[n % 2][:, WINDOW1 * t:WINDOW1 * (t + 1)],
                                            message[:, n % 2, t * P:(t + 1) * P], member[:, n % 2, t, 0:WINDOW1],
                                            start=True, stop=True)
                last.then_inc(p.summed, 1)

            pe.wait_ge(extra_flagged, 1)
            nc.tensor.matmul(ps_misc[:, 0:1], before[:, :], total[:, :], start=True, stop=True)
            nc.tensor.matmul(ps_misc[:, 1:2], all_ones[:, :], total[:, :], start=True, stop=True)\
              .then_inc(extra_counted, 1)
            pe.wait_ge(n_extra_ready, 1)
            n_extra = pe.value_load(n_extra_i[0:1, 0:1], min_val=0, max_val=EXTRA_TILES)
            with pe.Fori(0, EXTRA_GROUPS) as k:
                with pe.If(n_extra > k * P):
                    choices = GROUPS * (BLOCKS - 1)
                    ids_flat = tile_id[:, :, :].rearrange("p g b -> p (g b)")
                    for c in range(choices):
                        pe.wait_ge(chosen_ready, k * choices + (c + 1))
                        nc.tensor.matmul(ps_misc[:, 0:1], chosen[:, c % 2, :], ids_flat[:, c:c + 1],
                                         start=(c == 0), stop=(c == choices - 1)).then_inc(chosen_used, 1)
                    tables(extra, k, P)
                    for q in range(UNITS):
                        with pe.If(n_extra > k * P + q * UNIT):
                            at, unit = k * MACROS, k * UNITS + q
                            m = MACRO * q
                            first_layer(extra, m, unit + 1)
                            for j in range(MACRO):
                                if j + 1 < MACRO:
                                    first_layer(extra, m + j + 1, unit + 1)
                                second_layer(extra, at + (m + j), m + j)
                                if j >= 1:
                                    sum_single(extra, at + (m + j - 1), m + j - 1,
                                               MACRO * (at + (m + max(j - 2, 0))))
                            sum_single(extra, at + (m + MACRO - 1), m + MACRO - 1, MACRO * (at + (m + MACRO - 2)))

            pe.wait_ge(beyond_flagged, 1)
            nc.tensor.matmul(ps_misc[:, 0:1], all_ones[:, :], beyond[:, 0:1], start=True, stop=True)\
              .then_inc(beyond_counted, 1)
            pe.wait_ge(outside_ready, 1)
            outside = pe.value_load(outside_i[0:1, 0:1], min_val=0, max_val=2 * P)
            with pe.If(outside > 0):
                with pe.Fori(0, ALL_GROUPS) as k:
                    tables(general, k, 0)
                    for q in range(UNITS):
                        for j in range(MACRO):
                            macro = k * MACROS + (MACRO * q + j)
                            first_layer(general, j, k * UNITS + (q + 1))
                            second_layer(general, macro, j)
                            wait_apart(pe, general.msg_ready, macro + 1)
                            with pe.Fori(0, ALL_WINDOWS) as w:
                                pe.wait_ge(wide_members, macro * ALL_WINDOWS + w + 1)
                                for t in range(MACRO):
                                    last = nc.tensor.matmul(
                                        ps_sum[0][:, 0:WIDE], message[:, j % 2, t * P:(t + 1) * P],
                                        gathered[:, UNIT + MACRO * t:UNIT + MACRO * (t + 1), :],
                                        start=(t == 0), stop=(t == MACRO - 1))
                                last.then_inc(general.summed, 1)

            def node_first(i):
                if i >= 2:
                    pe.wait_ge(node_act, i - 1)
                nc.tensor.matmul(ps_h[i % 2][:, 0:CHUNK_NODES], bias_lanes[:, 3, :], one_lanes[:, 0:CHUNK_NODES],
                                 start=True, stop=False, skip_group_check=True)
                nc.tensor.matmul(ps_h[i % 2][:, 0:CHUNK_NODES], mw1_sb[:, :],
                                 agg[:, i * CHUNK_NODES:(i + 1) * CHUNK_NODES],
                                 start=False, stop=True, skip_group_check=True).then_inc(node_h, 1)

            def node_second(i):
                pe.wait_ge(node_act, i + 1)
                if i >= 2:
                    pe.wait_ge(node_scaled, i - 1)
                nc.tensor.matmul(ps_w[i % 2][0:NODE_TILE, :], one_lanes[:, 0:NODE_TILE], bias_rhs[:, 2, :, :],
                                 start=True, stop=False, skip_group_check=True)
                for t in range(CHUNK):
                    last = nc.tensor.matmul(ps_w[i % 2][0:NODE_TILE, t * P:(t + 1) * P],
                                            act_t[:, i % 2, t * NODE_TILE:(t + 1) * NODE_TILE], mw2_half[:, :],
                                            start=False, stop=True, skip_group_check=True)
                last.then_inc(node_out, 1)

            pe.wait_ge(agg_done, 1)
            node_first(0)
            for i in range(CHUNKS):
                if i + 1 < CHUNKS:
                    node_first(i + 1)
                node_second(i)

        @block.vector
        def _(dve):
            at = {"n": 0, "base": 0, "sem": dve_step}

            def step(ins):
                at["n"] += 1
                ins.then_inc(at["sem"], 1)

            def settle():
                dve.wait_ge(at["sem"], at["base"] + at["n"])

            def done(ins):
                step(ins)
                settle()

            V = nc.vector
            for p in (main, extra, general):
                dve.sem_inc(p.added, 1)
            dve.sem_inc(general.tables_ready, 1)
            dve.sem_inc(general_slots_free, 1)
            dve.wait_ge(weights_loaded, 8 * 16)
            dve.wait_ge(const_built, 1)
            done(V.tensor_copy(bias_parts[0:1, 0, :, :], bias_in[0:1, :, :]))
            done(V.tensor_tensor(bias_rest[0:1, :, :], bias_in[0:1, :, :], bias_parts[0:1, 0, :, :], ALU.subtract))
            done(V.tensor_copy(bias_parts[0:1, 1, :, :], bias_rest[0:1, :, :]))
            done(V.tensor_tensor(bias_rest[0:1, :, :], bias_rest[0:1, :, :], bias_parts[0:1, 1, :, :], ALU.subtract))
            done(V.tensor_copy(bias_parts[0:1, 2, :, :], bias_rest[0:1, :, :]))
            dve.sem_inc(biases_split, 1)
            step(V.tensor_scalar(fw2_half[:, :], raw_w[:, 0, :], 0.5, None, ALU.mult))
            step(V.tensor_scalar(mw2_half[:, :], raw_w[:, 1, :], 0.5, None, ALU.mult))
            step(V.tensor_copy(iota_f[:, :], iota_i[:, :]))
            done(V.tensor_scalar(lane_i[:, :], lane_i[:, :], 63, None, ALU.bitwise_and))
            done(V.tensor_copy(lane_f[:, :], lane_i[:, :]))
            done(V.tensor_scalar(rbf_scale[:, :], lane_f[:, :], float(RBF), None, ALU.is_lt))
            done(V.scalar_tensor_tensor(out=rbf_shift[:, :], in0=lane_f[:, :], scalar=-CUTOFF / (RBF - 1),
                                        in1=rbf_scale[:, :], op0=ALU.mult, op1=ALU.mult))
            step(V.memset(farthest[:, :], 0.0))
            dve.wait_ge(bias_placed, 48)
            dve.wait_ge(fw1_loaded, 64)
            for k in range(3):
                for t in range(CHUNK):
                    step(V.tensor_copy(bias_rhs[:, k, t, :], bias_lanes[:, k, :]))
            settle()
            dve.sem_inc(weights_ready, 1)

            def drop_far(g):
                dve.wait_ge(edges_loaded, 48 * (g + 1))
                step(V.tensor_scalar(drop[:, 0:EDGE_COLS], dist[:, 0:EDGE_COLS], CUTOFF, None, ALU.is_gt))
                done(V.tensor_scalar(dst_in[:, :], dst_in[:, :], ID_BITS, None, ALU.logical_shift_left))
                step(V.tensor_tensor_scan(dropped[:, :], ones_cols[:, :], drop[:, 0:EDGE_COLS], 0.0,
                                          ALU.mult, ALU.add))
                step(V.tensor_tensor(ids[:, 0:EDGE_COLS], src_in[:, :], dst_in[:, :], ALU.bitwise_or))
                settle()
                step(V.scalar_tensor_tensor(out=move[0][:, :], in0=dist[:, 0:EDGE_COLS], scalar=CUTOFF,
                                            in1=dropped[:, :], op0=ALU.is_le, op1=ALU.mult))
                done(V.tensor_scalar(counts[:, bass.ds(g, 1)], dropped[:, EDGE_COLS - 1:EDGE_COLS], -1.0,
                                     float(EDGE_COLS), ALU.mult, ALU.add))

            def shift_by(k):
                s, now, new = 1 << k, move[k % 2], move[1 - k % 2]
                keep = EDGE_COLS - s
                step(V.tensor_scalar(moves_now[:, :], now[:, :], s, None, ALU.bitwise_and))
                settle()
                step(V.scalar_tensor_tensor(out=new[:, :], in0=moves_now[:, :], scalar=0.0, in1=now[:, :],
                                            op0=ALU.is_equal, op1=ALU.mult))
                step(V.copy_predicated(dist[:, 0:keep], moves_now[:, s:EDGE_COLS], dist[:, s:EDGE_COLS]))
                step(V.copy_predicated(ids[:, 0:keep], moves_now[:, s:EDGE_COLS], ids[:, s:EDGE_COLS]))
                settle()
                dve.sem_inc(paused, 1)
                done(V.copy_predicated(new[:, 0:keep], moves_now[:, s:EDGE_COLS], now[:, s:EDGE_COLS]))

            def clear_empty(g):
                done(V.tensor_scalar(drop[:, :], iota_f[:, :], counts[:, bass.ds(g, 1)], FAR,
                                     ALU.is_ge, ALU.mult))
                done(V.scalar_tensor_tensor(out=dist[:, :], in0=dist[:, :], scalar=FAR, in1=drop[:, :],
                                            op0=ALU.min, op1=ALU.max))
                dve.sem_inc(compacted, 1)

            def tables(p, k, row_d, row_i, windows, window, which):
                done(V.tensor_scalar(row_int[:, 0, :], row_d, 0.5 / CUTOFF, None, ALU.mult))
                done(V.scalar_tensor_tensor(out=row_a[:, :], in0=row_int[:, 0, :], scalar=-2.0 * CUTOFF, in1=row_d,
                                            op0=ALU.mult, op1=ALU.add))
                done(V.scalar_tensor_tensor(out=row_a[:, :], in0=row_a[:, :], scalar=-1.0, in1=row_a[:, :],
                                            op0=ALU.mult, op1=ALU.max))
                step(V.tensor_scalar(row_int[:, 0, :], row_i, ID_MASK, None, ALU.bitwise_and))
                step(V.tensor_scalar(row_int[:, 1, :], row_i, ID_BITS, None, ALU.logical_shift_right))
                done(V.tensor_scalar(row_b[:, :], row_a[:, :], -1.0, 2.0 * CUTOFF, ALU.mult, ALU.add))
                step(V.tensor_copy(row_src[:, :], row_int[:, 0, :]))
                step(V.tensor_copy(row_dst[:, :], row_int[:, 1, :]))
                done(V.tensor_tensor(row_a[:, :], row_a[:, :], row_b[:, :], ALU.min))
                done(V.scalar_tensor_tensor(out=row_b[:, :], in0=row_a[:, :], scalar=(math.pi / (2 * CUTOFF)) ** 2,
                                            in1=row_a[:, :], op0=ALU.mult, op1=ALU.mult))
                done(V.tensor_scalar(row_a[:, :], row_b[:, :], COS[8], None, ALU.mult))
                for c in range(7, 0, -1):
                    done(V.scalar_tensor_tensor(out=row_a[:, :], in0=row_a[:, :], scalar=COS[c], in1=row_b[:, :],
                                                op0=ALU.add, op1=ALU.mult))
                done(V.tensor_scalar(row_a[:, :], row_a[:, :], 1.0, None, ALU.add))
                done(V.tensor_tensor(row_a[:, :], row_a[:, :], row_a[:, :], ALU.mult))
                step(V.scalar_tensor_tensor(out=row_cut[:, :], in0=row_d, scalar=CUTOFF, in1=row_a[:, :],
                                            op0=ALU.is_le, op1=ALU.mult))
                done(V.tensor_scalar(row_b[:, :], row_d, CUTOFF, NO_NODE, ALU.is_gt, ALU.mult))
                done(V.tensor_tensor(row_b[:, :], row_b[:, :], row_dst[:, :], ALU.add))
                done(V.tensor_reduce(row_min[:, :], row_b[:, :], op=ALU.min, axis=AX.X))
                dve.sem_inc(p.rows_ready, 1)
                dve.wait_ge(p.turned, k + 1)
                if windows == 0:
                    step(V.tensor_copy(src_next[:, :], ps_rows[:, 0:P]))
                    step(V.tensor_copy(cut_next[:, :], ps_rows[:, 2 * P:3 * P]))
                    done(V.tensor_copy(dst_next[:, :], ps_rows[:, P:2 * P]))
                    dve.sem_inc(p.tables_ready, 1)
                    return
                if windows == P:
                    done(V.tensor_copy(base_f[0:1, :], ps_rows[0:1, 3 * P:4 * P]))
                else:
                    done(V.tensor_reduce(base_f[0:1, 0:windows],
                                         ps_rows[0:1, 3 * P:4 * P].rearrange("p (w t) -> p w t", w=windows),
                                         op=ALU.min, axis=AX.X))
                done(V.tensor_scalar(base_f[0:1, 0:windows], base_f[0:1, 0:windows], float(AGG_COLS - window),
                                     None, ALU.min))
                dve.sem_inc(p.base_ready, 1)
                step(V.tensor_copy(base_next[0:1, 0:windows], base_f[0:1, 0:windows]))
                step(V.tensor_copy(src_next[:, :], ps_rows[:, 0:P]))
                step(V.tensor_copy(cut_next[:, :], ps_rows[:, 2 * P:3 * P]))
                done(V.tensor_copy(dst_next[:, :], ps_rows[:, P:2 * P]))
                dve.wait_ge(p.base_spread, k + 1)
                spread = ps_misc[:, 0:windows].rearrange("p (w t) -> p w t", t=1).to_broadcast([P, windows, P // windows])
                done(V.tensor_tensor(dst_next[:, :].rearrange("p (w t) -> p w t", w=windows),
                                     dst_next[:, :].rearrange("p (w t) -> p w t", w=windows), spread, ALU.subtract))
                done(V.scalar_tensor_tensor(out=row_b[:, :], in0=cut_next[:, :], scalar=0.0, in1=dst_next[:, :],
                                            op0=ALU.not_equal, op1=ALU.mult))
                done(V.tensor_reduce(reach[:, :], row_b[:, :], op=ALU.max, axis=AX.X))
                done(V.tensor_tensor(farthest[:, which:which + 1], farthest[:, which:which + 1], reach[:, :], ALU.max))
                dve.sem_inc(p.tables_ready, 1)

            def give_index(p, table, q, parity):
                step(V.tensor_copy(index[:, parity, :], table[:, UNIT * q:UNIT * (q + 1)]))
                settle()
                dve.sem_inc(p.index_ready, 1)

            def take_tables(windows):
                step(V.tensor_copy(src_now[:, :], src_next[:, :]))
                step(V.tensor_copy(dst_now[:, :], dst_next[:, :]))
                step(V.tensor_copy(cut_now[:, :], cut_next[:, :]))
                if windows:
                    step(V.tensor_copy(base_now[0:1, 0:windows], base_next[0:1, 0:windows]))
                settle()

            def activate(p, macro, n):
                dve.wait_ge(p.tanh_ready, macro + 1)
                V.scalar_tensor_tensor(out=act_t[:, n % 2, :], in0=half_tanh[:, n % 2, :], scalar=1.0,
                                       in1=ps_h[n % 2][:, :], op0=ALU.add, op1=ALU.mult).then_inc(p.act_ready, 1)

            def members(n, window):
                for t in range(MACRO):
                    c = MACRO * n + ORDER[t]
                    V.tensor_scalar(member[:, n % 2, t, 0:window], iota_f[:, 0:window], dst_now[:, c:c + 1],
                                    cut_now[:, c:c + 1], ALU.is_equal, ALU.mult)

            def messages(p, macro, n, gathers):
                dve.wait_ge(p.w_ready, macro + 1)
                dve.wait_ge(p.gathered[n % 8], gathers)
                g0 = MACRO * (n % 8)
                V.tensor_tensor(message[:, n % 2, :], ps_w[n % 2][:, :],
                                gathered[:, g0:g0 + MACRO, :].rearrange("p t f -> p (t f)"), ALU.mult)\
                 .then_inc(p.msg_ready, 1)

            def add_shared(p, macro, n):
                start = dve.value_load(base_now[0:1, n:n + 1], min_val=0, max_val=AGG_COLS - WINDOW)
                dve.wait_ge(p.summed, macro + 1)
                dve.wait_ge(p.added, macro + 1)
                V.tensor_tensor(agg[:, bass.ds(start, WINDOW)], agg[:, bass.ds(start, WINDOW)],
                                ps_sum[n % 2][:, 0:WINDOW], ALU.add).then_inc(p.added, 1)

            def group(g, last):
                first = g * MACROS
                take_tables(MACROS)
                activate(main, first, 0)
                for n in range(MACROS):
                    if n + 1 < MACROS:
                        activate(main, first + (n + 1), n + 1)
                    members(n, WINDOW)
                    messages(main, first + n, n, g * (64 * MACROS // 8) + 64 * (n // 8 + 1))
                    if n >= 1:
                        add_shared(main, first + (n - 1), n - 1)
                    if n % MACRO == MACRO - 1:
                        q = n // MACRO
                        if q + 2 < UNITS:
                            give_index(main, src_now, q + 2, q % 2)
                        if not last:
                            if q == 0:
                                drop_far(g + 1)
                            if q < 5:
                                shift_by(2 * q)
                                shift_by(2 * q + 1)
                            if q == 5:
                                clear_empty(g + 1)
                                tables(main, g + 1, dist[:, 0:P], ids[:, 0:P], MACROS, WINDOW, 0)
                            if q + 2 >= UNITS:
                                give_index(main, src_next, q + 2 - UNITS, q % 2)
                add_shared(main, first + (MACROS - 1), MACROS - 1)

            drop_far(0)
            for k in range(STEPS):
                shift_by(k)
            clear_empty(0)
            tables(main, 0, dist[:, 0:P], ids[:, 0:P], MACROS, WINDOW, 0)
            give_index(main, src_next, 0, 0)
            give_index(main, src_next, 1, 1)
            dve.wait_ge(const_built, 2)

            before_groups, per_group = at["n"], DVE_GROUP_STEPS
            with dve.Fori(0, GROUPS - 1) as g:
                at["n"], at["base"] = 0, g * per_group + before_groups
                group(g, False)
                assert at["n"] == per_group, at["n"]
            at["n"], at["base"] = before_groups + (GROUPS - 1) * per_group, 0
            group(GROUPS - 1, True)

            def number_extra():
                for b in range(BLOCKS - 1):
                    step(V.tensor_scalar(more[:, :, b], counts[:, :], float(P * (b + 1)), None, ALU.is_gt))
                done(V.tensor_copy(tile_id[:, :, :], tile_id_i[:, :, :]))
                choices = GROUPS * (BLOCKS - 1)
                flat = more[:, :, :].rearrange("p g b -> p (g b)")
                step(V.tensor_scalar(tile_id[:, :, :], tile_id[:, :, :], -float(ALL_TILES), None, ALU.add))
                done(V.tensor_tensor_scan(rank[:, :], ones_cols[:, 0:choices], flat, 0.0, ALU.mult, ALU.add))
                done(V.tensor_copy(total[:, :], rank[:, choices - 1:choices]))
                dve.sem_inc(extra_flagged, 1)
                done(V.tensor_tensor(rank[:, :], rank[:, :], flat, ALU.subtract))
                dve.wait_ge(extra_counted, 1)
                step(V.tensor_copy(n_extra_i[:, :], ps_misc[:, 1:2]))
                done(V.tensor_copy(offset[:, :], ps_misc[:, 0:1]))
                done(V.tensor_scalar(rank[:, :], rank[:, :], offset[:, 0:1], None, ALU.add))
                dve.sem_inc(n_extra_ready, 1)

            def list_extra(k):
                choices = GROUPS * (BLOCKS - 1)
                flat = more[:, :, :].rearrange("p g b -> p (g b)")
                for c in range(choices):
                    if c >= 2:
                        dve.wait_ge(chosen_used, k * choices + (c - 1))
                    V.tensor_scalar(chosen[:, c % 2, :], iota_f[:, 0:P], rank[:, c:c + 1], flat[:, c:c + 1],
                                    ALU.is_equal, ALU.mult).then_inc(chosen_ready, 1)
                dve.wait_ge(chosen_used, k * choices + choices)
                step(V.tensor_scalar(extra_list[:, :], ps_misc[:, 0:1], float(ALL_TILES), None, ALU.add))
                done(V.tensor_scalar(rank[:, :], rank[:, :], -float(P), None, ALU.add))
                dve.sem_inc(list_ready, 1)

            def add_single(p, macro, n):
                for t in range(MACRO):
                    c = MACRO * n + ORDER[t]
                    start = dve.value_load(base_now[0:1, c:c + 1], min_val=0, max_val=AGG_COLS - WINDOW1)
                    if t == 0:
                        dve.wait_ge(p.summed, macro + 1)
                    dve.wait_ge(p.added, macro * MACRO + (t + 1))
                    V.tensor_tensor(agg[:, bass.ds(start, WINDOW1)], agg[:, bass.ds(start, WINDOW1)],
                                    ps_sum[n % 2][:, WINDOW1 * t:WINDOW1 * (t + 1)], ALU.add).then_inc(p.added, 1)

            number_extra()
            dve.wait_ge(main.added, GROUPS * MACROS + 1)
            n_extra = dve.value_load(n_extra_i[0:1, 0:1], min_val=0, max_val=EXTRA_TILES)
            with dve.Fori(0, EXTRA_GROUPS) as k:
                with dve.If(n_extra > k * P):
                    at["sem"], at["n"], at["base"] = extra_step, 0, k * DVE_EXTRA_STEPS
                    list_extra(k)
                    dve.wait_ge(extra_rows_loaded, 32 * (k + 1))
                    tables(extra, k, row_dist[:, :], row_ids[:, :], P, WINDOW1, 1)
                    take_tables(P)
                    assert at["n"] == DVE_EXTRA_STEPS, at["n"]
                    dve.sem_inc(extra.index_ready, 1)
                    for q in range(UNITS):
                        with dve.If(n_extra > k * P + q * UNIT):
                            m, first = MACRO * q, k * MACROS
                            activate(extra, first + m, m)
                            for n in range(m, m + MACRO):
                                if n + 1 < m + MACRO:
                                    activate(extra, first + (n + 1), n + 1)
                                members(n, WINDOW1)
                                messages(extra, first + n, n, k * (64 * MACROS // 8) + 64 * (n // 8 + 1))
                                if n > m:
                                    add_single(extra, first + (n - 1), n - 1)
                            add_single(extra, first + (m + MACRO - 1), m + MACRO - 1)

            at["sem"], at["n"], at["base"] = general_step, 0, 0
            step(V.tensor_scalar(beyond[:, 0:1], farthest[:, 0:1], float(WINDOW), None, ALU.is_ge))
            done(V.tensor_scalar(beyond[:, 1:2], farthest[:, 1:2], float(WINDOW1), None, ALU.is_ge))
            done(V.tensor_tensor(beyond[:, 0:1], beyond[:, 0:1], beyond[:, 1:2], ALU.add))
            dve.sem_inc(beyond_flagged, 1)
            dve.wait_ge(beyond_counted, 1)
            done(V.tensor_copy(outside_i[:, :], ps_misc[:, 0:1]))
            dve.sem_inc(outside_ready, 1)
            outside = dve.value_load(outside_i[0:1, 0:1], min_val=0, max_val=2 * P)
            settled = at["n"]
            with dve.If(outside > 0):
                done(V.memset(agg[:, :], 0.0))
                with dve.Fori(0, ALL_GROUPS) as k:
                    at["n"], at["base"] = 0, k * DVE_GENERAL_STEPS + (settled + 1)
                    dve.wait_ge(general_rows_loaded, 32 * (k + 1))
                    tables(general, k, row_dist[:, :], row_ids[:, :], 0, 0, 0)
                    take_tables(0)
                    dve.sem_inc(general.index_ready, 1)
                    for q in range(UNITS):
                        for j in range(MACRO):
                            macro = k * MACROS + (MACRO * q + j)
                            activate(general, macro, j)
                            messages(general, macro, j, 64 * (k * UNITS + (q + 1)))
                            c = UNIT * q + MACRO * j
                            done(V.tensor_copy(dst_left[:, :], dst_now[:, c:c + MACRO]))
                            dve.sem_inc(paused, 1)
                            with dve.Fori(0, ALL_WINDOWS) as w:
                                now = macro * ALL_WINDOWS + w
                                for t in range(MACRO):
                                    last = V.tensor_scalar(
                                        gathered[:, UNIT + MACRO * t:UNIT + MACRO * (t + 1), :]
                                        .rearrange("p a b -> p (a b)"), iota_f[:, 0:WIDE],
                                        dst_left[:, ORDER[t]:ORDER[t] + 1], cut_now[:, c + ORDER[t]:c + ORDER[t] + 1],
                                        ALU.is_equal, ALU.mult)
                                last.then_inc(wide_members, 1)
                                dve.wait_ge(general.summed, now + 1)
                                dve.wait_ge(general.added, now + 1)
                                V.tensor_tensor(agg[:, bass.ds(w * WIDE, WIDE)], agg[:, bass.ds(w * WIDE, WIDE)],
                                                ps_sum[0][:, 0:WIDE], ALU.add).then_inc(general.added, 1)
                                V.tensor_scalar(dst_left[:, :], dst_left[:, :], -float(WIDE), None, ALU.add)\
                                 .then_inc(wide_moved, 1)
                                dve.wait_ge(wide_moved, now + 1)
                                dve.wait_ge(general.added, now + 2)
                        dve.sem_inc(general_slots_free, 1)
                    assert at["n"] == DVE_GENERAL_STEPS, at["n"]
            dve.sem_inc(agg_done, 1)
            at["sem"], at["n"], at["base"] = node_step, 0, 0

            def node_activate(i):
                dve.wait_ge(node_tanh, i + 1)
                V.scalar_tensor_tensor(out=act_t[:, i % 2, 0:CHUNK_NODES], in0=half_tanh[:, i % 2, 0:CHUNK_NODES],
                                       scalar=1.0, in1=ps_h[i % 2][:, 0:CHUNK_NODES],
                                       op0=ALU.add, op1=ALU.mult).then_inc(node_act, 1)

            def node_statistics(i):
                dve.wait_ge(node_out, i + 1)
                dve.wait_ge(x_again[i % RING], 16 * (i // RING + 1))
                if i >= 2:
                    dve.wait_ge(node_normed, i - 1)
                done(V.scalar_tensor_tensor(out=pre_norm[:, i % 2, :], in0=x_ring[:, i % RING, :], scalar=2.0,
                                            in1=ps_w[i % 2][0:NODE_TILE, :], op0=ALU.mult, op1=ALU.add))
                for t in range(CHUNK):
                    step(V.bn_stats(stats[:, i % 2, t, :], pre_norm[:, i % 2, t * P:(t + 1) * P]))
                settle()
                for t in range(CHUNK):
                    step(V.bn_aggr(mean_var[:, i % 2, t, :], stats[:, i % 2, t, :]))
                settle()
                dve.sem_inc(node_stats, 1)

            node_activate(0)
            for i in range(CHUNKS):
                if i + 1 < CHUNKS:
                    node_activate(i + 1)
                node_statistics(i)


DVE_GROUP_STEPS = 104
DVE_EXTRA_STEPS = 40
DVE_GENERAL_STEPS = 62

_INS = ["x", "src", "dst", "edge_weight", "L0_gnn_fw1", "L0_gnn_fb1", "L0_gnn_fw2", "L0_gnn_fb2", "L0_gnn_pw",
        "L0_gnn_pb", "L0_gnn_mw1", "L0_gnn_mb1", "L0_gnn_mw2", "L0_gnn_mb2"]


def kernel(**inputs):
    import numpy as _np
    import concourse.bacc as _bacc
    from concourse import mybir as _mybir
    from concourse.bass_utils import run_bass_kernel_spmd as _run

    nc = _bacc.Bacc("TRN2", target_bir_lowering=False, num_devices=1)
    arrays, args = {}, []
    for name in _INS:
        a = _np.ascontiguousarray(inputs[name])
        arrays[f"in_{name}"] = a
        args.append(nc.dram_tensor(f"in_{name}", a.shape, _mybir.dt.from_np(a.dtype), kind="ExternalInput").ap())
    args.append(nc.dram_tensor("out_nodes", (NODES, HIDDEN), F32, kind="ExternalOutput").ap())
    build(nc, *args)
    r = _run(nc, [arrays], core_ids=[0])
    return _np.asarray(r.results[0]["out_nodes"])
```

```python
import math
from contextlib import ExitStack

import concourse.bass as bass
from concourse import mybir

F32, I32, BF16 = mybir.dt.float32, mybir.dt.int32, mybir.dt.bfloat16
ALU, ACT, AX = mybir.AluOpType, mybir.ActivationFunctionType, mybir.AxisListType

NODES, HIDDEN, EDGES = 12500, 128, 400000
RBF, CUTOFF, EPS = 50, 10.0, 1e-5
WIDTH = CUTOFF / RBF * 0.5
P = 128

EDGE_COLS = 625
ROWS = EDGES // EDGE_COLS
GROUPS = ROWS // P
BLOCKS = -(-EDGE_COLS // P)
ROW_SLOTS = BLOCKS * P
STEPS = EDGE_COLS.bit_length()
ID_BITS = NODES.bit_length()
ID_MASK = (1 << ID_BITS) - 1
FAR = 2 * CUTOFF
NO_NODE = 65536.0

MACRO = 4
WINDOW = 192
WINDOW1 = 64
ORDER = (0, 2, 1, 3)
UNIT = 4 * MACRO
MACROS = P // MACRO
UNITS = P // UNIT
AGG_COLS = 12800
WIDE = 512
ALL_WINDOWS = AGG_COLS // WIDE

EXTRA_TILES = ROWS * (BLOCKS - 1)
EXTRA_GROUPS = EXTRA_TILES // P
ALL_TILES = ROWS * BLOCKS
ALL_GROUPS = ALL_TILES // P

NODE_TILE = 125
CHUNK = 4
CHUNK_NODES = NODE_TILE * CHUNK
CHUNKS = NODES // CHUNK_NODES
RING = 4

COS = [(-1) ** k / math.factorial(2 * k) for k in range(9)]


def build(nc, x, src, dst, edge_weight, fw1, fb1, fw2, fb2, pw, pb, mw1, mb1, mw2, mb2, out):
    ctx = ExitStack()
    with ctx:
        def sb(name, shape, dtype=F32):
            return ctx.enter_context(nc.sbuf_tensor(name, shape, dtype))

        def sem(name):
            return ctx.enter_context(nc.semaphore(name))

        proj = nc.dram_tensor("proj_rows", (NODES, HIDDEN), F32).ap()
        dist_tiles = nc.dram_tensor("dist_tiles", (ALL_TILES + 1, P), F32).ap()
        ids_tiles = nc.dram_tensor("ids_tiles", (ALL_TILES + 1, P), I32).ap()
        extra_dist = nc.dram_tensor("extra_dist", (EXTRA_TILES, P), F32).ap()

        dist_rows = dist_tiles[0:ALL_TILES, :].rearrange("(r b) s -> r (b s)", b=BLOCKS)
        ids_rows = ids_tiles[0:ALL_TILES, :].rearrange("(r b) s -> r (b s)", b=BLOCKS)
        edge_rows = [a.rearrange("(r c) -> r c", c=EDGE_COLS) for a in (edge_weight, src, dst)]
        x_nodes = x.rearrange("(j p) f -> p j f", p=NODE_TILE)
        proj_nodes = proj.rearrange("(j p) f -> p j f", p=NODE_TILE)
        out_nodes = out.rearrange("(j p) f -> p j f", p=NODE_TILE)

        ident = sb("ident", [P, P])
        ones_row = sb("ones_row", [1, P])
        before = sb("before", [P, P])
        all_ones = sb("all_ones", [P, P])
        iota_i = sb("iota_i", [P, ROW_SLOTS], I32)
        iota_f = sb("iota_f", [P, ROW_SLOTS])
        lane_i = sb("lane_i", [P, 1], I32)
        lane_f = sb("lane_f", [P, 1])
        rbf_scale = sb("rbf_scale", [P, 1])
        rbf_shift = sb("rbf_shift", [P, 1])
        fw1_halves = sb("fw1_halves", [P, 2, P])
        fw2_sb = sb("fw2_sb", [P, P])
        pw_sb = sb("pw_sb", [P, P])
        mw1_sb = sb("mw1_sb", [P, P])
        mw2_sb = sb("mw2_sb", [P, P])
        bias_in = sb("bias_in", [1, 4, P])
        bias_rest = sb("bias_rest", [1, 4, P])
        bias_parts = sb("bias_parts", [1, 3, 4, P], BF16)
        bias_lanes = sb("bias_lanes", [P, 4, P], BF16)
        bias_rhs = sb("bias_rhs", [P, 3, CHUNK, P], BF16)
        one_lanes = sb("one_lanes", [P, 512], BF16)

        dist = sb("dist", [P, ROW_SLOTS])
        ids = sb("ids", [P, ROW_SLOTS], I32)
        src_in = sb("src_in", [P, EDGE_COLS], I32)
        dst_in = sb("dst_in", [P, EDGE_COLS], I32)
        drop = sb("drop", [P, ROW_SLOTS])
        dropped = sb("dropped", [P, EDGE_COLS])
        move = [sb(f"move{i}", [P, EDGE_COLS], I32) for i in range(2)]
        moves_now = sb("moves_now", [P, EDGE_COLS], I32)
        ones_cols = sb("ones_cols", [P, EDGE_COLS])
        counts = sb("counts", [P, GROUPS])

        row_dist = sb("row_dist", [P, P])
        row_ids = sb("row_ids", [P, P], I32)
        row_cut = sb("row_cut", [P, P])
        row_src = sb("row_src", [P, P])
        row_dst = sb("row_dst", [P, P])
        row_int = sb("row_int", [P, 2, P], I32)
        row_a = sb("row_a", [P, P])
        row_b = sb("row_b", [P, P])
        row_min = sb("row_min", [P, 1])
        base_f = sb("base_f", [1, P])
        base_next = sb("base_next", [1, P], I32)
        base_now = sb("base_now", [1, P], I32)
        src_next = sb("src_next", [P, P], I32)
        dst_next = sb("dst_next", [P, P])
        cut_next = sb("cut_next", [P, P])
        src_now = sb("src_now", [P, P], I32)
        dst_now = sb("dst_now", [P, P])
        cut_now = sb("cut_now", [P, P])
        farthest = sb("farthest", [P, 2])
        reach = sb("reach", [P, 1])

        dist_bc = sb("dist_bc", [P, 2, MACRO, 2 * P])
        square = sb("square", [P, MACRO * 2 * P])
        rbf = sb("rbf", [P, 2, MACRO, 2 * P])
        act_t = sb("act_t", [P, 2, 512])
        gathered = sb("gathered", [P, 2 * UNIT, P])
        message = sb("message", [P, 2, 512])
        member = sb("member", [P, 2, MACRO, WINDOW])
        index = sb("index", [P, 2, UNIT], I32)
        agg = sb("agg", [P, AGG_COLS])

        more = sb("more", [P, GROUPS, BLOCKS - 1])
        rank = sb("rank", [P, GROUPS * (BLOCKS - 1)])
        tile_id = sb("tile_id", [P, GROUPS, BLOCKS - 1])
        tile_id_i = sb("tile_id_i", [P, GROUPS, BLOCKS - 1], I32)
        total = sb("total", [P, 1])
        offset = sb("offset", [P, 1])
        n_extra_i = sb("n_extra_i", [P, 1], I32)
        outside_i = sb("outside_i", [P, 1], I32)
        chosen = sb("chosen", [P, 2, P])
        extra_list = sb("extra_list", [P, 1], I32)
        empty_dist = sb("empty_dist", [1, P])
        empty_ids = sb("empty_ids", [1, P], I32)
        beyond = sb("beyond", [P, 2])
        dst_left = sb("dst_left", [P, MACRO])

        x_ring = sb("x_ring", [NODE_TILE, RING, 512])
        y_ring = sb("y_ring", [NODE_TILE, RING, 512])
        x_t = sb("x_t", [P, 2, 512])
        stats = sb("stats", [NODE_TILE, 2, CHUNK, 6])
        mean_var = sb("mean_var", [NODE_TILE, RING, CHUNK, 2])
        rstd = sb("rstd", [NODE_TILE, RING, CHUNK])
        shift = sb("shift", [NODE_TILE, RING, CHUNK])
        minus_half = sb("minus_half", [NODE_TILE, CHUNK])

        def bank(name):
            return ctx.enter_context(nc.psum_tensor(name, [P, 512], F32))

        ps_h = [bank("ps_h0"), bank("ps_h1")]
        ps_w = [bank("ps_w0"), bank("ps_w1")]
        ps_sum = [bank("ps_sum0"), bank("ps_sum1")]
        ps_rows = bank("ps_rows")
        ps_misc = bank("ps_misc")

        weights_loaded = sem("weights_loaded")
        fw1_loaded = sem("fw1_loaded")
        fw1_cleared = sem("fw1_cleared")
        const_built = sem("const_built")
        pool_step = sem("pool_step")
        dve_step = sem("dve_step")
        biases_split = sem("biases_split")
        bias_placed = sem("bias_placed")
        weights_ready = sem("weights_ready")

        x_loaded = [sem(f"x_loaded{i}") for i in range(RING)]
        x_turned = sem("x_turned")
        x_t_ready = sem("x_t_ready")
        projected = sem("projected")
        proj_copied = sem("proj_copied")
        proj_stored = [sem(f"proj_stored{i}") for i in range(RING)]
        proj_table = sem("proj_table")

        edges_loaded = sem("edges_loaded")
        compacted = sem("compacted")
        rows_stored = sem("rows_stored")
        empty_stored = sem("empty_stored")

        class Pass:

            def __init__(self, name):
                self.rows_ready = sem(name + "_rows_ready")
                self.turned = sem(name + "_turned")
                self.base_ready = sem(name + "_base_ready")
                self.base_spread = sem(name + "_base_spread")
                self.tables_ready = sem(name + "_tables_ready")
                self.dist_loaded = [sem(f"{name}_dist_loaded{i}") for i in range(2)]
                self.squared = sem(name + "_squared")
                self.rbf_ready = sem(name + "_rbf_ready")
                self.h_ready = sem(name + "_h_ready")
                self.act_ready = sem(name + "_act_ready")
                self.w_ready = sem(name + "_w_ready")
                self.gathered = [sem(f"{name}_gathered{i}") for i in range(8)]
                self.index_ready = sem(name + "_index_ready")
                self.msg_ready = sem(name + "_msg_ready")
                self.summed = sem(name + "_summed")
                self.added = sem(name + "_added")

        main = Pass("main")
        extra = Pass("extra")
        general = Pass("general")
        extra_flagged = sem("extra_flagged")
        extra_counted = sem("extra_counted")
        n_extra_ready = sem("n_extra_ready")
        chosen_ready = sem("chosen_ready")
        chosen_used = sem("chosen_used")
        list_ready = sem("list_ready")
        extra_step = sem("extra_step")
        extra_rows_loaded = sem("extra_rows_loaded")
        extra_dist_stored = sem("extra_dist_stored")
        beyond_flagged = sem("beyond_flagged")
        beyond_counted = sem("beyond_counted")
        outside_ready = sem("outside_ready")
        extra_rows_free = sem("extra_rows_free")
        general_slots_free = sem("general_slots_free")
        general_step = sem("general_step")
        general_rows_loaded = sem("general_rows_loaded")
        wide_members = sem("wide_members")
        wide_moved = sem("wide_moved")

        agg_done = sem("agg_done")
        node_step = sem("node_step")
        node_h = sem("node_h")
        node_summed = sem("node_summed")
        node_act = sem("node_act")
        node_out = sem("node_out")
        node_stats = sem("node_stats")
        node_scaled = sem("node_scaled")
        node_normed = sem("node_normed")
        x_again = [sem(f"x_again{i}") for i in range(RING)]
        out_stored = [sem(f"out_stored{i}") for i in range(RING)]

        paused = sem("paused")

        def wait_apart(engine, semaphore, value):
            engine.wait_ge(semaphore, value)
            engine.sem_inc(paused, 1)

        block = ctx.enter_context(nc.Block())

        @block.sync
        def _(sp):
            def load_edges(g):
                if not isinstance(g, int) or g > 0:
                    sp.wait_ge(main.rows_ready, g)
                sp.dma_start(dist[:, 0:EDGE_COLS], edge_rows[0][bass.ds(g * P, P), :]).then_inc(edges_loaded, 16)
                sp.dma_start(src_in[:, :], edge_rows[1][bass.ds(g * P, P), :]).then_inc(edges_loaded, 16)
                sp.dma_start(dst_in[:, :], edge_rows[2][bass.ds(g * P, P), :]).then_inc(edges_loaded, 16)

            def store_rows(g):
                sp.wait_ge(compacted, g + 1)
                sp.dma_start(dist_rows[bass.ds(g * P, P), :], dist[:, :]).then_inc(rows_stored, 16)
                sp.dma_start(ids_rows[bass.ds(g * P, P), :], ids[:, :]).then_inc(rows_stored, 16)
                sp.wait_ge(rows_stored, 32 * (g + 1))

            sp.sem_inc(extra_rows_free, 1)
            load_edges(0)
            sp.dma_start(pw_sb[:, :], pw).then_inc(weights_loaded, 16)
            sp.dma_start(mw1_sb[:, :], mw1).then_inc(weights_loaded, 16)
            sp.dma_start(fw2_sb[:, :], fw2).then_inc(weights_loaded, 16)
            sp.dma_start(mw2_sb[:, :], mw2).then_inc(weights_loaded, 16)
            for i, b in enumerate((fb2, pb, mb2, mb1)):
                sp.dma_start(bias_in[0:1, i, :], b.rearrange("(a n) -> a n", a=1)).then_inc(weights_loaded, 16)
            sp.wait_ge(fw1_cleared, 1)
            for half in range(2):
                sp.dma_start(fw1_halves[64 * half:64 * half + RBF, half, :], fw1).then_inc(fw1_loaded, 16)
                sp.dma_start(fw1_halves[64 * half + RBF:64 * half + RBF + 1, half, :],
                             fb1.rearrange("(a n) -> a n", a=1)).then_inc(fw1_loaded, 16)
            sp.wait_ge(biases_split, 1)
            for part in range(3):
                sp.dma_start(bias_lanes[part:part + 1, :, :], bias_parts[0:1, part, :, :]).then_inc(bias_placed, 16)

            def load_x(i, sems, slot):
                sp.dma_start(x_ring[:, slot, :].rearrange("p (j f) -> p j f", f=P),
                             x_nodes[:, bass.ds(i * CHUNK, CHUNK), :]).then_inc(sems[slot], 16)

            def store_proj(i, slot):
                sp.wait_ge(proj_copied, i + 1)
                sp.dma_start(proj_nodes[:, bass.ds(i * CHUNK, CHUNK), :],
                             y_ring[:, slot, :].rearrange("p (j f) -> p j f", f=P)).then_inc(proj_stored[slot], 16)

            for i in range(RING):
                load_x(i, x_loaded, i)
            for i in range(CHUNKS):
                if i + RING < CHUNKS:
                    sp.wait_ge(x_turned, i + 1)
                    load_x(i + RING, x_loaded, i % RING)
                store_proj(i, i % RING)
            for slot in range(RING):
                sp.wait_ge(proj_stored[slot], 16 * len(range(slot, CHUNKS, RING)))
            sp.sem_inc(proj_table, 1)

            def load_unit(tiles, stride_rows, unit, parity, loaded):
                rows = tiles[bass.ds(unit * (UNIT * stride_rows), UNIT * stride_rows), :]
                for half in range(2):
                    v = rows.rearrange("(k h b) s -> h b k s", h=2, b=stride_rows)[half, 0]
                    sp.dma_start(dist_bc[64 * half:64 * half + 64, parity, :, :]
                                 .rearrange("p m (t s) -> p (m t) s", s=P),
                                 v.partition_broadcast(64)).then_inc(loaded[parity], 16)

            store_rows(0)
            load_edges(1)

            def group(g, last, next_edges):
                for q in range(UNITS):
                    unit = g * UNITS + q
                    if not (isinstance(unit, int) and unit < 2):
                        sp.wait_ge(main.squared, unit)
                    load_unit(dist_tiles, BLOCKS, unit, q % 2, main.dist_loaded)
                if not last:
                    store_rows(g + 1)
                if next_edges:
                    load_edges(g + 2)

            group(0, False, True)
            with sp.Fori(1, GROUPS - 2) as g:
                group(g, False, True)
            group(GROUPS - 2, False, False)
            group(GROUPS - 1, True, False)

            sp.wait_ge(const_built, 2)
            sp.dma_start(dist_tiles[ALL_TILES:ALL_TILES + 1, :], empty_dist[:, :]).then_inc(empty_stored, 16)
            sp.dma_start(ids_tiles[ALL_TILES:ALL_TILES + 1, :], empty_ids[:, :]).then_inc(empty_stored, 16)
            sp.wait_ge(empty_stored, 32)
            sp.wait_ge(main.squared, GROUPS * UNITS + 1)

            sp.wait_ge(n_extra_ready, 1)
            n_extra = sp.value_load(n_extra_i[0:1, 0:1], min_val=0, max_val=EXTRA_TILES)
            with sp.Fori(0, EXTRA_GROUPS) as k:
                with sp.If(n_extra > k * P):
                    sp.wait_ge(extra_rows_loaded, 32 * (k + 1))
                    sp.dma_start(extra_dist[bass.ds(k * P, P), :], row_dist[:, :]).then_inc(extra_dist_stored, 16)
                    sp.wait_ge(extra_dist_stored, 16 * (k + 1))
                    sp.sem_inc(extra_rows_free, 1)
                    wait_apart(sp, extra.squared, k * UNITS + 1)
                    for q in range(UNITS):
                        with sp.If(n_extra > k * P + q * UNIT):
                            if q >= 2:
                                sp.wait_ge(extra.squared, k * UNITS + q)
                            load_unit(extra_dist, 1, k * UNITS + q, q % 2, extra.dist_loaded)

            sp.wait_ge(outside_ready, 1)
            outside = sp.value_load(outside_i[0:1, 0:1], min_val=0, max_val=2 * P)
            with sp.If(outside > 0):
                with sp.Fori(0, ALL_GROUPS) as k:
                    sp.wait_ge(general.tables_ready, k + 1)
                    sp.dma_start(row_dist[:, :], dist_tiles[bass.ds(k * P, P), :]).then_inc(general_rows_loaded, 16)
                    sp.dma_start(row_ids[:, :], ids_tiles[bass.ds(k * P, P), :]).then_inc(general_rows_loaded, 16)
                    for q in range(UNITS):
                        sp.wait_ge(general.squared, k * UNITS + (q + 1))
                        load_unit(dist_tiles, 1, k * UNITS + q, 0, general.dist_loaded)

            def load_x_again(i, slot):
                load_x(i, x_again, slot)

            for i in range(RING):
                load_x_again(i, i)
            for i in range(CHUNKS):
                if i >= 1 and i - 1 + RING < CHUNKS:
                    sp.wait_ge(node_summed, i)
                    load_x_again(i - 1 + RING, (i - 1) % RING)
                sp.wait_ge(node_normed, i + 1)
                sp.dma_start(out_nodes[:, i * CHUNK:(i + 1) * CHUNK, :],
                             y_ring[:, i % RING, :].rearrange("p (j f) -> p j f", f=P))\
                  .then_inc(out_stored[i % RING], 16)
            for slot in range(RING):
                sp.wait_ge(out_stored[slot], 16 * len(range(slot, CHUNKS, RING)))

        @block.gpsimd
        def _(pool):
            n = [0]

            def step(ins):
                n[0] += 1
                ins.then_inc(pool_step, 1)
                pool.wait_ge(pool_step, n[0])

            step(nc.gpsimd.memset(fw1_halves[:, :, :], 0.0))
            pool.sem_inc(fw1_cleared, 1)
            step(nc.gpsimd.iota(iota_i[:, :], pattern=[[1, ROW_SLOTS]], base=0, channel_multiplier=0))
            step(nc.gpsimd.iota(lane_i[:, :], pattern=[[1, 1]], base=0, channel_multiplier=1))
            step(nc.gpsimd.memset(ident[:, :], 0.0))
            step(nc.gpsimd.affine_select(out=ident[:, :], in_=ident[:, :], compare_op=ALU.not_equal, fill=1.0,
                                         base=0, pattern=[[-1, P]], channel_multiplier=1))
            step(nc.gpsimd.memset(ids[:, EDGE_COLS:ROW_SLOTS], 0))
            step(nc.gpsimd.memset(dist[:, EDGE_COLS:ROW_SLOTS], FAR))
            step(nc.gpsimd.memset(ones_cols[:, :], 1.0))
            step(nc.gpsimd.memset(bias_lanes[:, :, :], 0.0))
            step(nc.gpsimd.memset(one_lanes[:, :], 0.0))
            step(nc.gpsimd.memset(one_lanes[0:3, :], 1.0))
            pool.sem_inc(const_built, 1)
            step(nc.gpsimd.memset(all_ones[:, :], 1.0))
            step(nc.gpsimd.memset(ones_row[:, :], 1.0))
            step(nc.gpsimd.affine_select(out=before[:, :], in_=all_ones[:, :], compare_op=ALU.is_gt, fill=0.0,
                                         base=0, pattern=[[1, P]], channel_multiplier=-1))
            step(nc.gpsimd.iota(tile_id_i[:, :, :], pattern=[[P * BLOCKS, GROUPS], [1, BLOCKS - 1]],
                                base=1, channel_multiplier=BLOCKS))
            step(nc.gpsimd.memset(agg[:, :], 0.0))
            step(nc.gpsimd.memset(minus_half[:, :], -0.5))
            step(nc.gpsimd.memset(empty_dist[:, :], FAR))
            step(nc.gpsimd.memset(empty_ids[:, :], 0))
            pool.sem_inc(const_built, 1)
            pool.wait_ge(proj_table, 1)

            def gather_tile(table, c, slot, done):
                nc.gpsimd.indirect_dma_start(
                    out=gathered[:, slot, :], out_offset=None, in_=proj,
                    in_offset=bass.IndirectOffsetOnAxis(ap=table[:, c:c + 1], axis=0)).then_inc(done, 16)

            def gather_unit(p, unit, parity, first):
                pool.wait_ge(p.index_ready, unit + 1)
                for j in range(MACRO):
                    if not first:
                        wait_apart(pool, p.msg_ready, unit * MACRO + (j - 7))
                    for t in range(MACRO):
                        c = MACRO * j + ORDER[t]
                        gather_tile(index[:, parity, :], c, UNIT * parity + MACRO * j + t,
                                    p.gathered[MACRO * parity + j])

            for parity in range(2):
                gather_unit(main, parity, parity, True)
            with pool.Fori(2, GROUPS * UNITS, 2) as u:
                for parity in range(2):
                    gather_unit(main, u + parity, parity, False)

            pool.wait_ge(empty_stored, 32)
            pool.wait_ge(rows_stored, 32 * GROUPS)
            pool.wait_ge(n_extra_ready, 1)
            n_extra = pool.value_load(n_extra_i[0:1, 0:1], min_val=0, max_val=EXTRA_TILES)
            with pool.Fori(0, EXTRA_GROUPS) as k:
                with pool.If(n_extra > k * P):
                    pool.wait_ge(list_ready, k + 1)
                    wait_apart(pool, extra_rows_free, k + 1)
                    for rows, tiles in ((row_dist, dist_tiles), (row_ids, ids_tiles)):
                        nc.gpsimd.indirect_dma_start(
                            out=rows[:, :], out_offset=None, in_=tiles,
                            in_offset=bass.IndirectOffsetOnAxis(ap=extra_list[:, 0:1], axis=0),
                        ).then_inc(extra_rows_loaded, 16)
                    wait_apart(pool, extra.index_ready, k + 1)
                    for q in range(UNITS):
                        with pool.If(n_extra > k * P + q * UNIT):
                            for j in range(MACRO):
                                if q >= 2:
                                    wait_apart(pool, extra.msg_ready, k * MACROS + (MACRO * q + j - 7))
                                for t in range(MACRO):
                                    gather_tile(src_now, UNIT * q + MACRO * j + ORDER[t],
                                                UNIT * (q % 2) + MACRO * j + t, extra.gathered[MACRO * (q % 2) + j])

            pool.wait_ge(outside_ready, 1)
            outside = pool.value_load(outside_i[0:1, 0:1], min_val=0, max_val=2 * P)
            with pool.If(outside > 0):
                with pool.Fori(0, ALL_GROUPS) as k:
                    pool.wait_ge(general.index_ready, k + 1)
                    for q in range(UNITS):
                        wait_apart(pool, general_slots_free, k * UNITS + (q + 1))
                        for j in range(MACRO):
                            for t in range(MACRO):
                                gather_tile(src_now, UNIT * q + MACRO * j + ORDER[t], MACRO * j + t,
                                            general.gathered[j])

            for i in range(CHUNKS):
                pool.wait_ge(node_stats, i + 1)
                if i >= RING:
                    pool.wait_ge(node_normed, i - RING + 1)
                step(nc.gpsimd.tensor_scalar(shift[:, i % RING, :], mean_var[:, i % RING, :, 1], EPS, None, ALU.add))
                step(nc.gpsimd.tensor_tensor(rstd[:, i % RING, :], shift[:, i % RING, :], minus_half[:, :], ALU.pow))
                step(nc.gpsimd.tensor_tensor(shift[:, i % RING, :], mean_var[:, i % RING, :, 0], rstd[:, i % RING, :], ALU.mult))
                step(nc.gpsimd.tensor_scalar(shift[:, i % RING, :], shift[:, i % RING, :], -1.0, None, ALU.mult))
                pool.sem_inc(node_scaled, 1)

        @block.scalar
        def _(act):
            for p in (main, extra, general):
                act.sem_inc(p.squared, 1)
            def take_turned(i):
                act.wait_ge(x_turned, i + 1)
                if i >= 2:
                    act.wait_ge(projected, i - 1)
                nc.scalar.activation(x_t[:, i % 2, 0:CHUNK_NODES], ps_h[i % 2][:, 0:CHUNK_NODES], ACT.Copy)\
                  .then_inc(x_t_ready, 1)

            take_turned(0)
            for i in range(CHUNKS):
                if i + 1 < CHUNKS:
                    take_turned(i + 1)
                act.wait_ge(projected, i + 1)
                if i >= RING:
                    act.wait_ge(proj_stored[i % RING], 16 * (i // RING))
                nc.scalar.activation(y_ring[:, i % RING, :], ps_w[i % 2][0:NODE_TILE, :], ACT.Copy)\
                  .then_inc(proj_copied, 1)

            act.wait_ge(weights_ready, 1)

            def radial(p, unit, parity, wait=True):
                if wait:
                    act.wait_ge(p.dist_loaded[parity], 16 * (unit + (2 - parity)))
                nc.scalar.activation(square[:, :], dist_bc[:, parity, :, :], ACT.Square,
                                     bias=rbf_shift[:, 0:1], scale=rbf_scale[:, 0:1]).then_inc(p.squared, 1)
                act.wait_ge(p.squared, unit + 2)
                nc.scalar.activation(rbf[:, parity, :, :], square[:, :], ACT.Exp,
                                     scale=-1.0 / (2.0 * WIDTH * WIDTH)).then_inc(p.rbf_ready, 1)

            def silu(p, macro, parity):
                act.wait_ge(p.h_ready, macro + 1)
                nc.scalar.activation(act_t[:, parity, :], ps_h[parity][:, :], ACT.Silu).then_inc(p.act_ready, 1)

            def pair(u, last):
                for parity in range(2):
                    for j in range(MACRO):
                        if j == 2 and not (last and parity):
                            radial(main, u + (parity + 1), 1 - parity)
                        silu(main, u * MACRO + (MACRO * parity + j), j % 2)

            radial(main, 0, 0)
            with act.Fori(0, GROUPS * UNITS - 2, 2) as u:
                pair(u, False)
            pair(GROUPS * UNITS - 2, True)

            act.wait_ge(n_extra_ready, 1)
            n_extra = act.value_load(n_extra_i[0:1, 0:1], min_val=0, max_val=EXTRA_TILES)
            with act.Fori(0, EXTRA_GROUPS) as k:
                with act.If(n_extra > k * P):
                    for q in range(UNITS):
                        with act.If(n_extra > k * P + q * UNIT):
                            radial(extra, k * UNITS + q, q % 2)
                            for j in range(MACRO):
                                silu(extra, k * MACROS + (MACRO * q + j), j % 2)

            act.wait_ge(outside_ready, 1)
            outside = act.value_load(outside_i[0:1, 0:1], min_val=0, max_val=2 * P)
            with act.If(outside > 0):
                with act.Fori(0, ALL_GROUPS * UNITS) as u:
                    act.wait_ge(general.dist_loaded[0], 32 * (u + 1))
                    radial(general, u, 0, wait=False)
                    for j in range(MACRO):
                        silu(general, u * MACRO + j, j % 2)

            for i in range(CHUNKS + 2):
                if i < CHUNKS:
                    act.wait_ge(node_h, i + 1)
                    nc.scalar.activation(act_t[:, i % 2, 0:CHUNK_NODES], ps_h[i % 2][:, 0:CHUNK_NODES],
                                         ACT.Silu).then_inc(node_act, 1)
                if i >= 2:
                    k = i - 2
                    act.wait_ge(node_scaled, k + 1)
                    for t in range(CHUNK):
                        row = y_ring[:, k % RING, t * P:(t + 1) * P]
                        last = nc.scalar.activation(row, row, ACT.Identity, scale=rstd[:, k % RING, t:t + 1],
                                                    bias=shift[:, k % RING, t:t + 1])
                    last.then_inc(node_normed, 1)

        @block.tensor
        def _(pe):
            pe.wait_ge(const_built, 1)

            def turn(i):
                pe.wait_ge(x_loaded[i % RING], 16 * (i // RING + 1))
                if i >= 2:
                    pe.wait_ge(x_t_ready, i - 1)
                for t in range(CHUNK):
                    last = nc.tensor.transpose(ps_h[i % 2][:, t * NODE_TILE:(t + 1) * NODE_TILE],
                                               x_ring[:, i % RING, t * P:(t + 1) * P],
                                               ident[0:NODE_TILE, 0:NODE_TILE])
                last.then_inc(x_turned, 1)

            def project(i):
                pe.wait_ge(x_t_ready, i + 1)
                if i >= 2:
                    pe.wait_ge(proj_copied, i - 1)
                nc.tensor.matmul(ps_w[i % 2][0:NODE_TILE, :], one_lanes[:, 0:NODE_TILE],
                                 bias_rhs[:, 1, :, :], start=True, stop=False, skip_group_check=True)
                for t in range(CHUNK):
                    last = nc.tensor.matmul(ps_w[i % 2][0:NODE_TILE, t * P:(t + 1) * P],
                                            x_t[:, i % 2, t * NODE_TILE:(t + 1) * NODE_TILE], pw_sb[:, :],
                                            start=False, stop=True, skip_group_check=True)
                last.then_inc(projected, 1)

            turn(0)
            turn(1)
            pe.wait_ge(weights_ready, 1)
            for i in range(CHUNKS):
                project(i)
                if i + 2 < CHUNKS:
                    turn(i + 2)

            def turn_rows(p, k):
                pe.wait_ge(p.rows_ready, k + 1)
                for c, t in enumerate((row_src, row_dst, row_cut)):
                    nc.tensor.transpose(ps_rows[:, c * P:(c + 1) * P], t[:, :], ident[:, :])
                nc.tensor.transpose(ps_rows[0:1, 3 * P:4 * P], row_min[:, :], ident[:, :]).then_inc(p.turned, 1)

            def spread_base(p, k, windows):
                pe.wait_ge(p.base_ready, k + 1)
                nc.tensor.matmul(ps_misc[:, 0:windows], ones_row[0:1, :], base_f[0:1, 0:windows],
                                 start=True, stop=True).then_inc(p.base_spread, 1)

            def first_layer(p, n, units):
                pe.wait_ge(p.rbf_ready, units)
                for half in range(2):
                    last = nc.tensor.matmul(ps_h[n % 2][:, 256 * half:256 * half + 256], fw1_halves[:, half, :],
                                            rbf[:, (n // MACRO) % 2, n % MACRO, :], start=True, stop=True)
                last.then_inc(p.h_ready, 1)

            def second_layer(p, macro, n):
                pe.wait_ge(p.act_ready, macro + 1)
                nc.tensor.matmul(ps_w[n % 2][:, :], one_lanes[:, 0:P], bias_rhs[:, 0, :, :],
                                 start=True, stop=False, skip_group_check=True)
                for t in range(MACRO):
                    last = nc.tensor.matmul(ps_w[n % 2][:, t * P:(t + 1) * P], act_t[:, n % 2, t * P:(t + 1) * P],
                                            fw2_sb[:, :], start=False, stop=True, skip_group_check=True)
                last.then_inc(p.w_ready, 1)

            def sum_shared(p, macro, n, bank_wait):
                pe.wait_ge(p.msg_ready, macro + 1)
                if bank_wait is not None:
                    pe.wait_ge(p.added, bank_wait + 1)
                for t in range(MACRO):
                    last = nc.tensor.matmul(ps_sum[n % 2][:, 0:WINDOW], message[:, n % 2, t * P:(t + 1) * P],
                                            member[:, n % 2, t, :], start=(t == 0), stop=(t == MACRO - 1))
                last.then_inc(p.summed, 1)

            def group(g, last):
                at = g * MACROS
                unit = g * UNITS
                for n in range(MACROS):
                    if n + 1 < MACROS or not last:
                        first_layer(main, n + 1, unit + ((n + 1) // MACRO + 1))
                    second_layer(main, at + n, n)
                    if n >= 1:
                        sum_shared(main, at + (n - 1), n - 1, at if n == 1 else at + (n - 2) if n >= 3 else None)
                    if n == 28 and not last:
                        turn_rows(main, g + 1)
                    if n == 30 and not last:
                        spread_base(main, g + 1, MACROS)
                sum_shared(main, at + (MACROS - 1), MACROS - 1, at + (MACROS - 2))

            pe.wait_ge(const_built, 2)
            turn_rows(main, 0)
            spread_base(main, 0, MACROS)
            first_layer(main, 0, 1)
            with pe.Fori(0, GROUPS - 1) as g:
                group(g, False)
            group(GROUPS - 1, True)

            def sum_single(p, macro, n, bank_wait):
                pe.wait_ge(p.msg_ready, macro + 1)
                pe.wait_ge(p.added, bank_wait + 1)
                for t in range(MACRO):
                    last = nc.tensor.matmul(ps_sum[n % 2][:, WINDOW1 * t:WINDOW1 * (t + 1)],
                                            message[:, n % 2, t * P:(t + 1) * P], member[:, n % 2, t, 0:WINDOW1],
                                            start=True, stop=True)
                last.then_inc(p.summed, 1)

            pe.wait_ge(extra_flagged, 1)
            nc.tensor.matmul(ps_misc[:, 0:1], before[:, :], total[:, :], start=True, stop=True)
            nc.tensor.matmul(ps_misc[:, 1:2], all_ones[:, :], total[:, :], start=True, stop=True)\
              .then_inc(extra_counted, 1)
            pe.wait_ge(n_extra_ready, 1)
            n_extra = pe.value_load(n_extra_i[0:1, 0:1], min_val=0, max_val=EXTRA_TILES)
            with pe.Fori(0, EXTRA_GROUPS) as k:
                with pe.If(n_extra > k * P):
                    choices = GROUPS * (BLOCKS - 1)
                    ids_flat = tile_id[:, :, :].rearrange("p g b -> p (g b)")
                    for c in range(choices):
                        pe.wait_ge(chosen_ready, k * choices + (c + 1))
                        nc.tensor.matmul(ps_misc[:, 0:1], chosen[:, c % 2, :], ids_flat[:, c:c + 1],
                                         start=(c == 0), stop=(c == choices - 1)).then_inc(chosen_used, 1)
                    turn_rows(extra, k)
                    spread_base(extra, k, P)
                    for q in range(UNITS):
                        with pe.If(n_extra > k * P + q * UNIT):
                            at, unit = k * MACROS, k * UNITS + q
                            m = MACRO * q
                            first_layer(extra, m, unit + 1)
                            for j in range(MACRO):
                                if j + 1 < MACRO:
                                    first_layer(extra, m + j + 1, unit + 1)
                                second_layer(extra, at + (m + j), m + j)
                                if j >= 1:
                                    sum_single(extra, at + (m + j - 1), m + j - 1,
                                               MACRO * (at + (m + max(j - 2, 0))))
                            sum_single(extra, at + (m + MACRO - 1), m + MACRO - 1, MACRO * (at + (m + MACRO - 2)))

            pe.wait_ge(beyond_flagged, 1)
            nc.tensor.matmul(ps_misc[:, 0:1], all_ones[:, :], beyond[:, 0:1], start=True, stop=True)\
              .then_inc(beyond_counted, 1)
            pe.wait_ge(outside_ready, 1)
            outside = pe.value_load(outside_i[0:1, 0:1], min_val=0, max_val=2 * P)
            with pe.If(outside > 0):
                with pe.Fori(0, ALL_GROUPS) as k:
                    turn_rows(general, k)
                    for q in range(UNITS):
                        for j in range(MACRO):
                            macro = k * MACROS + (MACRO * q + j)
                            first_layer(general, j, k * UNITS + (q + 1))
                            second_layer(general, macro, j)
                            wait_apart(pe, general.msg_ready, macro + 1)
                            with pe.Fori(0, ALL_WINDOWS) as w:
                                pe.wait_ge(wide_members, macro * ALL_WINDOWS + w + 1)
                                for t in range(MACRO):
                                    last = nc.tensor.matmul(
                                        ps_sum[0][:, 0:WIDE], message[:, j % 2, t * P:(t + 1) * P],
                                        gathered[:, UNIT + MACRO * t:UNIT + MACRO * (t + 1), :],
                                        start=(t == 0), stop=(t == MACRO - 1))
                                last.then_inc(general.summed, 1)

            def node_first(i):
                if i >= 2:
                    pe.wait_ge(node_act, i - 1)
                nc.tensor.matmul(ps_h[i % 2][:, 0:CHUNK_NODES], bias_lanes[:, 3, :], one_lanes[:, 0:CHUNK_NODES],
                                 start=True, stop=False, skip_group_check=True)
                nc.tensor.matmul(ps_h[i % 2][:, 0:CHUNK_NODES], mw1_sb[:, :],
                                 agg[:, i * CHUNK_NODES:(i + 1) * CHUNK_NODES],
                                 start=False, stop=True, skip_group_check=True).then_inc(node_h, 1)

            def node_second(i):
                pe.wait_ge(node_act, i + 1)
                if i >= 2:
                    pe.wait_ge(node_summed, i - 1)
                nc.tensor.matmul(ps_w[i % 2][0:NODE_TILE, :], one_lanes[:, 0:NODE_TILE], bias_rhs[:, 2, :, :],
                                 start=True, stop=False, skip_group_check=True)
                for t in range(CHUNK):
                    last = nc.tensor.matmul(ps_w[i % 2][0:NODE_TILE, t * P:(t + 1) * P],
                                            act_t[:, i % 2, t * NODE_TILE:(t + 1) * NODE_TILE], mw2_sb[:, :],
                                            start=False, stop=True, skip_group_check=True)
                last.then_inc(node_out, 1)

            pe.wait_ge(agg_done, 1)
            node_first(0)
            for i in range(CHUNKS):
                if i + 1 < CHUNKS:
                    node_first(i + 1)
                node_second(i)

        @block.vector
        def _(dve):
            at = {"n": 0, "base": 0, "sem": dve_step}

            def step(ins):
                at["n"] += 1
                ins.then_inc(at["sem"], 1)

            def settle():
                dve.wait_ge(at["sem"], at["base"] + at["n"])

            def done(ins):
                step(ins)
                settle()

            V = nc.vector
            for p in (main, extra, general):
                dve.sem_inc(p.added, 1)
            dve.sem_inc(general.tables_ready, 1)
            dve.sem_inc(general_slots_free, 1)
            dve.wait_ge(weights_loaded, 8 * 16)
            dve.wait_ge(const_built, 1)
            done(V.tensor_copy(bias_parts[0:1, 0, :, :], bias_in[0:1, :, :]))
            done(V.tensor_tensor(bias_rest[0:1, :, :], bias_in[0:1, :, :], bias_parts[0:1, 0, :, :], ALU.subtract))
            done(V.tensor_copy(bias_parts[0:1, 1, :, :], bias_rest[0:1, :, :]))
            done(V.tensor_tensor(bias_rest[0:1, :, :], bias_rest[0:1, :, :], bias_parts[0:1, 1, :, :], ALU.subtract))
            done(V.tensor_copy(bias_parts[0:1, 2, :, :], bias_rest[0:1, :, :]))
            dve.sem_inc(biases_split, 1)
            step(V.tensor_copy(iota_f[:, :], iota_i[:, :]))
            done(V.tensor_scalar(lane_i[:, :], lane_i[:, :], 63, None, ALU.bitwise_and))
            done(V.tensor_copy(lane_f[:, :], lane_i[:, :]))
            done(V.tensor_scalar(rbf_scale[:, :], lane_f[:, :], float(RBF), None, ALU.is_lt))
            done(V.scalar_tensor_tensor(out=rbf_shift[:, :], in0=lane_f[:, :], scalar=-CUTOFF / (RBF - 1),
                                        in1=rbf_scale[:, :], op0=ALU.mult, op1=ALU.mult))
            step(V.memset(farthest[:, :], 0.0))
            dve.wait_ge(bias_placed, 48)
            dve.wait_ge(fw1_loaded, 64)
            for k in range(3):
                for t in range(CHUNK):
                    step(V.tensor_copy(bias_rhs[:, k, t, :], bias_lanes[:, k, :]))
            settle()
            dve.sem_inc(weights_ready, 1)

            def drop_far(g, part):
                settle()
                if part == 0:
                    dve.wait_ge(edges_loaded, 48 * (g + 1))
                    step(V.tensor_scalar(drop[:, 0:EDGE_COLS], dist[:, 0:EDGE_COLS], CUTOFF, None, ALU.is_gt))
                    step(V.tensor_scalar(dst_in[:, :], dst_in[:, :], ID_BITS, None, ALU.logical_shift_left))
                if part == 1:
                    step(V.tensor_tensor_scan(dropped[:, :], ones_cols[:, :], drop[:, 0:EDGE_COLS], 0.0,
                                              ALU.mult, ALU.add))
                    step(V.tensor_tensor(ids[:, 0:EDGE_COLS], src_in[:, :], dst_in[:, :], ALU.bitwise_or))
                if part == 2:
                    step(V.scalar_tensor_tensor(out=move[0][:, :], in0=dist[:, 0:EDGE_COLS], scalar=CUTOFF,
                                                in1=dropped[:, :], op0=ALU.is_le, op1=ALU.mult))
                    step(V.tensor_scalar(counts[:, bass.ds(g, 1)], dropped[:, EDGE_COLS - 1:EDGE_COLS], -1.0,
                                         float(EDGE_COLS), ALU.mult, ALU.add))

            def shift_by(k, part):
                s, now, new = 1 << k, move[k % 2], move[1 - k % 2]
                keep = EDGE_COLS - s
                settle()
                if part == 0:
                    done(V.tensor_scalar(moves_now[:, :], now[:, :], s, None, ALU.bitwise_and))
                    if k + 1 < STEPS:
                        step(V.scalar_tensor_tensor(out=new[:, :], in0=moves_now[:, :], scalar=0.0, in1=now[:, :],
                                                    op0=ALU.is_equal, op1=ALU.mult))
                if part == 1:
                    dve.sem_inc(paused, 1)
                    step(V.copy_predicated(dist[:, 0:keep], moves_now[:, s:EDGE_COLS], dist[:, s:EDGE_COLS]))
                    step(V.copy_predicated(ids[:, 0:keep], moves_now[:, s:EDGE_COLS], ids[:, s:EDGE_COLS]))
                    if k + 1 < STEPS:
                        step(V.copy_predicated(new[:, 0:keep], moves_now[:, s:EDGE_COLS], now[:, s:EDGE_COLS]))

            def clear_empty(g):
                settle()
                done(V.tensor_scalar(drop[:, :], iota_f[:, :], counts[:, bass.ds(g, 1)], FAR,
                                     ALU.is_ge, ALU.mult))
                done(V.scalar_tensor_tensor(out=dist[:, :], in0=dist[:, :], scalar=FAR, in1=drop[:, :],
                                            op0=ALU.min, op1=ALU.max))
                dve.sem_inc(compacted, 1)

            def tables_angle(row_d, row_i):
                done(V.tensor_scalar(row_int[:, 0, :], row_d, 0.5 / CUTOFF, None, ALU.mult))
                done(V.scalar_tensor_tensor(out=row_a[:, :], in0=row_int[:, 0, :], scalar=-2.0 * CUTOFF, in1=row_d,
                                            op0=ALU.mult, op1=ALU.add))
                done(V.scalar_tensor_tensor(out=row_a[:, :], in0=row_a[:, :], scalar=-1.0, in1=row_a[:, :],
                                            op0=ALU.mult, op1=ALU.max))
                step(V.tensor_scalar(row_int[:, 0, :], row_i, ID_MASK, None, ALU.bitwise_and))
                step(V.tensor_scalar(row_int[:, 1, :], row_i, ID_BITS, None, ALU.logical_shift_right))
                done(V.tensor_scalar(row_b[:, :], row_a[:, :], -1.0, 2.0 * CUTOFF, ALU.mult, ALU.add))
                step(V.tensor_copy(row_src[:, :], row_int[:, 0, :]))
                step(V.tensor_copy(row_dst[:, :], row_int[:, 1, :]))
                done(V.tensor_tensor(row_a[:, :], row_a[:, :], row_b[:, :], ALU.min))
                done(V.scalar_tensor_tensor(out=row_b[:, :], in0=row_a[:, :], scalar=(math.pi / (2 * CUTOFF)) ** 2,
                                            in1=row_a[:, :], op0=ALU.mult, op1=ALU.mult))

            def tables_cosine():
                done(V.tensor_scalar(row_a[:, :], row_b[:, :], COS[8], None, ALU.mult))
                for c in range(7, 0, -1):
                    done(V.scalar_tensor_tensor(out=row_a[:, :], in0=row_a[:, :], scalar=COS[c], in1=row_b[:, :],
                                                op0=ALU.add, op1=ALU.mult))
                done(V.tensor_scalar(row_a[:, :], row_a[:, :], 1.0, None, ALU.add))
                done(V.tensor_tensor(row_a[:, :], row_a[:, :], row_a[:, :], ALU.mult))

            def tables_rows(p, row_d):
                step(V.scalar_tensor_tensor(out=row_cut[:, :], in0=row_d, scalar=CUTOFF, in1=row_a[:, :],
                                            op0=ALU.is_le, op1=ALU.mult))
                done(V.tensor_scalar(row_b[:, :], row_d, CUTOFF, NO_NODE, ALU.is_gt, ALU.mult))
                done(V.tensor_tensor(row_b[:, :], row_b[:, :], row_dst[:, :], ALU.add))
                done(V.tensor_reduce(row_min[:, :], row_b[:, :], op=ALU.min, axis=AX.X))
                dve.sem_inc(p.rows_ready, 1)

            def tables_turned(p, k):
                dve.wait_ge(p.turned, k + 1)
                step(V.tensor_copy(src_next[:, :], ps_rows[:, 0:P]))
                step(V.tensor_copy(cut_next[:, :], ps_rows[:, 2 * P:3 * P]))
                done(V.tensor_copy(dst_next[:, :], ps_rows[:, P:2 * P]))

            def tables_base(p, windows, window):
                if windows == P:
                    done(V.tensor_copy(base_f[0:1, :], ps_rows[0:1, 3 * P:4 * P]))
                else:
                    done(V.tensor_reduce(base_f[0:1, 0:windows],
                                         ps_rows[0:1, 3 * P:4 * P].rearrange("p (w t) -> p w t", w=windows),
                                         op=ALU.min, axis=AX.X))
                done(V.tensor_scalar(base_f[0:1, 0:windows], base_f[0:1, 0:windows], float(AGG_COLS - window),
                                     None, ALU.min))
                dve.sem_inc(p.base_ready, 1)
                done(V.tensor_copy(base_next[0:1, 0:windows], base_f[0:1, 0:windows]))

            def tables_window(p, k, windows, which):
                dve.wait_ge(p.base_spread, k + 1)
                spread = ps_misc[:, 0:windows].rearrange("p (w t) -> p w t", t=1).to_broadcast([P, windows, P // windows])
                done(V.tensor_tensor(dst_next[:, :].rearrange("p (w t) -> p w t", w=windows),
                                     dst_next[:, :].rearrange("p (w t) -> p w t", w=windows), spread, ALU.subtract))
                done(V.scalar_tensor_tensor(out=row_b[:, :], in0=cut_next[:, :], scalar=0.0, in1=dst_next[:, :],
                                            op0=ALU.not_equal, op1=ALU.mult))
                done(V.tensor_reduce(reach[:, :], row_b[:, :], op=ALU.max, axis=AX.X))
                done(V.tensor_tensor(farthest[:, which:which + 1], farthest[:, which:which + 1], reach[:, :], ALU.max))
                dve.sem_inc(p.tables_ready, 1)

            def tables(p, k, row_d, row_i, windows, window, which):
                tables_angle(row_d, row_i)
                tables_cosine()
                tables_rows(p, row_d)
                dve.wait_ge(p.turned, k + 1)
                tables_base(p, windows, window)
                tables_turned(p, k)
                tables_window(p, k, windows, which)

            def give_index(p, table, q, parity):
                step(V.tensor_copy(index[:, parity, :], table[:, UNIT * q:UNIT * (q + 1)]))
                settle()
                dve.sem_inc(p.index_ready, 1)

            def take_tables(windows):
                step(V.tensor_copy(src_now[:, :], src_next[:, :]))
                step(V.tensor_copy(dst_now[:, :], dst_next[:, :]))
                step(V.tensor_copy(cut_now[:, :], cut_next[:, :]))
                if windows:
                    step(V.tensor_copy(base_now[0:1, 0:windows], base_next[0:1, 0:windows]))
                settle()

            def members(n, window):
                for t in range(MACRO):
                    c = MACRO * n + ORDER[t]
                    V.tensor_scalar(member[:, n % 2, t, 0:window], iota_f[:, 0:window], dst_now[:, c:c + 1],
                                    cut_now[:, c:c + 1], ALU.is_equal, ALU.mult)

            def messages(p, macro, n, gathers):
                dve.wait_ge(p.w_ready, macro + 1)
                dve.wait_ge(p.gathered[n % 8], gathers)
                g0 = MACRO * (n % 8)
                V.tensor_tensor(message[:, n % 2, :], ps_w[n % 2][:, :],
                                gathered[:, g0:g0 + MACRO, :].rearrange("p t f -> p (t f)"), ALU.mult)\
                 .then_inc(p.msg_ready, 1)

            def shared_start(n):
                return dve.value_load(base_now[0:1, n:n + 1], min_val=0, max_val=AGG_COLS - WINDOW)

            def add_shared(p, macro, n, start):
                dve.wait_ge(p.summed, macro + 1)
                dve.wait_ge(p.added, macro + 1)
                V.tensor_tensor(agg[:, bass.ds(start, WINDOW)], agg[:, bass.ds(start, WINDOW)],
                                ps_sum[n % 2][:, 0:WINDOW], ALU.add).then_inc(p.added, 1)

            def next_group(g, n):
                row_d, row_i = dist[:, 0:P], ids[:, 0:P]
                if n < 3:
                    drop_far(g, n)
                elif n < 3 + 2 * STEPS:
                    shift_by((n - 3) // 2, (n - 3) % 2)
                elif n == 23:
                    clear_empty(g)
                elif n == 24:
                    tables_angle(row_d, row_i)
                elif n == 25:
                    tables_cosine()
                elif n == 26:
                    tables_rows(main, row_d)
                elif n == 29:
                    tables_turned(main, g)
                    give_index(main, src_next, 0, 0)
                    tables_base(main, MACROS, WINDOW)
                elif n == 31:
                    tables_window(main, g, MACROS, 0)

            def group(g, last):
                first = g * MACROS
                take_tables(MACROS)
                members(0, WINDOW)
                for n in range(MACROS):
                    messages(main, first + n, n, g * (64 * MACROS // 8) + 64 * (n // 8 + 1))
                    if not last:
                        next_group(g + 1, n)
                    if n >= 1:
                        add_shared(main, first + (n - 1), n - 1, start)
                    if n + 1 < MACROS:
                        members(n + 1, WINDOW)
                    start = shared_start(n)
                    if n % MACRO == MACRO - 1 and n // MACRO + 2 < UNITS:
                        give_index(main, src_now, n // MACRO + 2, (n // MACRO) % 2)
                if not last:
                    give_index(main, src_next, 1, 1)
                add_shared(main, first + (MACROS - 1), MACROS - 1, start)

            for part in range(3):
                drop_far(0, part)
            for k in range(STEPS):
                for part in range(2):
                    shift_by(k, part)
            clear_empty(0)
            tables(main, 0, dist[:, 0:P], ids[:, 0:P], MACROS, WINDOW, 0)
            give_index(main, src_next, 0, 0)
            give_index(main, src_next, 1, 1)
            dve.wait_ge(const_built, 2)

            before_groups, per_group = at["n"], DVE_GROUP_STEPS
            with dve.Fori(0, GROUPS - 1) as g:
                at["n"], at["base"] = 0, g * per_group + before_groups
                group(g, False)
                assert at["n"] == per_group, at["n"]
            at["n"], at["base"] = before_groups + (GROUPS - 1) * per_group, 0
            group(GROUPS - 1, True)

            def number_extra():
                for b in range(BLOCKS - 1):
                    step(V.tensor_scalar(more[:, :, b], counts[:, :], float(P * (b + 1)), None, ALU.is_gt))
                done(V.tensor_copy(tile_id[:, :, :], tile_id_i[:, :, :]))
                choices = GROUPS * (BLOCKS - 1)
                flat = more[:, :, :].rearrange("p g b -> p (g b)")
                step(V.tensor_scalar(tile_id[:, :, :], tile_id[:, :, :], -float(ALL_TILES), None, ALU.add))
                done(V.tensor_tensor_scan(rank[:, :], ones_cols[:, 0:choices], flat, 0.0, ALU.mult, ALU.add))
                done(V.tensor_copy(total[:, :], rank[:, choices - 1:choices]))
                dve.sem_inc(extra_flagged, 1)
                done(V.tensor_tensor(rank[:, :], rank[:, :], flat, ALU.subtract))
                dve.wait_ge(extra_counted, 1)
                step(V.tensor_copy(n_extra_i[:, :], ps_misc[:, 1:2]))
                done(V.tensor_copy(offset[:, :], ps_misc[:, 0:1]))
                done(V.tensor_scalar(rank[:, :], rank[:, :], offset[:, 0:1], None, ALU.add))
                dve.sem_inc(n_extra_ready, 1)

            def list_extra(k):
                choices = GROUPS * (BLOCKS - 1)
                flat = more[:, :, :].rearrange("p g b -> p (g b)")
                for c in range(choices):
                    if c >= 2:
                        dve.wait_ge(chosen_used, k * choices + (c - 1))
                    V.tensor_scalar(chosen[:, c % 2, :], iota_f[:, 0:P], rank[:, c:c + 1], flat[:, c:c + 1],
                                    ALU.is_equal, ALU.mult).then_inc(chosen_ready, 1)
                dve.wait_ge(chosen_used, k * choices + choices)
                step(V.tensor_scalar(extra_list[:, :], ps_misc[:, 0:1], float(ALL_TILES), None, ALU.add))
                done(V.tensor_scalar(rank[:, :], rank[:, :], -float(P), None, ALU.add))
                dve.sem_inc(list_ready, 1)

            def add_single(p, macro, n):
                for t in range(MACRO):
                    c = MACRO * n + ORDER[t]
                    start = dve.value_load(base_now[0:1, c:c + 1], min_val=0, max_val=AGG_COLS - WINDOW1)
                    if t == 0:
                        dve.wait_ge(p.summed, macro + 1)
                    dve.wait_ge(p.added, macro * MACRO + (t + 1))
                    V.tensor_tensor(agg[:, bass.ds(start, WINDOW1)], agg[:, bass.ds(start, WINDOW1)],
                                    ps_sum[n % 2][:, WINDOW1 * t:WINDOW1 * (t + 1)], ALU.add).then_inc(p.added, 1)

            number_extra()
            dve.wait_ge(main.added, GROUPS * MACROS + 1)
            n_extra = dve.value_load(n_extra_i[0:1, 0:1], min_val=0, max_val=EXTRA_TILES)
            with dve.Fori(0, EXTRA_GROUPS) as k:
                with dve.If(n_extra > k * P):
                    at["sem"], at["n"], at["base"] = extra_step, 0, k * DVE_EXTRA_STEPS
                    list_extra(k)
                    dve.wait_ge(extra_rows_loaded, 32 * (k + 1))
                    tables(extra, k, row_dist[:, :], row_ids[:, :], P, WINDOW1, 1)
                    take_tables(P)
                    assert at["n"] == DVE_EXTRA_STEPS, at["n"]
                    dve.sem_inc(extra.index_ready, 1)
                    for q in range(UNITS):
                        with dve.If(n_extra > k * P + q * UNIT):
                            m, first = MACRO * q, k * MACROS
                            for n in range(m, m + MACRO):
                                members(n, WINDOW1)
                                messages(extra, first + n, n, k * (64 * MACROS // 8) + 64 * (n // 8 + 1))
                                if n > m:
                                    add_single(extra, first + (n - 1), n - 1)
                            add_single(extra, first + (m + MACRO - 1), m + MACRO - 1)

            at["sem"], at["n"], at["base"] = general_step, 0, 0
            step(V.tensor_scalar(beyond[:, 0:1], farthest[:, 0:1], float(WINDOW), None, ALU.is_ge))
            done(V.tensor_scalar(beyond[:, 1:2], farthest[:, 1:2], float(WINDOW1), None, ALU.is_ge))
            done(V.tensor_tensor(beyond[:, 0:1], beyond[:, 0:1], beyond[:, 1:2], ALU.add))
            dve.sem_inc(beyond_flagged, 1)
            dve.wait_ge(beyond_counted, 1)
            done(V.tensor_copy(outside_i[:, :], ps_misc[:, 0:1]))
            dve.sem_inc(outside_ready, 1)
            outside = dve.value_load(outside_i[0:1, 0:1], min_val=0, max_val=2 * P)
            settled = at["n"]
            with dve.If(outside > 0):
                done(V.memset(agg[:, :], 0.0))
                with dve.Fori(0, ALL_GROUPS) as k:
                    at["n"], at["base"] = 0, k * DVE_GENERAL_STEPS + (settled + 1)
                    dve.wait_ge(general_rows_loaded, 32 * (k + 1))
                    tables_angle(row_dist[:, :], row_ids[:, :])
                    tables_cosine()
                    tables_rows(general, row_dist[:, :])
                    tables_turned(general, k)
                    dve.sem_inc(general.tables_ready, 1)
                    take_tables(0)
                    dve.sem_inc(general.index_ready, 1)
                    for q in range(UNITS):
                        for j in range(MACRO):
                            macro = k * MACROS + (MACRO * q + j)
                            messages(general, macro, j, 64 * (k * UNITS + (q + 1)))
                            c = UNIT * q + MACRO * j
                            done(V.tensor_copy(dst_left[:, :], dst_now[:, c:c + MACRO]))
                            dve.sem_inc(paused, 1)
                            with dve.Fori(0, ALL_WINDOWS) as w:
                                now = macro * ALL_WINDOWS + w
                                for t in range(MACRO):
                                    last = V.tensor_scalar(
                                        gathered[:, UNIT + MACRO * t:UNIT + MACRO * (t + 1), :]
                                        .rearrange("p a b -> p (a b)"), iota_f[:, 0:WIDE],
                                        dst_left[:, ORDER[t]:ORDER[t] + 1], cut_now[:, c + ORDER[t]:c + ORDER[t] + 1],
                                        ALU.is_equal, ALU.mult)
                                last.then_inc(wide_members, 1)
                                dve.wait_ge(general.summed, now + 1)
                                dve.wait_ge(general.added, now + 1)
                                V.tensor_tensor(agg[:, bass.ds(w * WIDE, WIDE)], agg[:, bass.ds(w * WIDE, WIDE)],
                                                ps_sum[0][:, 0:WIDE], ALU.add).then_inc(general.added, 1)
                                V.tensor_scalar(dst_left[:, :], dst_left[:, :], -float(WIDE), None, ALU.add)\
                                 .then_inc(wide_moved, 1)
                                dve.wait_ge(wide_moved, now + 1)
                                dve.wait_ge(general.added, now + 2)
                        dve.sem_inc(general_slots_free, 1)
                    assert at["n"] == DVE_GENERAL_STEPS, at["n"]
            dve.sem_inc(agg_done, 1)
            at["sem"], at["n"], at["base"] = node_step, 0, 0

            def node_statistics(i):
                slot = i % RING
                dve.wait_ge(node_out, i + 1)
                dve.wait_ge(x_again[slot], 16 * (i // RING + 1))
                if i >= RING:
                    dve.wait_ge(out_stored[slot], 16 * (i // RING))
                done(V.scalar_tensor_tensor(out=y_ring[:, slot, :], in0=x_ring[:, slot, :], scalar=2.0,
                                            in1=ps_w[i % 2][0:NODE_TILE, :], op0=ALU.mult, op1=ALU.add))
                dve.sem_inc(node_summed, 1)
                for t in range(CHUNK):
                    step(V.bn_stats(stats[:, i % 2, t, :], y_ring[:, slot, t * P:(t + 1) * P]))
                settle()
                for t in range(CHUNK):
                    last = V.bn_aggr(mean_var[:, slot, t, :], stats[:, i % 2, t, :])
                last.then_inc(node_stats, 1)

            for i in range(CHUNKS):
                node_statistics(i)


DVE_GROUP_STEPS = 102
DVE_EXTRA_STEPS = 40
DVE_GENERAL_STEPS = 62

_INS = ["x", "src", "dst", "edge_weight", "L0_gnn_fw1", "L0_gnn_fb1", "L0_gnn_fw2", "L0_gnn_fb2", "L0_gnn_pw",
        "L0_gnn_pb", "L0_gnn_mw1", "L0_gnn_mb1", "L0_gnn_mw2", "L0_gnn_mb2"]


def kernel(**inputs):
    import numpy as _np
    import concourse.bacc as _bacc
    from concourse import mybir as _mybir
    from concourse.bass_utils import run_bass_kernel_spmd as _run

    nc = _bacc.Bacc("TRN2", target_bir_lowering=False, num_devices=1)
    arrays, args = {}, []
    for name in _INS:
        a = _np.ascontiguousarray(inputs[name])
        arrays[f"in_{name}"] = a
        args.append(nc.dram_tensor(f"in_{name}", a.shape, _mybir.dt.from_np(a.dtype), kind="ExternalInput").ap())
    args.append(nc.dram_tensor("out_nodes", (NODES, HIDDEN), F32, kind="ExternalOutput").ap())
    build(nc, *args)
    r = _run(nc, [arrays], core_ids=[0])
    return _np.asarray(r.results[0]["out_nodes"])
```

```python
import math
from contextlib import ExitStack

import concourse.bass as bass
from concourse import mybir

F32, I32, BF16 = mybir.dt.float32, mybir.dt.int32, mybir.dt.bfloat16
ALU, ACT, AX = mybir.AluOpType, mybir.ActivationFunctionType, mybir.AxisListType

NODES, HIDDEN, EDGES = 12500, 128, 400000
RBF, CUTOFF, EPS = 50, 10.0, 1e-5
WIDTH = CUTOFF / RBF * 0.5
P = 128

EDGE_COLS = 625
ROWS = EDGES // EDGE_COLS
GROUPS = ROWS // P
BLOCKS = -(-EDGE_COLS // P)
ROW_SLOTS = BLOCKS * P
STEPS = EDGE_COLS.bit_length()
ID_BITS = NODES.bit_length()
ID_MASK = (1 << ID_BITS) - 1
FAR = 2 * CUTOFF
NO_NODE = 65536.0

MACRO = 4
WINDOW = 192
WINDOW1 = 64
ORDER = (0, 2, 1, 3)
UNIT = 4 * MACRO
MACROS = P // MACRO
UNITS = P // UNIT
AGG_COLS = 12800
WIDE = 512
ALL_WINDOWS = AGG_COLS // WIDE

EXTRA_TILES = ROWS * (BLOCKS - 1)
EXTRA_GROUPS = EXTRA_TILES // P
ALL_TILES = ROWS * BLOCKS
ALL_GROUPS = ALL_TILES // P

NODE_TILE = 125
CHUNK = 4
CHUNK_NODES = NODE_TILE * CHUNK
CHUNKS = NODES // CHUNK_NODES

BEHIND = 4
N_WEIGHTS = 8
N_CHOICES = GROUPS * (BLOCKS - 1)
CHOSEN = 8
CHOICES = [range(c, min(c + CHOSEN, N_CHOICES)) for c in range(0, N_CHOICES, CHOSEN)]
RING = 8

COS = [(-1) ** k / math.factorial(2 * k) for k in range(9)]


def build(nc, x, src, dst, edge_weight, fw1, fb1, fw2, fb2, pw, pb, mw1, mb1, mw2, mb2, out):
    ctx = ExitStack()
    with ctx:
        def sb(name, shape, dtype=F32):
            return ctx.enter_context(nc.sbuf_tensor(name, shape, dtype))

        def sem(name):
            return ctx.enter_context(nc.semaphore(name))

        proj = nc.dram_tensor("proj_rows", (NODES, HIDDEN), F32).ap()
        dist_tiles = nc.dram_tensor("dist_tiles", (ALL_TILES + 1, P), F32).ap()
        ids_tiles = nc.dram_tensor("ids_tiles", (ALL_TILES + 1, P), I32).ap()
        extra_dist = nc.dram_tensor("extra_dist", (EXTRA_TILES, P), F32).ap()

        dist_rows = dist_tiles[0:ALL_TILES, :].rearrange("(r b) s -> r (b s)", b=BLOCKS)
        ids_rows = ids_tiles[0:ALL_TILES, :].rearrange("(r b) s -> r (b s)", b=BLOCKS)
        edge_rows = [a.rearrange("(r c) -> r c", c=EDGE_COLS) for a in (edge_weight, src, dst)]
        x_nodes = x.rearrange("(j p) f -> p j f", p=NODE_TILE)
        proj_nodes = proj.rearrange("(j p) f -> p j f", p=NODE_TILE)
        out_nodes = out.rearrange("(j p) f -> p j f", p=NODE_TILE)

        ident = sb("ident", [P, P])
        ones_row = sb("ones_row", [1, P])
        before = sb("before", [P, P])
        all_ones = sb("all_ones", [P, P])
        iota_i = sb("iota_i", [P, ROW_SLOTS], I32)
        iota_f = sb("iota_f", [P, ROW_SLOTS])
        lane_i = sb("lane_i", [P, 1], I32)
        lane_f = sb("lane_f", [P, 1])
        rbf_scale = sb("rbf_scale", [P, 1])
        rbf_shift = sb("rbf_shift", [P, 1])
        fw1_halves = sb("fw1_halves", [P, 2, P])
        fw2_sb = sb("fw2_sb", [P, P])
        pw_sb = sb("pw_sb", [P, P])
        mw1_sb = sb("mw1_sb", [P, P])
        mw2_sb = sb("mw2_sb", [P, P])
        mb1_col = sb("mb1_col", [P, 1])
        pb_rows = sb("pb_rows", [NODE_TILE, P])
        bias_in = sb("bias_in", [1, 2, P])
        bias_rest = sb("bias_rest", [1, 2, P])
        bias_parts = sb("bias_parts", [1, 3, 2, P], BF16)
        bias_lanes = sb("bias_lanes", [P, 2, P], BF16)
        bias_rhs = sb("bias_rhs", [P, 2, CHUNK, P], BF16)
        one_lanes = sb("one_lanes", [P, 512], BF16)

        dist = sb("dist", [P, ROW_SLOTS])
        ids = sb("ids", [P, ROW_SLOTS], I32)
        src_in = sb("src_in", [P, EDGE_COLS], I32)
        dst_in = sb("dst_in", [P, EDGE_COLS], I32)
        drop = sb("drop", [P, ROW_SLOTS])
        dropped = sb("dropped", [P, EDGE_COLS])
        move = [sb(f"move{i}", [P, EDGE_COLS], I32) for i in range(2)]
        moves_now = sb("moves_now", [P, EDGE_COLS], I32)
        ones_cols = sb("ones_cols", [P, EDGE_COLS])
        counts = sb("counts", [P, GROUPS])

        row_dist = sb("row_dist", [P, P])
        row_ids = sb("row_ids", [P, P], I32)
        row_cut = sb("row_cut", [P, P])
        row_src = sb("row_src", [P, P])
        row_dst = sb("row_dst", [P, P])
        row_int = sb("row_int", [P, 2, P], I32)
        row_a = sb("row_a", [P, P])
        row_b = sb("row_b", [P, P])
        row_min = sb("row_min", [P, 1])
        base_f = sb("base_f", [1, P])
        base_next = sb("base_next", [1, P], I32)
        base_now = sb("base_now", [1, P], I32)
        src_next = sb("src_next", [P, P], I32)
        dst_next = sb("dst_next", [P, P])
        cut_next = sb("cut_next", [P, P])
        src_now = sb("src_now", [P, P], I32)
        dst_now = sb("dst_now", [P, P])
        cut_now = sb("cut_now", [P, P])
        farthest = sb("farthest", [P, 2])
        reach = sb("reach", [P, 1])

        dist_bc = sb("dist_bc", [P, 2, MACRO, 2 * P])
        square = sb("square", [P, MACRO * 2 * P])
        rbf = sb("rbf", [P, 2, MACRO, 2 * P])
        act_t = sb("act_t", [P, 2, 512])
        gathered = sb("gathered", [P, 2 * UNIT, P])
        message = sb("message", [P, 2, 512])
        member = sb("member", [P, 2, MACRO, WINDOW])
        index = sb("index", [P, 2, UNIT], I32)
        agg = sb("agg", [P, AGG_COLS])

        more = sb("more", [P, GROUPS, BLOCKS - 1])
        rank = sb("rank", [P, N_CHOICES])
        tile_id = sb("tile_id", [P, GROUPS, BLOCKS - 1])
        tile_id_i = sb("tile_id_i", [P, GROUPS, BLOCKS - 1], I32)
        total = sb("total", [P, 1])
        offset = sb("offset", [P, 1])
        n_extra_i = sb("n_extra_i", [P, 1], I32)
        outside_i = sb("outside_i", [P, 1], I32)
        chosen = sb("chosen", [P, CHOSEN, P])
        extra_list = sb("extra_list", [P, 1], I32)
        empty_dist = sb("empty_dist", [1, P])
        empty_ids = sb("empty_ids", [1, P], I32)
        beyond = sb("beyond", [P, 2])
        dst_left = sb("dst_left", [P, MACRO])

        x_ring = sb("x_ring", [NODE_TILE, RING, 512])
        x_t = sb("x_t", [P, 2, 512])
        stats = sb("stats", [NODE_TILE, 2, CHUNK, 6])
        mean_var = sb("mean_var", [NODE_TILE, RING, CHUNK, 2])
        minus_mean = sb("minus_mean", [NODE_TILE, RING, CHUNK])
        var_eps = sb("var_eps", [NODE_TILE, RING, CHUNK])
        rstd = sb("rstd", [NODE_TILE, RING, CHUNK])
        shift = sb("shift", [NODE_TILE, RING, CHUNK])
        minus_half = sb("minus_half", [NODE_TILE, CHUNK])

        def node_rows(slot):
            return gathered[0:NODE_TILE, CHUNK * slot:CHUNK * (slot + 1), :].rearrange("p t f -> p (t f)")

        def bank(name):
            return ctx.enter_context(nc.psum_tensor(name, [P, 512], F32))

        ps_h = [bank("ps_h0"), bank("ps_h1")]
        ps_w = [bank("ps_w0"), bank("ps_w1")]
        ps_sum = [bank("ps_sum0"), bank("ps_sum1")]
        ps_rows = bank("ps_rows")
        ps_misc = bank("ps_misc")

        weights_loaded = sem("weights_loaded")
        biases_loaded = sem("biases_loaded")
        pw_loaded = sem("pw_loaded")
        pb_loaded = sem("pb_loaded")
        fw1_cleared = sem("fw1_cleared")
        const_built = sem("const_built")
        pool_step = sem("pool_step")
        dve_step = sem("dve_step")
        biases_split = sem("biases_split")
        bias_placed = sem("bias_placed")
        weights_ready = sem("weights_ready")
        lanes_ready = sem("lanes_ready")
        sources_ready = sem("sources_ready")
        sums_cleared = sem("sums_cleared")
        sources_turned = sem("sources_turned")

        x_loaded = [sem(f"x_loaded{i}") for i in range(RING)]
        x_turned = sem("x_turned")
        x_t_ready = sem("x_t_ready")
        projected = sem("projected")
        proj_copied = sem("proj_copied")
        proj_biased = sem("proj_biased")
        proj_stored = [sem(f"proj_stored{i}") for i in range(RING)]
        proj_table = sem("proj_table")

        edges_loaded = sem("edges_loaded")
        compacted = sem("compacted")
        rows_stored = sem("rows_stored")
        empty_stored = sem("empty_stored")

        class Pass:

            def __init__(self, name, macros):
                self.rows_ready = sem(name + "_rows_ready")
                self.turned = sem(name + "_turned")
                self.base_ready = sem(name + "_base_ready")
                self.base_spread = sem(name + "_base_spread")
                self.tables_ready = sem(name + "_tables_ready")
                self.dist_loaded = [sem(f"{name}_dist_loaded{i}") for i in range(2)]
                self.squared = sem(name + "_squared")
                self.rbf_ready = sem(name + "_rbf_ready")
                self.h_ready = sem(name + "_h_ready")
                self.act_ready = sem(name + "_act_ready")
                self.w_ready = sem(name + "_w_ready")
                self.gathered = [sem(f"{name}_gathered{i}") for i in range(macros)]
                self.index_ready = sem(name + "_index_ready")
                self.msg_ready = sem(name + "_msg_ready")
                self.summed = sem(name + "_summed")
                self.added = sem(name + "_added")

        main = Pass("main", 2 * MACRO)
        extra = Pass("extra", 2 * MACRO)
        general = Pass("general", MACRO)
        extra_flagged = sem("extra_flagged")
        extra_counted = sem("extra_counted")
        n_extra_ready = sem("n_extra_ready")
        chosen_ready = sem("chosen_ready")
        chosen_used = sem("chosen_used")
        list_ready = sem("list_ready")
        extra_step = sem("extra_step")
        extra_rows_loaded = sem("extra_rows_loaded")
        extra_dist_stored = sem("extra_dist_stored")
        beyond_flagged = sem("beyond_flagged")
        beyond_counted = sem("beyond_counted")
        outside_ready = sem("outside_ready")
        extra_over = sem("extra_over")
        general_slots_free = sem("general_slots_free")
        general_step = sem("general_step")
        outside_step = sem("outside_step")
        general_rows_loaded = sem("general_rows_loaded")
        wide_members = sem("wide_members")
        wide_moved = sem("wide_moved")

        agg_done = sem("agg_done")
        node_step = sem("node_step")
        node_h = sem("node_h")
        node_summed = sem("node_summed")
        node_act = sem("node_act")
        node_out = sem("node_out")
        node_stats = sem("node_stats")
        node_scaled = sem("node_scaled")
        node_normed = sem("node_normed")
        last_normed = sem("last_normed")
        x_again = [sem(f"x_again{i}") for i in range(RING)]
        out_stored = [sem(f"out_stored{i}") for i in range(RING)]

        paused = sem("paused")

        def wait_apart(engine, semaphore, value):
            engine.wait_ge(semaphore, value)
            engine.sem_inc(paused, 1)

        block = ctx.enter_context(nc.Block())

        @block.sync
        def _(sp):
            def load_edges(g):
                if not isinstance(g, int) or g > 0:
                    sp.wait_ge(main.rows_ready, g)
                sp.dma_start(dist[:, 0:EDGE_COLS], edge_rows[0][bass.ds(g * P, P), :]).then_inc(edges_loaded, 16)
                sp.dma_start(src_in[:, :], edge_rows[1][bass.ds(g * P, P), :]).then_inc(edges_loaded, 16)
                sp.dma_start(dst_in[:, :], edge_rows[2][bass.ds(g * P, P), :]).then_inc(edges_loaded, 16)

            def store_rows(g):
                sp.wait_ge(compacted, g + 1)
                sp.dma_start(dist_rows[bass.ds(g * P, P), :], dist[:, :]).then_inc(rows_stored, 16)
                sp.dma_start(ids_rows[bass.ds(g * P, P), :], ids[:, :]).then_inc(rows_stored, 16)
                sp.wait_ge(rows_stored, 32 * (g + 1))

            def load_x(i, sems, slot):
                sp.dma_start(x_ring[:, slot, :].rearrange("p (j f) -> p j f", f=P),
                             x_nodes[:, bass.ds(i * CHUNK, CHUNK), :]).then_inc(sems[slot], 16)

            load_x(0, x_loaded, 0)
            load_edges(0)
            load_x(1, x_loaded, 1)
            sp.dma_start(pw_sb[:, :], pw).then_inc(pw_loaded, 16)
            sp.dma_start(pb_rows[:, :], pb.rearrange("(a n) -> a n", a=1)[0, :].partition_broadcast(NODE_TILE))\
              .then_inc(pb_loaded, 16)

            def store_proj(i, slot):
                sp.wait_ge(proj_biased, i + 1)
                sp.dma_start(proj_nodes[:, bass.ds(i * CHUNK, CHUNK), :],
                             node_rows(slot).rearrange("p (j f) -> p j f", f=P)).then_inc(proj_stored[slot], 16)

            for i in range(2, RING):
                load_x(i, x_loaded, i)
            for i, b in enumerate((fb2, mb2)):
                sp.dma_start(bias_in[0:1, i, :], b.rearrange("(a n) -> a n", a=1)).then_inc(biases_loaded, 16)
            sp.dma_start(fw2_sb[:, :], fw2).then_inc(weights_loaded, 16)
            sp.dma_start(mw1_sb[:, :], mw1).then_inc(weights_loaded, 16)
            sp.dma_start(mw2_sb[:, :], mw2).then_inc(weights_loaded, 16)
            sp.dma_start(mb1_col[:, :], mb1.rearrange("(n a) -> n a", a=1)).then_inc(weights_loaded, 16)
            sp.wait_ge(fw1_cleared, 1)
            for half in range(2):
                sp.dma_start(fw1_halves[64 * half:64 * half + RBF, half, :], fw1).then_inc(weights_loaded, 16)
                sp.dma_start(fw1_halves[64 * half + RBF:64 * half + RBF + 1, half, :],
                             fb1.rearrange("(a n) -> a n", a=1)).then_inc(weights_loaded, 16)

            for i in range(CHUNKS):
                if i + RING < CHUNKS:
                    sp.wait_ge(x_turned, i + 1)
                    load_x(i + RING, x_loaded, i % RING)
                store_proj(i, i % RING)
            for slot in range(RING):
                sp.wait_ge(proj_stored[slot], 16 * len(range(slot, CHUNKS, RING)))
            sp.sem_inc(proj_table, 1)

            def load_unit(tiles, stride_rows, unit, parity, loaded):
                rows = tiles[bass.ds(unit * (UNIT * stride_rows), UNIT * stride_rows), :]
                for half in range(2):
                    v = rows.rearrange("(k h b) s -> h b k s", h=2, b=stride_rows)[half, 0]
                    sp.dma_start(dist_bc[64 * half:64 * half + 64, parity, :, :]
                                 .rearrange("p m (t s) -> p (m t) s", s=P),
                                 v.partition_broadcast(64)).then_inc(loaded[parity], 16)

            def load_first_group():
                load_edges(1)
                sp.wait_ge(const_built, 1)
                sp.wait_ge(biases_split, 1)
                for part in range(3):
                    sp.dma_start(bias_lanes[part:part + 1, :, :], bias_parts[0:1, part, :, :])\
                      .then_inc(bias_placed, 16)
                sp.wait_ge(const_built, 3)
                sp.dma_start(dist_tiles[ALL_TILES:ALL_TILES + 1, :], empty_dist[:, :]).then_inc(empty_stored, 16)
                sp.dma_start(ids_tiles[ALL_TILES:ALL_TILES + 1, :], empty_ids[:, :]).then_inc(empty_stored, 16)

            store_rows(0)

            def group(g, last, next_edges):
                for q in range(UNITS):
                    unit = g * UNITS + q
                    if not (isinstance(unit, int) and unit < 2):
                        sp.wait_ge(main.squared, unit)
                    load_unit(dist_tiles, BLOCKS, unit, q % 2, main.dist_loaded)
                    if isinstance(unit, int) and unit == 1:
                        load_first_group()
                if not last:
                    store_rows(g + 1)
                if next_edges:
                    load_edges(g + 2)

            group(0, False, True)
            with sp.Fori(1, GROUPS - 2) as g:
                group(g, False, True)
            group(GROUPS - 2, False, False)

            for i in range(RING):
                load_x(i, x_again, i)
            group(GROUPS - 1, True, False)

            def store_extra(k):
                sp.wait_ge(extra_rows_loaded, 32 * (k + 1))
                sp.dma_start(extra_dist[bass.ds(k * P, P), :], row_dist[:, :]).then_inc(extra_dist_stored, 16)
                sp.wait_ge(extra_dist_stored, 16 * (k + 1))

            def extra_units(k, q):
                with sp.If(n_extra > k * P + q * UNIT):
                    if q >= 2:
                        sp.wait_ge(extra.squared, k * UNITS + q)
                    elif isinstance(k, int):
                        sp.wait_ge(main.squared, GROUPS * UNITS + q)
                    load_unit(extra_dist, 1, k * UNITS + q, q % 2, extra.dist_loaded)
                    if q + 1 < UNITS:
                        extra_units(k, q + 1)

            store_extra(0)
            sp.wait_ge(n_extra_ready, 1)
            n_extra = sp.value_load(n_extra_i[0:1, 0:1], min_val=0, max_val=EXTRA_TILES)
            extra_units(0, 0)
            with sp.If(n_extra > P):
                with sp.Fori(1, EXTRA_GROUPS) as k:
                    with sp.If(n_extra > k * P):
                        store_extra(k)
                        wait_apart(sp, extra.squared, k * UNITS + 1)
                        extra_units(k, 0)
                sp.wait_ge(outside_ready, 2)

            sp.wait_ge(outside_ready, 1)
            outside = sp.value_load(outside_i[0:1, 0:1], min_val=0, max_val=2 * P)
            with sp.If(outside > 0):
                sp.wait_ge(extra_over, 1)
                with sp.Fori(0, ALL_GROUPS) as k:
                    sp.wait_ge(general.tables_ready, k + 1)
                    sp.dma_start(row_dist[:, :], dist_tiles[bass.ds(k * P, P), :]).then_inc(general_rows_loaded, 16)
                    sp.dma_start(row_ids[:, :], ids_tiles[bass.ds(k * P, P), :]).then_inc(general_rows_loaded, 16)
                    for q in range(UNITS):
                        sp.wait_ge(general.squared, k * UNITS + (q + 1))
                        load_unit(dist_tiles, 1, k * UNITS + q, 0, general.dist_loaded)

            for i in range(CHUNKS):
                sp.wait_ge(node_normed, i + 1)
                sp.wait_ge(last_normed, i + 1)
                sp.dma_start(out_nodes[:, i * CHUNK:(i + 1) * CHUNK, :],
                             node_rows(i % RING).rearrange("p (j f) -> p j f", f=P))\
                  .then_inc(out_stored[i % RING], 16)
                if i + RING < CHUNKS:
                    sp.wait_ge(node_summed, i + 1)
                    load_x(i + RING, x_again, i % RING)
            for slot in range(RING):
                sp.wait_ge(out_stored[slot], 16 * len(range(slot, CHUNKS, RING)))

        @block.gpsimd
        def _(pool):
            n = [0]

            def step(ins):
                n[0] += 1
                ins.then_inc(pool_step, 1)
                pool.wait_ge(pool_step, n[0])

            step(nc.gpsimd.memset(fw1_halves[:, :, :], 0.0))
            pool.sem_inc(fw1_cleared, 1)
            step(nc.gpsimd.memset(bias_lanes[:, :, :], 0.0))
            step(nc.gpsimd.memset(ones_cols[:, :], 1.0))
            pool.sem_inc(const_built, 1)
            step(nc.gpsimd.memset(ident[:, :], 0.0))
            step(nc.gpsimd.affine_select(out=ident[:, :], in_=ident[:, :], compare_op=ALU.not_equal, fill=1.0,
                                         base=0, pattern=[[-1, P]], channel_multiplier=1))
            step(nc.gpsimd.memset(one_lanes[:, :], 0.0))
            step(nc.gpsimd.memset(one_lanes[0:3, :], 1.0))
            step(nc.gpsimd.iota(iota_i[:, :], pattern=[[1, ROW_SLOTS]], base=0, channel_multiplier=0))
            step(nc.gpsimd.iota(lane_i[:, :], pattern=[[1, 1]], base=0, channel_multiplier=1))
            step(nc.gpsimd.memset(ids[:, EDGE_COLS:ROW_SLOTS], 0))
            step(nc.gpsimd.memset(dist[:, EDGE_COLS:ROW_SLOTS], FAR))
            pool.sem_inc(const_built, 1)
            step(nc.gpsimd.memset(all_ones[:, :], 1.0))
            step(nc.gpsimd.memset(ones_row[:, :], 1.0))
            step(nc.gpsimd.affine_select(out=before[:, :], in_=all_ones[:, :], compare_op=ALU.is_gt, fill=0.0,
                                         base=0, pattern=[[1, P]], channel_multiplier=-1))
            step(nc.gpsimd.iota(tile_id_i[:, :, :], pattern=[[P * BLOCKS, GROUPS], [1, BLOCKS - 1]],
                                base=1, channel_multiplier=BLOCKS))
            step(nc.gpsimd.memset(minus_half[:, :], -0.5))
            step(nc.gpsimd.memset(empty_dist[:, :], FAR))
            step(nc.gpsimd.memset(empty_ids[:, :], 0))
            pool.sem_inc(const_built, 1)

            pool.wait_ge(pb_loaded, 16)
            for i in range(CHUNKS):
                pool.wait_ge(proj_copied, i + 1)
                rows = gathered[0:NODE_TILE, CHUNK * (i % RING):CHUNK * (i % RING + 1), :]
                nc.gpsimd.tensor_tensor(rows, rows, pb_rows[:, :].rearrange("p (t f) -> p t f", t=1)
                                        .to_broadcast([NODE_TILE, CHUNK, P]), ALU.add).then_inc(proj_biased, 1)
            pool.wait_ge(proj_table, 1)

            def gather_tile(table, c, slot, done):
                nc.gpsimd.indirect_dma_start(
                    out=gathered[:, slot, :], out_offset=None, in_=proj,
                    in_offset=bass.IndirectOffsetOnAxis(ap=table[:, c:c + 1], axis=0)).then_inc(done, 16)

            def gather_unit(p, unit, parity, first):
                pool.wait_ge(p.index_ready, unit + 1)
                for j in range(MACRO):
                    if not first:
                        wait_apart(pool, p.msg_ready, unit * MACRO + (j - 7))
                    for t in range(MACRO):
                        c = MACRO * j + ORDER[t]
                        gather_tile(index[:, parity, :], c, UNIT * parity + MACRO * j + t,
                                    p.gathered[MACRO * parity + j])

            for parity in range(2):
                gather_unit(main, parity, parity, True)
            ahead = (GROUPS - 1) * UNITS + UNITS // 2
            with pool.Fori(2, ahead, 2) as u:
                for parity in range(2):
                    gather_unit(main, u + parity, parity, False)

            def gather_rows():
                for rows, tiles in ((row_dist, dist_tiles), (row_ids, ids_tiles)):
                    nc.gpsimd.indirect_dma_start(
                        out=rows[:, :], out_offset=None, in_=tiles,
                        in_offset=bass.IndirectOffsetOnAxis(ap=extra_list[:, 0:1], axis=0),
                    ).then_inc(extra_rows_loaded, 16)

            pool.wait_ge(empty_stored, 32)
            pool.wait_ge(rows_stored, 32 * GROUPS)
            pool.wait_ge(list_ready, 1)
            gather_rows()
            with pool.Fori(ahead, GROUPS * UNITS, 2) as u:
                for parity in range(2):
                    gather_unit(main, u + parity, parity, False)

            def extra_units(k, q):
                with pool.If(n_extra > k * P + q * UNIT):
                    for j in range(MACRO):
                        if q >= 2:
                            wait_apart(pool, extra.msg_ready, k * MACROS + (MACRO * q + j - 7))
                        elif isinstance(k, int):
                            pool.wait_ge(main.msg_ready, GROUPS * MACROS + MACRO * q + j - 7)
                        for t in range(MACRO):
                            gather_tile(src_now, UNIT * q + MACRO * j + ORDER[t],
                                        UNIT * (q % 2) + MACRO * j + t, extra.gathered[MACRO * (q % 2) + j])
                    if q + 1 < UNITS:
                        extra_units(k, q + 1)

            pool.wait_ge(n_extra_ready, 1)
            n_extra = pool.value_load(n_extra_i[0:1, 0:1], min_val=0, max_val=EXTRA_TILES)
            pool.wait_ge(extra.index_ready, 1)
            extra_units(0, 0)
            with pool.If(n_extra > P):
                with pool.Fori(1, EXTRA_GROUPS) as k:
                    with pool.If(n_extra > k * P):
                        pool.wait_ge(list_ready, k + 1)
                        wait_apart(pool, extra_dist_stored, 16 * k)
                        gather_rows()
                        wait_apart(pool, extra.index_ready, k + 1)
                        extra_units(k, 0)
                pool.wait_ge(outside_ready, 2)

            pool.wait_ge(outside_ready, 1)
            outside = pool.value_load(outside_i[0:1, 0:1], min_val=0, max_val=2 * P)
            with pool.If(outside > 0):
                pool.wait_ge(extra_over, 1)
                with pool.Fori(0, ALL_GROUPS) as k:
                    pool.wait_ge(general.index_ready, k + 1)
                    for q in range(UNITS):
                        wait_apart(pool, general_slots_free, k * UNITS + (q + 1))
                        for j in range(MACRO):
                            for t in range(MACRO):
                                gather_tile(src_now, UNIT * q + MACRO * j + ORDER[t], MACRO * j + t,
                                            general.gathered[j])

            for i in range(CHUNKS):
                pool.wait_ge(node_stats, i + 1)
                if i >= RING:
                    pool.wait_ge(node_normed, i - RING + 1)
                step(nc.gpsimd.tensor_tensor(rstd[:, i % RING, :], var_eps[:, i % RING, :], minus_half[:, :], ALU.pow))
                step(nc.gpsimd.tensor_tensor(shift[:, i % RING, :], minus_mean[:, i % RING, :], rstd[:, i % RING, :],
                                             ALU.mult))
                pool.sem_inc(node_scaled, 1)
                row = node_rows(i % RING)[:, (CHUNK - 1) * P:CHUNK * P]
                nc.gpsimd.tensor_scalar(row, row, rstd[:, i % RING, CHUNK - 1:CHUNK],
                                        shift[:, i % RING, CHUNK - 1:CHUNK], ALU.mult, ALU.add)\
                  .then_inc(last_normed, 1)

        @block.scalar
        def _(act):
            for p in (main, extra, general):
                act.sem_inc(p.squared, 1)

            def take_turned(i):
                act.wait_ge(x_turned, i + 1)
                if i >= 2:
                    act.wait_ge(projected, i - 1)
                nc.scalar.activation(x_t[:, i % 2, 0:CHUNK_NODES], ps_h[i % 2][:, 0:CHUNK_NODES], ACT.Copy)\
                  .then_inc(x_t_ready, 1)

            take_turned(0)
            for i in range(CHUNKS):
                if i + 1 < CHUNKS:
                    take_turned(i + 1)
                act.wait_ge(projected, i + 1)
                if i >= RING:
                    act.wait_ge(proj_stored[i % RING], 16 * (i // RING))
                nc.scalar.activation(node_rows(i % RING), ps_w[i % 2][0:NODE_TILE, :], ACT.Copy)\
                  .then_inc(proj_copied, 1)
            act.wait_ge(const_built, 1)
            for i in range(AGG_COLS // WIDE):
                nc.scalar.activation(agg[:, WIDE * i:WIDE * (i + 1)], ones_cols[:, 0:WIDE], ACT.Copy, scale=0.0)\
                  .then_inc(sums_cleared, 1)
            act.wait_ge(lanes_ready, 1)

            def radial(p, unit, parity, wait=True):
                if wait:
                    act.wait_ge(p.dist_loaded[parity], 16 * (unit + (2 - parity)))
                nc.scalar.activation(square[:, :], dist_bc[:, parity, :, :], ACT.Square,
                                     bias=rbf_shift[:, 0:1], scale=rbf_scale[:, 0:1]).then_inc(p.squared, 1)
                act.wait_ge(p.squared, unit + 2)
                nc.scalar.activation(rbf[:, parity, :, :], square[:, :], ACT.Exp,
                                     scale=-1.0 / (2.0 * WIDTH * WIDTH)).then_inc(p.rbf_ready, 1)

            def silu(p, macro, parity):
                act.wait_ge(p.h_ready, macro + 1)
                nc.scalar.activation(act_t[:, parity, :], ps_h[parity][:, :], ACT.Silu).then_inc(p.act_ready, 1)

            def pair(u, last):
                for parity in range(2):
                    for j in range(MACRO):
                        if j == 2 and not (last and parity):
                            radial(main, u + (parity + 1), 1 - parity)
                        silu(main, u * MACRO + (MACRO * parity + j), j % 2)

            radial(main, 0, 0)
            with act.Fori(0, GROUPS * UNITS - 2, 2) as u:
                pair(u, False)
            pair(GROUPS * UNITS - 2, True)

            act.wait_ge(n_extra_ready, 1)
            n_extra = act.value_load(n_extra_i[0:1, 0:1], min_val=0, max_val=EXTRA_TILES)

            def extra_units(k, q):
                with act.If(n_extra > k * P + q * UNIT):
                    radial(extra, k * UNITS + q, q % 2)
                    for j in range(MACRO):
                        silu(extra, k * MACROS + (MACRO * q + j), j % 2)
                    if q + 1 < UNITS:
                        extra_units(k, q + 1)

            extra_units(0, 0)
            with act.If(n_extra > P):
                with act.Fori(1, EXTRA_GROUPS) as k:
                    extra_units(k, 0)
                act.wait_ge(outside_ready, 2)

            act.wait_ge(outside_ready, 1)
            outside = act.value_load(outside_i[0:1, 0:1], min_val=0, max_val=2 * P)
            with act.If(outside > 0):
                with act.Fori(0, ALL_GROUPS * UNITS) as u:
                    act.wait_ge(general.dist_loaded[0], 32 * (u + 1))
                    radial(general, u, 0, wait=False)
                    for j in range(MACRO):
                        silu(general, u * MACRO + j, j % 2)

            for i in range(CHUNKS + BEHIND):
                if i < CHUNKS:
                    act.wait_ge(node_h, i + 1)
                    nc.scalar.activation(act_t[:, i % 2, 0:CHUNK_NODES], ps_h[i % 2][:, 0:CHUNK_NODES],
                                         ACT.Silu, bias=mb1_col[:, 0:1]).then_inc(node_act, 1)
                if i >= BEHIND:
                    k = i - BEHIND
                    act.wait_ge(node_scaled, k + 1)
                    for t in range(CHUNK - 1):
                        row = node_rows(k % RING)[:, t * P:(t + 1) * P]
                        last = nc.scalar.activation(row, row, ACT.Identity, scale=rstd[:, k % RING, t:t + 1],
                                                    bias=shift[:, k % RING, t:t + 1])
                    last.then_inc(node_normed, 1)

        @block.tensor
        def _(pe):
            pe.wait_ge(const_built, 2)

            def turn(i):
                pe.wait_ge(x_loaded[i % RING], 16 * (i // RING + 1))
                if i >= 2:
                    pe.wait_ge(x_t_ready, i - 1)
                for t in range(CHUNK):
                    last = nc.tensor.transpose(ps_h[i % 2][:, t * NODE_TILE:(t + 1) * NODE_TILE],
                                               x_ring[:, i % RING, t * P:(t + 1) * P],
                                               ident[0:NODE_TILE, 0:NODE_TILE])
                last.then_inc(x_turned, 1)

            def project(i):
                pe.wait_ge(x_t_ready, i + 1)
                if i >= 2:
                    pe.wait_ge(proj_copied, i - 1)
                for t in range(CHUNK):
                    last = nc.tensor.matmul(ps_w[i % 2][0:NODE_TILE, t * P:(t + 1) * P],
                                            x_t[:, i % 2, t * NODE_TILE:(t + 1) * NODE_TILE], pw_sb[:, :],
                                            start=True, stop=True)
                last.then_inc(projected, 1)

            turn(0)
            turn(1)
            pe.wait_ge(pw_loaded, 16)
            for i in range(CHUNKS):
                project(i)
                if i + 2 < CHUNKS:
                    turn(i + 2)

            def turn_rows(p, k):
                pe.wait_ge(p.rows_ready, k + 1)
                for c, t in enumerate((row_src, row_dst, row_cut)):
                    nc.tensor.transpose(ps_rows[:, c * P:(c + 1) * P], t[:, :], ident[:, :])
                nc.tensor.transpose(ps_rows[0:1, 3 * P:4 * P], row_min[:, :], ident[:, :]).then_inc(p.turned, 1)

            def spread_base(p, k, windows):
                pe.wait_ge(p.base_ready, k + 1)
                nc.tensor.matmul(ps_misc[:, 0:windows], ones_row[0:1, :], base_f[0:1, 0:windows],
                                 start=True, stop=True).then_inc(p.base_spread, 1)

            def first_layer(p, n, units):
                pe.wait_ge(p.rbf_ready, units)
                for half in range(2):
                    last = nc.tensor.matmul(ps_h[n % 2][:, 256 * half:256 * half + 256], fw1_halves[:, half, :],
                                            rbf[:, (n // MACRO) % 2, n % MACRO, :], start=True, stop=True)
                last.then_inc(p.h_ready, 1)

            def second_layer(p, macro, n):
                pe.wait_ge(p.act_ready, macro + 1)
                nc.tensor.matmul(ps_w[n % 2][:, :], one_lanes[:, 0:P], bias_rhs[:, 0, :, :],
                                 start=True, stop=False, skip_group_check=True)
                for t in range(MACRO):
                    last = nc.tensor.matmul(ps_w[n % 2][:, t * P:(t + 1) * P], act_t[:, n % 2, t * P:(t + 1) * P],
                                            fw2_sb[:, :], start=False, stop=True, skip_group_check=True)
                last.then_inc(p.w_ready, 1)

            def sum_shared(p, macro, n, bank_wait):
                pe.wait_ge(p.msg_ready, macro + 1)
                if bank_wait is not None:
                    pe.wait_ge(p.added, bank_wait + 1)
                for t in range(MACRO):
                    last = nc.tensor.matmul(ps_sum[n % 2][:, 0:WINDOW], message[:, n % 2, t * P:(t + 1) * P],
                                            member[:, n % 2, t, :], start=(t == 0), stop=(t == MACRO - 1))
                last.then_inc(p.summed, 1)

            def count_extra():
                pe.wait_ge(extra_flagged, 1)
                nc.tensor.matmul(ps_misc[:, 0:1], before[:, :], total[:, :], start=True, stop=True)
                nc.tensor.matmul(ps_misc[:, 1:2], all_ones[:, :], total[:, :], start=True, stop=True)\
                  .then_inc(extra_counted, 1)

            def choose(k, part):
                ids_flat = tile_id[:, :, :].rearrange("p g b -> p (g b)")
                for c in CHOICES[part]:
                    pe.wait_ge(chosen_ready, k * N_CHOICES + (c + 1))
                    nc.tensor.matmul(ps_misc[:, 0:1], chosen[:, c % CHOSEN, :], ids_flat[:, c:c + 1],
                                     start=(c == 0), stop=(c == N_CHOICES - 1)).then_inc(chosen_used, 1)

            def count_beyond(times):
                pe.wait_ge(beyond_flagged, times)
                nc.tensor.matmul(ps_misc[:, 0:1], all_ones[:, :], beyond[:, 0:1], start=True, stop=True)\
                  .then_inc(beyond_counted, 1)

            def prepare_extra(n):
                if n == 2:
                    count_extra()
                elif n in (6, 9, 12):
                    choose(0, (n - 6) // 3)
                elif n == 23:
                    turn_rows(extra, 0)
                elif n == 26:
                    spread_base(extra, 0, P)
                elif n == 30:
                    count_beyond(1)

            def group(g, last):
                at = g * MACROS
                unit = g * UNITS
                for n in range(MACROS):
                    if n + 1 < MACROS or not last:
                        first_layer(main, n + 1, unit + ((n + 1) // MACRO + 1))
                    second_layer(main, at + n, n)
                    if n >= 1:
                        sum_shared(main, at + (n - 1), n - 1, at if n == 1 else at + (n - 2) if n >= 3 else None)
                    if n == 28 and not last:
                        turn_rows(main, g + 1)
                    if n == 30 and not last:
                        spread_base(main, g + 1, MACROS)
                    if last:
                        prepare_extra(n)
                sum_shared(main, at + (MACROS - 1), MACROS - 1, at + (MACROS - 2))

            pe.wait_ge(const_built, 3)
            pe.wait_ge(weights_loaded, 16 * N_WEIGHTS)
            pe.wait_ge(sources_ready, 1)
            nc.tensor.transpose(ps_rows[:, 0:P], row_src[:, :], ident[:, :]).then_inc(sources_turned, 1)
            turn_rows(main, 0)
            spread_base(main, 0, MACROS)
            pe.wait_ge(weights_ready, 1)
            first_layer(main, 0, 1)
            with pe.Fori(0, GROUPS - 1) as g:
                group(g, False)
            group(GROUPS - 1, True)

            def sum_single(p, macro, n, bank_wait):
                pe.wait_ge(p.msg_ready, macro + 1)
                pe.wait_ge(p.added, bank_wait + 1)
                for t in range(MACRO):
                    last = nc.tensor.matmul(ps_sum[n % 2][:, WINDOW1 * t:WINDOW1 * (t + 1)],
                                            message[:, n % 2, t * P:(t + 1) * P], member[:, n % 2, t, 0:WINDOW1],
                                            start=True, stop=True)
                last.then_inc(p.summed, 1)

            def extra_units(k, q):
                with pe.If(n_extra > k * P + q * UNIT):
                    at, unit = k * MACROS, k * UNITS + q
                    m = MACRO * q
                    first_layer(extra, m, unit + 1)
                    for j in range(MACRO):
                        if j + 1 < MACRO:
                            first_layer(extra, m + j + 1, unit + 1)
                        second_layer(extra, at + (m + j), m + j)
                        if j >= 1:
                            if isinstance(k, int) and q == 0 and j == 1:
                                pe.wait_ge(main.added, GROUPS * MACROS + 1)
                            sum_single(extra, at + (m + j - 1), m + j - 1,
                                       MACRO * (at + (m + max(j - 2, 0))))
                    sum_single(extra, at + (m + MACRO - 1), m + MACRO - 1, MACRO * (at + (m + MACRO - 2)))
                    if q + 1 < UNITS:
                        extra_units(k, q + 1)

            pe.wait_ge(n_extra_ready, 1)
            n_extra = pe.value_load(n_extra_i[0:1, 0:1], min_val=0, max_val=EXTRA_TILES)
            extra_units(0, 0)
            with pe.If(n_extra > P):
                with pe.Fori(1, EXTRA_GROUPS) as k:
                    with pe.If(n_extra > k * P):
                        for part in range(len(CHOICES)):
                            choose(k, part)
                        turn_rows(extra, k)
                        spread_base(extra, k, P)
                        extra_units(k, 0)
                count_beyond(2)
                pe.wait_ge(outside_ready, 2)

            pe.wait_ge(outside_ready, 1)
            outside = pe.value_load(outside_i[0:1, 0:1], min_val=0, max_val=2 * P)
            with pe.If(outside > 0):
                with pe.Fori(0, ALL_GROUPS) as k:
                    turn_rows(general, k)
                    for q in range(UNITS):
                        for j in range(MACRO):
                            macro = k * MACROS + (MACRO * q + j)
                            first_layer(general, j, k * UNITS + (q + 1))
                            second_layer(general, macro, j)
                            wait_apart(pe, general.msg_ready, macro + 1)
                            with pe.Fori(0, ALL_WINDOWS) as w:
                                pe.wait_ge(wide_members, macro * ALL_WINDOWS + w + 1)
                                for t in range(MACRO):
                                    last = nc.tensor.matmul(
                                        ps_sum[0][:, 0:WIDE], message[:, j % 2, t * P:(t + 1) * P],
                                        gathered[:, UNIT + MACRO * t:UNIT + MACRO * (t + 1), :],
                                        start=(t == 0), stop=(t == MACRO - 1))
                                last.then_inc(general.summed, 1)

            def node_first(i):
                if i >= 2:
                    pe.wait_ge(node_act, i - 1)
                nc.tensor.matmul(ps_h[i % 2][:, 0:CHUNK_NODES], mw1_sb[:, :],
                                 agg[:, i * CHUNK_NODES:(i + 1) * CHUNK_NODES],
                                 start=True, stop=True).then_inc(node_h, 1)

            def node_second(i):
                pe.wait_ge(node_act, i + 1)
                if i >= 2:
                    pe.wait_ge(node_summed, i - 1)
                nc.tensor.matmul(ps_w[i % 2][0:NODE_TILE, :], one_lanes[:, 0:NODE_TILE], bias_rhs[:, 1, :, :],
                                 start=True, stop=False, skip_group_check=True)
                for t in range(CHUNK):
                    last = nc.tensor.matmul(ps_w[i % 2][0:NODE_TILE, t * P:(t + 1) * P],
                                            act_t[:, i % 2, t * NODE_TILE:(t + 1) * NODE_TILE], mw2_sb[:, :],
                                            start=False, stop=True, skip_group_check=True)
                last.then_inc(node_out, 1)

            pe.wait_ge(agg_done, 1)
            node_first(0)
            for i in range(CHUNKS):
                if i + 1 < CHUNKS:
                    node_first(i + 1)
                node_second(i)

        @block.vector
        def _(dve):
            at = {"n": 0, "base": 0, "sem": dve_step}

            def step(ins):
                at["n"] += 1
                ins.then_inc(at["sem"], 1)

            def settle():
                if not isinstance(at["base"], int) or at["base"] + at["n"] > 0:
                    dve.wait_ge(at["sem"], at["base"] + at["n"])

            def done(ins):
                step(ins)
                settle()

            V = nc.vector
            for p in (main, extra, general):
                dve.sem_inc(p.added, 1)
            dve.sem_inc(general.tables_ready, 1)
            dve.sem_inc(general_slots_free, 1)

            def split_biases():
                dve.wait_ge(biases_loaded, 2 * 16)
                done(V.tensor_copy(bias_parts[0:1, 0, :, :], bias_in[0:1, :, :]))
                done(V.tensor_tensor(bias_rest[0:1, :, :], bias_in[0:1, :, :], bias_parts[0:1, 0, :, :], ALU.subtract))
                done(V.tensor_copy(bias_parts[0:1, 1, :, :], bias_rest[0:1, :, :]))
                done(V.tensor_tensor(bias_rest[0:1, :, :], bias_rest[0:1, :, :], bias_parts[0:1, 1, :, :],
                                     ALU.subtract))
                done(V.tensor_copy(bias_parts[0:1, 2, :, :], bias_rest[0:1, :, :]))
                dve.sem_inc(biases_split, 1)

            def build_lanes():
                dve.wait_ge(const_built, 2)
                step(V.tensor_copy(iota_f[:, :], iota_i[:, :]))
                step(V.memset(farthest[:, :], 0.0))
                done(V.tensor_scalar(lane_i[:, :], lane_i[:, :], 63, None, ALU.bitwise_and))
                done(V.tensor_copy(lane_f[:, :], lane_i[:, :]))
                done(V.tensor_scalar(rbf_scale[:, :], lane_f[:, :], float(RBF), None, ALU.is_lt))
                done(V.scalar_tensor_tensor(out=rbf_shift[:, :], in0=lane_f[:, :], scalar=-CUTOFF / (RBF - 1),
                                            in1=rbf_scale[:, :], op0=ALU.mult, op1=ALU.mult))
                dve.sem_inc(lanes_ready, 1)

            def repeat_biases():
                dve.wait_ge(bias_placed, 48)
                for k in range(2):
                    for t in range(CHUNK):
                        step(V.tensor_copy(bias_rhs[:, k, t, :], bias_lanes[:, k, :]))
                settle()
                dve.sem_inc(weights_ready, 1)

            def drop_far(g, part):
                settle()
                if part == 0:
                    dve.wait_ge(edges_loaded, 48 * (g + 1))
                    step(V.tensor_scalar(drop[:, 0:EDGE_COLS], dist[:, 0:EDGE_COLS], CUTOFF, None, ALU.is_gt))
                    step(V.tensor_scalar(dst_in[:, :], dst_in[:, :], ID_BITS, None, ALU.logical_shift_left))
                if part == 1:
                    step(V.tensor_tensor_scan(dropped[:, :], ones_cols[:, :], drop[:, 0:EDGE_COLS], 0.0,
                                              ALU.mult, ALU.add))
                    step(V.tensor_tensor(ids[:, 0:EDGE_COLS], src_in[:, :], dst_in[:, :], ALU.bitwise_or))
                if part == 2:
                    step(V.scalar_tensor_tensor(out=move[0][:, :], in0=dist[:, 0:EDGE_COLS], scalar=CUTOFF,
                                                in1=dropped[:, :], op0=ALU.is_le, op1=ALU.mult))
                    step(V.tensor_scalar(counts[:, bass.ds(g, 1)], dropped[:, EDGE_COLS - 1:EDGE_COLS], -1.0,
                                         float(EDGE_COLS), ALU.mult, ALU.add))

            def shift_by(k, part):
                s, now, new = 1 << k, move[k % 2], move[1 - k % 2]
                keep = EDGE_COLS - s
                settle()
                if part == 0:
                    done(V.tensor_scalar(moves_now[:, :], now[:, :], s, None, ALU.bitwise_and))
                    if k + 1 < STEPS:
                        step(V.scalar_tensor_tensor(out=new[:, :], in0=moves_now[:, :], scalar=0.0, in1=now[:, :],
                                                    op0=ALU.is_equal, op1=ALU.mult))
                if part == 1:
                    dve.sem_inc(paused, 1)
                    step(V.copy_predicated(dist[:, 0:keep], moves_now[:, s:EDGE_COLS], dist[:, s:EDGE_COLS]))
                    step(V.copy_predicated(ids[:, 0:keep], moves_now[:, s:EDGE_COLS], ids[:, s:EDGE_COLS]))
                    if k + 1 < STEPS:
                        step(V.copy_predicated(new[:, 0:keep], moves_now[:, s:EDGE_COLS], now[:, s:EDGE_COLS]))

            def clear_empty(g):
                settle()
                done(V.tensor_scalar(drop[:, :], iota_f[:, :], counts[:, bass.ds(g, 1)], FAR,
                                     ALU.is_ge, ALU.mult))
                done(V.scalar_tensor_tensor(out=dist[:, :], in0=dist[:, :], scalar=FAR, in1=drop[:, :],
                                            op0=ALU.min, op1=ALU.max))
                dve.sem_inc(compacted, 1)

            def tables_angle(row_d, row_i):
                done(V.tensor_scalar(row_int[:, 0, :], row_d, 0.5 / CUTOFF, None, ALU.mult))
                done(V.scalar_tensor_tensor(out=row_a[:, :], in0=row_int[:, 0, :], scalar=-2.0 * CUTOFF, in1=row_d,
                                            op0=ALU.mult, op1=ALU.add))
                done(V.scalar_tensor_tensor(out=row_a[:, :], in0=row_a[:, :], scalar=-1.0, in1=row_a[:, :],
                                            op0=ALU.mult, op1=ALU.max))
                step(V.tensor_scalar(row_int[:, 0, :], row_i, ID_MASK, None, ALU.bitwise_and))
                step(V.tensor_scalar(row_int[:, 1, :], row_i, ID_BITS, None, ALU.logical_shift_right))
                done(V.tensor_scalar(row_b[:, :], row_a[:, :], -1.0, 2.0 * CUTOFF, ALU.mult, ALU.add))
                step(V.tensor_copy(row_src[:, :], row_int[:, 0, :]))
                step(V.tensor_copy(row_dst[:, :], row_int[:, 1, :]))
                done(V.tensor_tensor(row_a[:, :], row_a[:, :], row_b[:, :], ALU.min))
                done(V.scalar_tensor_tensor(out=row_b[:, :], in0=row_a[:, :], scalar=(math.pi / (2 * CUTOFF)) ** 2,
                                            in1=row_a[:, :], op0=ALU.mult, op1=ALU.mult))

            def tables_cosine():
                done(V.tensor_scalar(row_a[:, :], row_b[:, :], COS[8], None, ALU.mult))
                for c in range(7, 0, -1):
                    done(V.scalar_tensor_tensor(out=row_a[:, :], in0=row_a[:, :], scalar=COS[c], in1=row_b[:, :],
                                                op0=ALU.add, op1=ALU.mult))
                done(V.tensor_scalar(row_a[:, :], row_a[:, :], 1.0, None, ALU.add))
                done(V.tensor_tensor(row_a[:, :], row_a[:, :], row_a[:, :], ALU.mult))

            def tables_rows(p, row_d):
                step(V.scalar_tensor_tensor(out=row_cut[:, :], in0=row_d, scalar=CUTOFF, in1=row_a[:, :],
                                            op0=ALU.is_le, op1=ALU.mult))
                done(V.tensor_scalar(row_b[:, :], row_d, CUTOFF, NO_NODE, ALU.is_gt, ALU.mult))
                done(V.tensor_tensor(row_b[:, :], row_b[:, :], row_dst[:, :], ALU.add))
                done(V.tensor_reduce(row_min[:, :], row_b[:, :], op=ALU.min, axis=AX.X))
                dve.sem_inc(p.rows_ready, 1)

            def tables_turned(p, k):
                dve.wait_ge(p.turned, k + 1)
                step(V.tensor_copy(src_next[:, :], ps_rows[:, 0:P]))
                step(V.tensor_copy(cut_next[:, :], ps_rows[:, 2 * P:3 * P]))
                done(V.tensor_copy(dst_next[:, :], ps_rows[:, P:2 * P]))

            def tables_base(p, windows, window):
                if windows == P:
                    done(V.tensor_copy(base_f[0:1, :], ps_rows[0:1, 3 * P:4 * P]))
                else:
                    done(V.tensor_reduce(base_f[0:1, 0:windows],
                                         ps_rows[0:1, 3 * P:4 * P].rearrange("p (w t) -> p w t", w=windows),
                                         op=ALU.min, axis=AX.X))
                done(V.tensor_scalar(base_f[0:1, 0:windows], base_f[0:1, 0:windows], float(AGG_COLS - window),
                                     None, ALU.min))
                dve.sem_inc(p.base_ready, 1)
                done(V.tensor_copy(base_next[0:1, 0:windows], base_f[0:1, 0:windows]))

            def tables_window(p, k, windows, which):
                dve.wait_ge(p.base_spread, k + 1)
                spread = ps_misc[:, 0:windows].rearrange("p (w t) -> p w t", t=1)\
                    .to_broadcast([P, windows, P // windows])
                done(V.tensor_tensor(dst_next[:, :].rearrange("p (w t) -> p w t", w=windows),
                                     dst_next[:, :].rearrange("p (w t) -> p w t", w=windows), spread, ALU.subtract))
                done(V.scalar_tensor_tensor(out=row_b[:, :], in0=cut_next[:, :], scalar=0.0, in1=dst_next[:, :],
                                            op0=ALU.not_equal, op1=ALU.mult))
                done(V.tensor_reduce(reach[:, :], row_b[:, :], op=ALU.max, axis=AX.X))
                done(V.tensor_tensor(farthest[:, which:which + 1], farthest[:, which:which + 1], reach[:, :], ALU.max))
                dve.sem_inc(p.tables_ready, 1)

            def tables(p, k, row_d, row_i, windows, window, which):
                tables_angle(row_d, row_i)
                tables_cosine()
                tables_rows(p, row_d)
                dve.wait_ge(p.turned, k + 1)
                tables_base(p, windows, window)
                tables_turned(p, k)
                tables_window(p, k, windows, which)

            def give_index(p, table, q, parity):
                step(V.tensor_copy(index[:, parity, :], table[:, UNIT * q:UNIT * (q + 1)]))
                settle()
                dve.sem_inc(p.index_ready, 1)

            def take_tables(windows, sources=True):
                if sources:
                    step(V.tensor_copy(src_now[:, :], src_next[:, :]))
                step(V.tensor_copy(dst_now[:, :], dst_next[:, :]))
                step(V.tensor_copy(cut_now[:, :], cut_next[:, :]))
                if windows:
                    step(V.tensor_copy(base_now[0:1, 0:windows], base_next[0:1, 0:windows]))
                settle()

            def members(n, window):
                for t in range(MACRO):
                    c = MACRO * n + ORDER[t]
                    V.tensor_scalar(member[:, n % 2, t, 0:window], iota_f[:, 0:window], dst_now[:, c:c + 1],
                                    cut_now[:, c:c + 1], ALU.is_equal, ALU.mult)

            def messages(p, macro, n, gathers):
                dve.wait_ge(p.w_ready, macro + 1)
                dve.wait_ge(p.gathered[n % 8], gathers)
                g0 = MACRO * (n % 8)
                V.tensor_tensor(message[:, n % 2, :], ps_w[n % 2][:, :],
                                gathered[:, g0:g0 + MACRO, :].rearrange("p t f -> p (t f)"), ALU.mult)\
                 .then_inc(p.msg_ready, 1)

            def shared_start(n):
                return dve.value_load(base_now[0:1, n:n + 1], min_val=0, max_val=AGG_COLS - WINDOW)

            def add_shared(p, macro, n, start):
                dve.wait_ge(p.summed, macro + 1)
                dve.wait_ge(p.added, macro + 1)
                V.tensor_tensor(agg[:, bass.ds(start, WINDOW)], agg[:, bass.ds(start, WINDOW)],
                                ps_sum[n % 2][:, 0:WINDOW], ALU.add).then_inc(p.added, 1)

            def next_group(g, n):
                row_d, row_i = dist[:, 0:P], ids[:, 0:P]
                if n < 3:
                    drop_far(g, n)
                elif n < 3 + 2 * STEPS:
                    shift_by((n - 3) // 2, (n - 3) % 2)
                elif n == 23:
                    clear_empty(g)
                elif n == 24:
                    tables_angle(row_d, row_i)
                elif n == 25:
                    tables_cosine()
                elif n == 26:
                    tables_rows(main, row_d)
                elif n == 29:
                    tables_turned(main, g)
                    give_index(main, src_next, 0, 0)
                    tables_base(main, MACROS, WINDOW)
                elif n == 31:
                    tables_window(main, g, MACROS, 0)

            def number_extra(part):
                flat = more[:, :, :].rearrange("p g b -> p (g b)")
                if part == 0:
                    for b in range(BLOCKS - 1):
                        step(V.tensor_scalar(more[:, :, b], counts[:, :], float(P * (b + 1)), None, ALU.is_gt))
                    done(V.tensor_copy(tile_id[:, :, :], tile_id_i[:, :, :]))
                    step(V.tensor_scalar(tile_id[:, :, :], tile_id[:, :, :], -float(ALL_TILES), None, ALU.add))
                    done(V.tensor_tensor_scan(rank[:, :], ones_cols[:, 0:N_CHOICES], flat, 0.0, ALU.mult, ALU.add))
                    done(V.tensor_copy(total[:, :], rank[:, N_CHOICES - 1:N_CHOICES]))
                    dve.sem_inc(extra_flagged, 1)
                if part == 1:
                    done(V.tensor_tensor(rank[:, :], rank[:, :], flat, ALU.subtract))
                    dve.wait_ge(extra_counted, 1)
                    step(V.tensor_copy(n_extra_i[:, :], ps_misc[:, 1:2]))
                    done(V.tensor_copy(offset[:, :], ps_misc[:, 0:1]))
                    done(V.tensor_scalar(rank[:, :], rank[:, :], offset[:, 0:1], None, ALU.add))
                    dve.sem_inc(n_extra_ready, 1)

            def choose(k, part):
                flat = more[:, :, :].rearrange("p g b -> p (g b)")
                for c in CHOICES[part]:
                    if c >= CHOSEN:
                        dve.wait_ge(chosen_used, k * N_CHOICES + (c - CHOSEN + 1))
                    V.tensor_scalar(chosen[:, c % CHOSEN, :], iota_f[:, 0:P], rank[:, c:c + 1], flat[:, c:c + 1],
                                    ALU.is_equal, ALU.mult).then_inc(chosen_ready, 1)

            def write_list(k):
                dve.wait_ge(chosen_used, k * N_CHOICES + N_CHOICES)
                step(V.tensor_scalar(extra_list[:, :], ps_misc[:, 0:1], float(ALL_TILES), None, ALU.add))
                done(V.tensor_scalar(rank[:, :], rank[:, :], -float(P), None, ALU.add))
                dve.sem_inc(list_ready, 1)

            def flag_beyond():
                step(V.tensor_scalar(beyond[:, 0:1], farthest[:, 0:1], float(WINDOW), None, ALU.is_ge))
                done(V.tensor_scalar(beyond[:, 1:2], farthest[:, 1:2], float(WINDOW1), None, ALU.is_ge))
                done(V.tensor_tensor(beyond[:, 0:1], beyond[:, 0:1], beyond[:, 1:2], ALU.add))
                dve.sem_inc(beyond_flagged, 1)

            def take_outside(times):
                dve.wait_ge(beyond_counted, times)
                done(V.tensor_copy(outside_i[:, :], ps_misc[:, 0:1]))
                dve.sem_inc(outside_ready, 1)

            def prepare_extra(n):
                if n == 0:
                    number_extra(0)
                elif n == 3:
                    number_extra(1)
                elif n in (4, 7, 10):
                    choose(0, (n - 4) // 3)
                elif n == 13:
                    write_list(0)
                elif n == 19:
                    dve.wait_ge(extra_rows_loaded, 32)
                    tables_angle(row_dist[:, :], row_ids[:, :])
                elif n == 20:
                    tables_cosine()
                elif n == 21:
                    tables_rows(extra, row_dist[:, :])
                elif n == 24:
                    tables_turned(extra, 0)
                    done(V.tensor_copy(src_now[:, :], src_next[:, :]))
                    dve.sem_inc(extra.index_ready, 1)
                    tables_base(extra, P, WINDOW1)
                elif n == 27:
                    tables_window(extra, 0, P, 1)
                elif n == 28:
                    flag_beyond()
                elif n == 31:
                    take_outside(1)

            def group(g, last):
                first = g * MACROS
                take_tables(MACROS)
                members(0, WINDOW)
                for n in range(MACROS):
                    messages(main, first + n, n, g * (64 * MACROS // 8) + 64 * (n // 8 + 1))
                    if last:
                        prepare_extra(n)
                    else:
                        next_group(g + 1, n)
                    if n >= 1:
                        add_shared(main, first + (n - 1), n - 1, start)
                    if n + 1 < MACROS:
                        members(n + 1, WINDOW)
                    start = shared_start(n)
                    if n % MACRO == MACRO - 1 and n // MACRO + 2 < UNITS:
                        give_index(main, src_now, n // MACRO + 2, (n // MACRO) % 2)
                if not last:
                    give_index(main, src_next, 1, 1)
                add_shared(main, first + (MACROS - 1), MACROS - 1, start)

            drop_far(0, 0)
            dve.wait_ge(const_built, 1)
            drop_far(0, 1)
            drop_far(0, 2)
            for k in range(STEPS):
                for part in range(2):
                    shift_by(k, part)
            settle()
            done(V.tensor_scalar(row_int[:, 0, :], ids[:, 0:P], ID_MASK, None, ALU.bitwise_and))
            done(V.tensor_copy(row_src[:, :], row_int[:, 0, :]))
            dve.sem_inc(sources_ready, 1)
            build_lanes()
            clear_empty(0)
            dve.wait_ge(sources_turned, 1)
            give_index(main, ps_rows, 0, 0)
            give_index(main, ps_rows, 1, 1)
            split_biases()
            tables(main, 0, dist[:, 0:P], ids[:, 0:P], MACROS, WINDOW, 0)
            dve.wait_ge(const_built, 3)
            dve.wait_ge(sums_cleared, AGG_COLS // WIDE)
            repeat_biases()

            before_groups, per_group = at["n"], DVE_GROUP_STEPS
            with dve.Fori(0, GROUPS - 1) as g:
                at["n"], at["base"] = 0, g * per_group + before_groups
                group(g, False)
                assert at["n"] == per_group, at["n"]
            at["n"], at["base"] = before_groups + (GROUPS - 1) * per_group, 0
            group(GROUPS - 1, True)

            def single_starts(n):
                _, starts = nc.values_load_multi_w_load_instructions(
                    base_now[0:1, MACRO * n:MACRO * (n + 1)], engines=[mybir.EngineType.DVE], min_val=0,
                    max_val=AGG_COLS - WINDOW1)
                return [starts[t] for t in ORDER]

            def add_single(p, macro, n, starts):
                for t in range(MACRO):
                    if t == 0:
                        dve.wait_ge(p.summed, macro + 1)
                    dve.wait_ge(p.added, macro * MACRO + (t + 1))
                    V.tensor_tensor(agg[:, bass.ds(starts[t], WINDOW1)], agg[:, bass.ds(starts[t], WINDOW1)],
                                    ps_sum[n % 2][:, WINDOW1 * t:WINDOW1 * (t + 1)], ALU.add).then_inc(p.added, 1)

            def extra_units(k, q):
                with dve.If(n_extra > k * P + q * UNIT):
                    m, first, starts = MACRO * q, k * MACROS, []
                    for n in range(m, m + MACRO):
                        members(n, WINDOW1)
                        starts.append(single_starts(n))
                        messages(extra, first + n, n, k * (64 * MACROS // 8) + 64 * (n // 8 + 1))
                        if n > m:
                            add_single(extra, first + (n - 1), n - 1, starts[-2])
                    add_single(extra, first + (m + MACRO - 1), m + MACRO - 1, starts[-1])
                    if q + 1 < UNITS:
                        extra_units(k, q + 1)

            dve.wait_ge(main.added, GROUPS * MACROS + 1)
            take_tables(P, sources=False)
            n_extra = dve.value_load(n_extra_i[0:1, 0:1], min_val=0, max_val=EXTRA_TILES)
            extra_units(0, 0)
            with dve.If(n_extra > P):
                with dve.Fori(1, EXTRA_GROUPS) as k:
                    with dve.If(n_extra > k * P):
                        at["sem"], at["n"], at["base"] = extra_step, 0, (k - 1) * DVE_EXTRA_STEPS
                        for part in range(len(CHOICES)):
                            choose(k, part)
                        write_list(k)
                        dve.wait_ge(extra_rows_loaded, 32 * (k + 1))
                        tables(extra, k, row_dist[:, :], row_ids[:, :], P, WINDOW1, 1)
                        take_tables(P)
                        assert at["n"] == DVE_EXTRA_STEPS, at["n"]
                        dve.sem_inc(extra.index_ready, 1)
                        extra_units(k, 0)
                at["sem"], at["n"], at["base"] = outside_step, 0, 0
                flag_beyond()
                take_outside(2)
            dve.sem_inc(extra_over, 1)

            at["sem"], at["n"], at["base"] = general_step, 0, 0
            outside = dve.value_load(outside_i[0:1, 0:1], min_val=0, max_val=2 * P)
            with dve.If(outside > 0):
                done(V.memset(agg[:, :], 0.0))
                with dve.Fori(0, ALL_GROUPS) as k:
                    at["n"], at["base"] = 0, k * DVE_GENERAL_STEPS + 1
                    dve.wait_ge(general_rows_loaded, 32 * (k + 1))
                    tables_angle(row_dist[:, :], row_ids[:, :])
                    tables_cosine()
                    tables_rows(general, row_dist[:, :])
                    tables_turned(general, k)
                    dve.sem_inc(general.tables_ready, 1)
                    take_tables(0)
                    dve.sem_inc(general.index_ready, 1)
                    for q in range(UNITS):
                        for j in range(MACRO):
                            macro = k * MACROS + (MACRO * q + j)
                            messages(general, macro, j, 64 * (k * UNITS + (q + 1)))
                            c = UNIT * q + MACRO * j
                            done(V.tensor_copy(dst_left[:, :], dst_now[:, c:c + MACRO]))
                            dve.sem_inc(paused, 1)
                            with dve.Fori(0, ALL_WINDOWS) as w:
                                now = macro * ALL_WINDOWS + w
                                for t in range(MACRO):
                                    last = V.tensor_scalar(
                                        gathered[:, UNIT + MACRO * t:UNIT + MACRO * (t + 1), :]
                                        .rearrange("p a b -> p (a b)"), iota_f[:, 0:WIDE],
                                        dst_left[:, ORDER[t]:ORDER[t] + 1], cut_now[:, c + ORDER[t]:c + ORDER[t] + 1],
                                        ALU.is_equal, ALU.mult)
                                last.then_inc(wide_members, 1)
                                dve.wait_ge(general.summed, now + 1)
                                dve.wait_ge(general.added, now + 1)
                                V.tensor_tensor(agg[:, bass.ds(w * WIDE, WIDE)], agg[:, bass.ds(w * WIDE, WIDE)],
                                                ps_sum[0][:, 0:WIDE], ALU.add).then_inc(general.added, 1)
                                V.tensor_scalar(dst_left[:, :], dst_left[:, :], -float(WIDE), None, ALU.add)\
                                 .then_inc(wide_moved, 1)
                                dve.wait_ge(wide_moved, now + 1)
                                dve.wait_ge(general.added, now + 2)
                        dve.sem_inc(general_slots_free, 1)
                    assert at["n"] == DVE_GENERAL_STEPS, at["n"]
            dve.sem_inc(agg_done, 1)
            at["sem"], at["n"], at["base"] = node_step, 0, 0

            def residual(i):
                slot = i % RING
                dve.wait_ge(node_out, i + 1)
                dve.wait_ge(x_again[slot], 16 * (i // RING + 1))
                if i >= RING:
                    dve.wait_ge(out_stored[slot], 16 * (i // RING))
                V.scalar_tensor_tensor(out=node_rows(slot), in0=x_ring[:, slot, :], scalar=2.0,
                                       in1=ps_w[i % 2][0:NODE_TILE, :], op0=ALU.mult, op1=ALU.add)\
                 .then_inc(node_summed, 1)

            def statistics(i):
                slot = i % RING
                dve.wait_ge(node_summed, i + 1)
                for t in range(CHUNK):
                    step(V.bn_stats(stats[:, i % 2, t, :], node_rows(slot)[:, t * P:(t + 1) * P]))
                settle()
                for t in range(CHUNK):
                    step(V.bn_aggr(mean_var[:, slot, t, :], stats[:, i % 2, t, :]))

            def give_statistics(i):
                slot = i % RING
                settle()
                V.tensor_scalar(minus_mean[:, slot, :], mean_var[:, slot, :, 0], -1.0, None, ALU.mult)
                V.tensor_scalar(var_eps[:, slot, :], mean_var[:, slot, :, 1], EPS, None, ALU.add)\
                 .then_inc(node_stats, 1)

            residual(0)
            for i in range(CHUNKS):
                if i + 1 < CHUNKS:
                    residual(i + 1)
                if i >= 1:
                    give_statistics(i - 1)
                statistics(i)
            give_statistics(CHUNKS - 1)


DVE_GROUP_STEPS = 102
DVE_EXTRA_STEPS = 40
DVE_GENERAL_STEPS = 62

_INS = ["x", "src", "dst", "edge_weight", "L0_gnn_fw1", "L0_gnn_fb1", "L0_gnn_fw2", "L0_gnn_fb2", "L0_gnn_pw",
        "L0_gnn_pb", "L0_gnn_mw1", "L0_gnn_mb1", "L0_gnn_mw2", "L0_gnn_mb2"]


def kernel(**inputs):
    import numpy as _np
    import concourse.bacc as _bacc
    from concourse import mybir as _mybir
    from concourse.bass_utils import run_bass_kernel_spmd as _run

    nc = _bacc.Bacc("TRN2", target_bir_lowering=False, num_devices=1)
    arrays, args = {}, []
    for name in _INS:
        a = _np.ascontiguousarray(inputs[name])
        arrays[f"in_{name}"] = a
        args.append(nc.dram_tensor(f"in_{name}", a.shape, _mybir.dt.from_np(a.dtype), kind="ExternalInput").ap())
    args.append(nc.dram_tensor("out_nodes", (NODES, HIDDEN), F32, kind="ExternalOutput").ap())
    build(nc, *args)
    r = _run(nc, [arrays], core_ids=[0])
    return _np.asarray(r.results[0]["out_nodes"])
```
